# Optimizing a Trainium2 kernel written in Bass

```python
import numpy as np
import jax
import jax.numpy as jnp

def _softmax(x, axis=-1):
    return jax.nn.softmax(x, axis=axis)

def _gelu(x):
    return jax.nn.gelu(x, approximate=True)

def _silu(x):
    return jax.nn.silu(x)

def _sigmoid(x):
    return jax.nn.sigmoid(x)

def _layernorm(x, axis=-1, eps=1e-05):
    m = jnp.mean(x, axis=axis, keepdims=True)
    v = jnp.var(x, axis=axis, keepdims=True)
    return (x - m) / jnp.sqrt(v + eps)

def _scatter_add(tgt, idx, src, axis=0):
    return tgt.at[idx].add(src)

def _segment_sum(src, seg, n):
    return jax.ops.segment_sum(src, seg, n)
kernel_name = 'mk_macaron_d2_jaxref_r8_895da4'

def setup_inputs(seed: int=0):
    np.random.seed(seed)
    _w = jnp.asarray

    def _L0_attn_setup():
        import jax, jax.numpy as jnp
        import numpy as np
        D_MODEL = 128
        NHEAD = 16
        HEAD_DIM = D_MODEL // NHEAD
        SCALE = float(np.sqrt(HEAD_DIM))
        key = jax.random.key(seed)
        ks = jax.random.split(key, 6)
        B, T = (2, 256)
        x = jax.random.normal(ks[0], (B, T, D_MODEL), dtype=jnp.float32)
        s = 1.0 / np.sqrt(D_MODEL)
        qkv_w = jax.random.uniform(ks[1], (3 * D_MODEL, D_MODEL), jnp.float32, -s, s)
        qkv_b = jax.random.uniform(ks[2], (3 * D_MODEL,), jnp.float32, -s, s)
        out_w = jax.random.uniform(ks[3], (D_MODEL, D_MODEL), jnp.float32, -s, s)
        out_b = jax.random.uniform(ks[4], (D_MODEL,), jnp.float32, -s, s)
        decay_alpha = jnp.full((NHEAD,), 0.1, dtype=jnp.float32)
        return {'x': x, 'qkv_w': qkv_w, 'qkv_b': qkv_b, 'out_w': out_w, 'out_b': out_b, 'decay_alpha': decay_alpha}
    _L0_attn_in = _L0_attn_setup()

    def _L0_ffn_setup():
        import jax, jax.numpy as jnp
        import numpy as np
        DIM = 128
        DEPTH = 2
        HEADS = 8
        DIM_HEAD = 64
        WINDOW = 64
        INNER = HEADS * DIM_HEAD
        HID = int(DIM * 4 * 2 / 3)
        B, N = (2, 1024)
        QK_SCALE = 8.0

        def shift_token(t):
            t1, t2 = jnp.split(t, 2, axis=-1)
            t2 = jnp.pad(t2, ((0, 0), (1, 0), (0, 0)))[:, :-1]
            return jnp.concatenate([t1, t2], axis=-1)

        def l2norm(t):
            return t / jnp.clip(jnp.linalg.norm(t, axis=-1, keepdims=True), 1e-12)

        def rotate_half(x):
            x1, x2 = jnp.split(x, 2, axis=-1)
            return jnp.concatenate([-x2, x1], axis=-1)

        def rotary_xpos(q, k):
            n = q.shape[-2]
            half_idx = jnp.arange(0, DIM_HEAD, 2, dtype=jnp.float32)
            inv_freq = 1.0 / 10000.0 ** (half_idx / DIM_HEAD)
            t = jnp.arange(n, dtype=jnp.float32)
            freqs = t[:, None] * inv_freq[None, :]
            freqs = jnp.concatenate([freqs, freqs], axis=-1)
            base = (half_idx + 0.4 * DIM_HEAD) / (1.4 * DIM_HEAD)
            power = (t - n // 2) / float(WINDOW // 2)
            scale = base[None, :] ** power[:, None]
            scale = jnp.concatenate([scale, scale], axis=-1)
            cos, sin = (jnp.cos(freqs), jnp.sin(freqs))
            q = q * cos * scale + rotate_half(q) * sin * scale
            k = k * cos / scale + rotate_half(k) * sin / scale
            return (q, k)

        def local_attention(q, k, v):
            b, h, n, d = q.shape
            w = n // WINDOW
            bq = q.reshape(b, h, w, WINDOW, d) * QK_SCALE
            bk = k.reshape(b, h, w, WINDOW, d)
            bv = v.reshape(b, h, w, WINDOW, d)

            def look_around(t):
                p = jnp.pad(t, ((0, 0), (0, 0), (1, 0), (0, 0), (0, 0)))
                return jnp.concatenate([p[:, :, :w], p[:, :, 1:]], axis=3)
            bk, bv = (look_around(bk), look_around(bv))
            bt = jnp.arange(n).reshape(w, WINDOW)
            btp = jnp.pad(bt, ((1, 0), (0, 0)), constant_values=-1)
            btk = jnp.concatenate([btp[:w], btp[1:]], axis=1)
            sim = jnp.einsum('bhwid,bhwjd->bhwij', bq, bk)
            i = bt[:, :, None]
            j = btk[:, None, :]
            mask = (i < j) | (i > j + WINDOW) | (j == -1)
            sim = jnp.where(mask, -jnp.finfo(sim.dtype).max, sim)
            attn = jax.nn.softmax(sim, axis=-1)
            out = jnp.einsum('bhwij,bhwjd->bhwid', attn, bv)
            return out.reshape(b, h, n, d)

        def _layer(x, wqkv, qs, ksc, wo, lg, lb, w1, b1, w2, b2):
            b, n, _ = x.shape
            h = shift_token(x)
            qkv = h @ wqkv
            q, k, v = jnp.split(qkv, 3, axis=-1)
            to_heads = lambda t: t.reshape(b, n, HEADS, DIM_HEAD).transpose(0, 2, 1, 3)
            q, k, v = (to_heads(q), to_heads(k), to_heads(v))
            q = l2norm(q) * qs
            k = l2norm(k) * ksc
            q, k = rotary_xpos(q, k)
            o = local_attention(q, k, v)
            o = o.transpose(0, 2, 1, 3).reshape(b, n, INNER)
            x = x + o @ wo
            h = shift_token(x)
            mu = h.mean(-1, keepdims=True)
            var = h.var(-1, keepdims=True)
            h = (h - mu) / jnp.sqrt(var + 1e-05) * lg + lb
            h = h @ w1 + b1
            a, g = jnp.split(h, 2, axis=-1)
            h = a * jax.nn.gelu(g, approximate=False)
            x = x + h @ w2 + b2
            return x
        key = jax.random.key(seed)
        ks = jax.random.split(key, 6)
        return {'x': jax.random.normal(ks[0], (B, N, DIM), jnp.float32), 'wqkv': jax.random.normal(ks[1], (DEPTH, DIM, 3 * INNER), jnp.float32) * 0.02, 'q_scale': jnp.ones((DEPTH, DIM_HEAD), jnp.float32), 'k_scale': jnp.ones((DEPTH, DIM_HEAD), jnp.float32), 'wo': jax.random.normal(ks[2], (DEPTH, INNER, DIM), jnp.float32) * 0.02, 'ln_g': jnp.ones((DEPTH, DIM), jnp.float32), 'ln_b': jnp.zeros((DEPTH, DIM), jnp.float32), 'w1': jax.random.normal(ks[3], (DEPTH, DIM, 2 * HID), jnp.float32) * 0.02, 'b1': jnp.zeros((DEPTH, 2 * HID), jnp.float32), 'w2': jax.random.normal(ks[4], (DEPTH, HID, DIM), jnp.float32) * 0.02, 'b2': jnp.zeros((DEPTH, DIM), jnp.float32)}
    _L0_ffn_in = _L0_ffn_setup()

    def _L1_attn_setup():
        import jax, jax.numpy as jnp
        import numpy as np
        D_MODEL = 128
        B, T = (4, 512)
        LN_EPS = 1e-05
        DEN_EPS = 1e-06
        key = jax.random.key(seed)
        ks = jax.random.split(key, 10)
        s = 1.0 / np.sqrt(D_MODEL)
        return {'x': jax.random.normal(ks[0], (B, T, D_MODEL), dtype=jnp.float32), 'w_qkv': jax.random.normal(ks[1], (D_MODEL, 3 * D_MODEL), dtype=jnp.float32) * s, 'b_qkv': jnp.zeros((3 * D_MODEL,), dtype=jnp.float32), 'w_gate': jax.random.normal(ks[2], (D_MODEL, D_MODEL), dtype=jnp.float32) * s, 'b_gate': jnp.zeros((D_MODEL,), dtype=jnp.float32), 'w_proj': jax.random.normal(ks[3], (D_MODEL, D_MODEL), dtype=jnp.float32) * s, 'b_proj': jnp.zeros((D_MODEL,), dtype=jnp.float32), 'ln_g': jnp.ones((D_MODEL,), dtype=jnp.float32), 'ln_b': jnp.zeros((D_MODEL,), dtype=jnp.float32)}
    _L1_attn_in = _L1_attn_setup()

    def _L1_ffn_setup():
        import jax, jax.numpy as jnp
        import numpy as np
        D = 128
        E = 12
        HS = 2 * D
        HR = 3 * D
        TAU = 1.5

        def _geglu(h):
            a, g = jnp.split(h, 2, axis=-1)
            return a * jax.nn.gelu(g, approximate=False)
        key = jax.random.key(seed)
        ks = jax.random.split(key, 12)

        def xavier(k, shape):
            fan_in, fan_out = (shape[-2], shape[-1])
            lim = jnp.sqrt(6.0 / (fan_in + fan_out))
            return jax.random.uniform(k, shape, jnp.float32, -lim, lim)
        x = jax.random.normal(ks[0], (2, 128, D), jnp.float32)
        Ws1 = xavier(ks[1], (D, 2 * HS))
        bs1 = jnp.zeros((2 * HS,), jnp.float32)
        Ws2 = xavier(ks[2], (HS, D))
        bs2 = jnp.zeros((D,), jnp.float32)
        We1 = xavier(ks[3], (E, D, 2 * HR))
        be1 = jnp.zeros((E, 2 * HR), jnp.float32)
        We2 = xavier(ks[4], (E, HR, D))
        be2 = jnp.zeros((E, D), jnp.float32)
        Wr = xavier(ks[5], (D, E))
        br = jnp.zeros((E,), jnp.float32)
        return {'x': x, 'Ws1': Ws1, 'bs1': bs1, 'Ws2': Ws2, 'bs2': bs2, 'We1': We1, 'be1': be1, 'We2': We2, 'be2': be2, 'Wr': Wr, 'br': br}
    _L1_ffn_in = _L1_ffn_setup()
    _d = {'L0_attn_x': _L0_attn_in['x'], 'L0_attn_qkv_w': _L0_attn_in['qkv_w'], 'L0_attn_qkv_b': _L0_attn_in['qkv_b'], 'L0_attn_out_w': _L0_attn_in['out_w'], 'L0_attn_out_b': _L0_attn_in['out_b'], 'L0_attn_decay_alpha': _L0_attn_in['decay_alpha'], 'L0_ffn_wqkv': _L0_ffn_in['wqkv'], 'L0_ffn_q_scale': _L0_ffn_in['q_scale'], 'L0_ffn_k_scale': _L0_ffn_in['k_scale'], 'L0_ffn_wo': _L0_ffn_in['wo'], 'L0_ffn_ln_g': _L0_ffn_in['ln_g'], 'L0_ffn_ln_b': _L0_ffn_in['ln_b'], 'L0_ffn_w1': _L0_ffn_in['w1'], 'L0_ffn_b1': _L0_ffn_in['b1'], 'L0_ffn_w2': _L0_ffn_in['w2'], 'L0_ffn_b2': _L0_ffn_in['b2'], 'L1_attn_w_qkv': _L1_attn_in['w_qkv'], 'L1_attn_b_qkv': _L1_attn_in['b_qkv'], 'L1_attn_w_gate': _L1_attn_in['w_gate'], 'L1_attn_b_gate': _L1_attn_in['b_gate'], 'L1_attn_w_proj': _L1_attn_in['w_proj'], 'L1_attn_b_proj': _L1_attn_in['b_proj'], 'L1_attn_ln_g': _L1_attn_in['ln_g'], 'L1_attn_ln_b': _L1_attn_in['ln_b'], 'L1_ffn_Ws1': _L1_ffn_in['Ws1'], 'L1_ffn_bs1': _L1_ffn_in['bs1'], 'L1_ffn_Ws2': _L1_ffn_in['Ws2'], 'L1_ffn_bs2': _L1_ffn_in['bs2'], 'L1_ffn_We1': _L1_ffn_in['We1'], 'L1_ffn_be1': _L1_ffn_in['be1'], 'L1_ffn_We2': _L1_ffn_in['We2'], 'L1_ffn_be2': _L1_ffn_in['be2'], 'L1_ffn_Wr': _L1_ffn_in['Wr'], 'L1_ffn_br': _L1_ffn_in['br']}
    _x0 = _d['L0_attn_x']
    _d['L0_attn_x'] = jax.random.normal(jax.random.fold_in(jax.random.key(seed), 1), (8, 256, 128), dtype=_x0.dtype)
    del _x0
    return _d

def reference(L0_attn_x, L0_attn_qkv_w, L0_attn_qkv_b, L0_attn_out_w, L0_attn_out_b, L0_attn_decay_alpha, L0_ffn_wqkv, L0_ffn_q_scale, L0_ffn_k_scale, L0_ffn_wo, L0_ffn_ln_g, L0_ffn_ln_b, L0_ffn_w1, L0_ffn_b1, L0_ffn_w2, L0_ffn_b2, L1_attn_w_qkv, L1_attn_b_qkv, L1_attn_w_gate, L1_attn_b_gate, L1_attn_w_proj, L1_attn_b_proj, L1_attn_ln_g, L1_attn_ln_b, L1_ffn_Ws1, L1_ffn_bs1, L1_ffn_Ws2, L1_ffn_bs2, L1_ffn_We1, L1_ffn_be1, L1_ffn_We2, L1_ffn_be2, L1_ffn_Wr, L1_ffn_br):

    def _L0_attn_ref(x, qkv_w, qkv_b, out_w, out_b, decay_alpha):
        import jax, jax.numpy as jnp
        import numpy as np
        D_MODEL = 128
        NHEAD = 16
        HEAD_DIM = D_MODEL // NHEAD
        SCALE = float(np.sqrt(HEAD_DIM))
        B, T, D = x.shape
        qkv = x @ qkv_w.T + qkv_b
        qkv = qkv.reshape(B, T, 3, NHEAD, HEAD_DIM).transpose(2, 0, 3, 1, 4)
        q, k, v = (qkv[0], qkv[1], qkv[2])
        logits = jnp.einsum('bhqd,bhkd->bhqk', q, k) / SCALE
        pos = jnp.arange(T, dtype=jnp.float32)
        dist = jnp.abs(pos[None, :] - pos[:, None])
        alpha = jax.nn.softplus(decay_alpha)
        logits = logits - alpha[:, None, None] * dist[None]
        attn = jax.nn.softmax(logits, axis=-1)
        out = jnp.einsum('bhqk,bhkd->bhqd', attn, v)
        out = out.transpose(0, 2, 1, 3).reshape(B, T, D)
        out = out @ out_w.T + out_b
        return out

    def _L0_ffn_ref(x, wqkv, q_scale, k_scale, wo, ln_g, ln_b, w1, b1, w2, b2):
        import jax, jax.numpy as jnp
        import numpy as np
        DIM = 128
        DEPTH = 2
        HEADS = 8
        DIM_HEAD = 64
        WINDOW = 64
        INNER = HEADS * DIM_HEAD
        HID = int(DIM * 4 * 2 / 3)
        B, N = (2, 1024)
        QK_SCALE = 8.0

        def shift_token(t):
            t1, t2 = jnp.split(t, 2, axis=-1)
            t2 = jnp.pad(t2, ((0, 0), (1, 0), (0, 0)))[:, :-1]
            return jnp.concatenate([t1, t2], axis=-1)

        def l2norm(t):
            return t / jnp.clip(jnp.linalg.norm(t, axis=-1, keepdims=True), 1e-12)

        def rotate_half(x):
            x1, x2 = jnp.split(x, 2, axis=-1)
            return jnp.concatenate([-x2, x1], axis=-1)

        def rotary_xpos(q, k):
            n = q.shape[-2]
            half_idx = jnp.arange(0, DIM_HEAD, 2, dtype=jnp.float32)
            inv_freq = 1.0 / 10000.0 ** (half_idx / DIM_HEAD)
            t = jnp.arange(n, dtype=jnp.float32)
            freqs = t[:, None] * inv_freq[None, :]
            freqs = jnp.concatenate([freqs, freqs], axis=-1)
            base = (half_idx + 0.4 * DIM_HEAD) / (1.4 * DIM_HEAD)
            power = (t - n // 2) / float(WINDOW // 2)
            scale = base[None, :] ** power[:, None]
            scale = jnp.concatenate([scale, scale], axis=-1)
            cos, sin = (jnp.cos(freqs), jnp.sin(freqs))
            q = q * cos * scale + rotate_half(q) * sin * scale
            k = k * cos / scale + rotate_half(k) * sin / scale
            return (q, k)

        def local_attention(q, k, v):
            b, h, n, d = q.shape
            w = n // WINDOW
            bq = q.reshape(b, h, w, WINDOW, d) * QK_SCALE
            bk = k.reshape(b, h, w, WINDOW, d)
            bv = v.reshape(b, h, w, WINDOW, d)

            def look_around(t):
                p = jnp.pad(t, ((0, 0), (0, 0), (1, 0), (0, 0), (0, 0)))
                return jnp.concatenate([p[:, :, :w], p[:, :, 1:]], axis=3)
            bk, bv = (look_around(bk), look_around(bv))
            bt = jnp.arange(n).reshape(w, WINDOW)
            btp = jnp.pad(bt, ((1, 0), (0, 0)), constant_values=-1)
            btk = jnp.concatenate([btp[:w], btp[1:]], axis=1)
            sim = jnp.einsum('bhwid,bhwjd->bhwij', bq, bk)
            i = bt[:, :, None]
            j = btk[:, None, :]
            mask = (i < j) | (i > j + WINDOW) | (j == -1)
            sim = jnp.where(mask, -jnp.finfo(sim.dtype).max, sim)
            attn = jax.nn.softmax(sim, axis=-1)
            out = jnp.einsum('bhwij,bhwjd->bhwid', attn, bv)
            return out.reshape(b, h, n, d)

        def _layer(x, wqkv, qs, ksc, wo, lg, lb, w1, b1, w2, b2):
            b, n, _ = x.shape
            h = shift_token(x)
            qkv = h @ wqkv
            q, k, v = jnp.split(qkv, 3, axis=-1)
            to_heads = lambda t: t.reshape(b, n, HEADS, DIM_HEAD).transpose(0, 2, 1, 3)
            q, k, v = (to_heads(q), to_heads(k), to_heads(v))
            q = l2norm(q) * qs
            k = l2norm(k) * ksc
            q, k = rotary_xpos(q, k)
            o = local_attention(q, k, v)
            o = o.transpose(0, 2, 1, 3).reshape(b, n, INNER)
            x = x + o @ wo
            h = shift_token(x)
            mu = h.mean(-1, keepdims=True)
            var = h.var(-1, keepdims=True)
            h = (h - mu) / jnp.sqrt(var + 1e-05) * lg + lb
            h = h @ w1 + b1
            a, g = jnp.split(h, 2, axis=-1)
            h = a * jax.nn.gelu(g, approximate=False)
            x = x + h @ w2 + b2
            return x
        for l in range(DEPTH):
            x = _layer(x, wqkv[l], q_scale[l], k_scale[l], wo[l], ln_g[l], ln_b[l], w1[l], b1[l], w2[l], b2[l])
        return x

    def _L1_attn_ref(x, w_qkv, b_qkv, w_gate, b_gate, w_proj, b_proj, ln_g, ln_b):
        import jax, jax.numpy as jnp
        import numpy as np
        D_MODEL = 128
        B, T = (4, 512)
        LN_EPS = 1e-05
        DEN_EPS = 1e-06
        mu = jnp.mean(x, axis=-1, keepdims=True)
        var = jnp.mean(jnp.square(x - mu), axis=-1, keepdims=True)
        xn = (x - mu) * jax.lax.rsqrt(var + LN_EPS) * ln_g + ln_b
        qkv = xn @ w_qkv + b_qkv
        q, k, v = jnp.split(qkv, 3, axis=-1)
        gate = jax.nn.sigmoid(xn @ w_gate + b_gate)
        k = k * gate
        q = jax.nn.elu(q) + 1.0
        k = jax.nn.elu(k) + 1.0
        attn = jnp.einsum('btd,bsd->bts', q, k)
        tq = jnp.arange(q.shape[1])
        mask = (tq[:, None] >= tq[None, :]).astype(attn.dtype)
        attn = attn * mask
        out_num = jnp.einsum('bts,bsd->btd', attn, v)
        k_cumsum = jnp.cumsum(k, axis=1)
        out_den = jnp.sum(q * k_cumsum, axis=-1, keepdims=True) + DEN_EPS
        return out_num / out_den @ w_proj + b_proj

    def _L1_ffn_ref(x, Ws1, bs1, Ws2, bs2, We1, be1, We2, be2, Wr, br):
        import jax, jax.numpy as jnp
        import numpy as np
        D = 128
        E = 12
        HS = 2 * D
        HR = 3 * D
        TAU = 1.5

        def _geglu(h):
            a, g = jnp.split(h, 2, axis=-1)
            return a * jax.nn.gelu(g, approximate=False)
        B, T, Dm = x.shape
        xf = x.reshape(-1, Dm)
        ys = _geglu(xf @ Ws1 + bs1) @ Ws2 + bs2
        logits = (xf @ Wr + br) / TAU
        top_val, top_idx = jax.lax.top_k(logits, 2)
        top_w = jax.nn.softmax(top_val, axis=-1)
        onehot = jax.nn.one_hot(top_idx, E, dtype=x.dtype)
        w = jnp.einsum('nke,nk->ne', onehot, top_w)
        h = jnp.einsum('nd,edh->enh', xf, We1) + be1[:, None, :]
        act = _geglu(h)
        yE = jnp.einsum('enh,ehd->end', act, We2) + be2[:, None, :]
        yr = jnp.einsum('end,ne->nd', yE, w)
        return (ys + yr).reshape(B, T, Dm)
    x = L0_attn_x
    x = x + 0.5 * _L0_ffn_ref(_layernorm(x, axis=-1), L0_ffn_wqkv, L0_ffn_q_scale, L0_ffn_k_scale, L0_ffn_wo, L0_ffn_ln_g, L0_ffn_ln_b, L0_ffn_w1, L0_ffn_b1, L0_ffn_w2, L0_ffn_b2)
    x = x + _L0_attn_ref(_layernorm(x, axis=-1), L0_attn_qkv_w, L0_attn_qkv_b, L0_attn_out_w, L0_attn_out_b, L0_attn_decay_alpha)
    x = x + 0.5 * _L0_ffn_ref(_layernorm(x, axis=-1), L0_ffn_wqkv, L0_ffn_q_scale, L0_ffn_k_scale, L0_ffn_wo, L0_ffn_ln_g, L0_ffn_ln_b, L0_ffn_w1, L0_ffn_b1, L0_ffn_w2, L0_ffn_b2)
    x = x + 0.5 * _L1_ffn_ref(_layernorm(x, axis=-1), L1_ffn_Ws1, L1_ffn_bs1, L1_ffn_Ws2, L1_ffn_bs2, L1_ffn_We1, L1_ffn_be1, L1_ffn_We2, L1_ffn_be2, L1_ffn_Wr, L1_ffn_br)
    x = x + _L1_attn_ref(_layernorm(x, axis=-1), L1_attn_w_qkv, L1_attn_b_qkv, L1_attn_w_gate, L1_attn_b_gate, L1_attn_w_proj, L1_attn_b_proj, L1_attn_ln_g, L1_attn_ln_b)
    x = x + 0.5 * _L1_ffn_ref(_layernorm(x, axis=-1), L1_ffn_Ws1, L1_ffn_bs1, L1_ffn_Ws2, L1_ffn_bs2, L1_ffn_We1, L1_ffn_be1, L1_ffn_We2, L1_ffn_be2, L1_ffn_Wr, L1_ffn_br)
    return x

_drawn_inputs = setup_inputs


def setup_inputs(seed=0):
    import zlib

    import numpy as np

    out = dict(_drawn_inputs(seed))
    spreads = {'L0_attn_decay_alpha': (0.10000000149011612, 0.6),
     'L0_ffn_q_scale': (1.0, 0.6),
     'L0_ffn_k_scale': (1.0, 0.6),
     'L0_ffn_ln_g': (1.0, 0.6),
     'L0_ffn_ln_b': (0.0, 0.8),
     'L0_ffn_b1': (0.0, 0.8),
     'L0_ffn_b2': (0.0, 0.1),
     'L1_attn_b_qkv': (0.0, 0.468),
     'L1_attn_b_gate': (0.0, 2.0),
     'L1_attn_b_proj': (0.0, 0.5),
     'L1_attn_ln_g': (1.0, 0.6),
     'L1_attn_ln_b': (0.0, 0.518),
     'L1_ffn_bs1': (0.0, 0.756),
     'L1_ffn_bs2': (0.0, 0.541),
     'L1_ffn_be1': (0.0, 0.406),
     'L1_ffn_be2': (0.0, 0.673),
     'L1_ffn_br': (0.0, 2.0)}
    factors = {'L0_ffn_w1': 4.798,
     'L0_ffn_w2': 4.66,
     'L1_attn_w_gate': 64.0,
     'L0_attn_qkv_b': 5.911,
     'L0_attn_out_b': 4.007}
    for name, (base, spread) in spreads.items():
        noise = np.random.default_rng([zlib.crc32(name.encode()), seed]).standard_normal(out[name].shape)
        drawn = base * np.exp(spread * noise) if base else spread * noise
        out[name] = jnp.asarray(drawn.astype(out[name].dtype))
    for name, factor in factors.items():
        out[name] = (out[name] * factor).astype(out[name].dtype)
    return out
```

```python
from collections import namedtuple
from contextlib import ExitStack

import concourse.bass as bass
import numpy as np
from concourse import mybir

F32 = mybir.dt.float32
U32 = mybir.dt.uint32
ALU = mybir.AluOpType
ACT = mybir.ActivationFunctionType
AX_X = mybir.AxisListType.X

P = 128
D = 128
NBATCH, SEQ = 8, 256
NT = NBATCH * SEQ // P
CH = 512
NCH = NT * P // CH
CT = CH // P
DEPTH, LH, LD, WIN = 2, 8, 64, 64
INNER = LH * LD
HID = int(D * 4 * 2 / 3)
HCH = [(0, 128), (128, 128), (256, HID - 256)]
QK_SCALE = 8.0
AH, AD = 16, 8
E, HS, HR, TAU = 12, 2 * D, 3 * D, 1.5
NEG = -1e25
LN_EPS, DEN_EPS = 1e-5, 1e-6
ARENA = 18432

V_BE1, V_BS1, V_B1, V_LG, V_LB, V_QKVB, V_LQKVB, V_LGATE, V_LNG, V_LNB, V_N = (
    0, 72, 76, 88, 90, 92, 95, 98, 99, 100, 101)

SEMS = """
ld_first ld_vec ld_rows ld_late ld_w1 ld_e0 ld_e1 vec_zero vec_ps vec_ready wt_ps wt_ready zeros_set tab_ready
ph_pe ph_act ph_dve ph_pool x_new stats_raw stats_ready rs_var rs_ready ln_done ln_ps ln_T u_copied
hT_ready q_ps k_ps v_ps sq_done rq_ab rk_ab qr_ready kadd_ready ss_raw ss_ready rn_ready rn_self kr_ready qT_ps qT_ready
kT_ps kT_ready v_ready sim_ready mx_ready smax_ready exp_done rden_ready probs_ready pT_ps pT_ready pv_done o_ready
y_ps x1_done
w1_free h_ps m_stats m_raw m_var m_rs hn_ready hnT_ps hT2_ready up_ps gelu_done act_ready dn_ps x1b_ready x2_ready xT_ps
xT_done x2_copied
ustg_ready aq_ps av_ps aq_ready av_ready a_qm a_sim a_mx a_max a_exp a_rd a_prob a_Tps a_Tready a_pv a_o a_yps a_out vm_ready
alpha_ready bias_ready
r_lps r_lsb r_ltps r_max r_idx r_m12 r_e r_w r_wps r_wT r_self s_up s_gelu s_act s_dn s_out e_up e_gelu e_act e_dn e_acc
n_xn n_proj n_min n_exp n_feat n_gexp n_g n_gd n_k n_v n_att n_am n_num n_den n_rec n_o n_oT_ps n_oT n_yps n_out n_fa
out_done fin_x vm_zero rs_self passed
""".split()

Semaphores = namedtuple("Semaphores", SEMS)


class Step:

    def __init__(self, Q=None):
        inner = Q is None
        self.att = inner or 0 <= Q < NT
        self.prev = inner or 1 <= Q <= NT
        self.prev2 = inner or Q >= 2
        self.nx = inner or 0 <= Q + 1 < NT
        self.rv = inner or 0 <= Q + 2 < NT
        self.r1 = inner or Q + 2 >= 1
        self.hv = inner or (Q % 2 == 1 and 0 <= Q + 3 < NT)
        self.first = not inner and Q + 1 <= 0
        self.pairs = None if inner else 4 * Q

    def after(self, n, u):
        return self.pairs is None or self.pairs + u >= n


def rotary_tables():
    f = np.float32
    half = np.arange(0, LD, 2, dtype=f)
    inv = f(1.0) / np.power(f(10000.0), half / f(LD)).astype(f)
    t = np.arange(SEQ, dtype=f)
    fr = (t[:, None] * inv[None, :]).astype(f)
    fr = np.concatenate([fr, fr], -1)
    base = ((half + f(0.4 * LD)) / f(1.4 * LD)).astype(f)
    power = ((t - SEQ // 2) / f(WIN // 2)).astype(f)
    sc = np.power(base[None, :].astype(f), power[:, None]).astype(f)
    sc = np.concatenate([sc, sc], -1)
    sign = np.concatenate([-np.ones(LD // 2, f), np.ones(LD // 2, f)])
    cos, sin = np.cos(fr).astype(f), np.sin(fr).astype(f) * sign
    tabs = np.stack([cos * sc, sin * sc, cos / sc, sin / sc]).astype(f)
    return np.ascontiguousarray(tabs.reshape(4, 2, P, LD).transpose(2, 0, 1, 3))


def constants():
    i, j = np.arange(P)[:, None], np.arange(P)[None, :]
    f = np.float32
    j1 = np.arange(64, SEQ)[None, :]
    band0 = np.where((j <= i) & (i - j <= WIN), 0, NEG).astype(f)
    band1 = np.where((j1 <= i + P) & (i + P - j1 <= WIN), 0, NEG).astype(f)
    jj = np.arange(SEQ)[None, :]
    dist = np.stack([np.abs(jj - i), np.abs(jj - i - P)], 1).astype(f)
    tri = (i <= j).astype(f)
    return {
        "ident": np.eye(P, dtype=f),
        "shift": np.concatenate([(j == i + 1), (i == P - 1) & (j == 0)], 1).astype(f),
        "rot": rotary_tables(),
        "band": np.concatenate([band0, band0, band1, band1], 1),
        "dist": dist,
        "headmask": (i // AD == np.arange(AH)[None, :]).astype(f),
        "causal": np.concatenate([tri, np.ones((P, P), f), tri], 1),
        "iota": np.broadcast_to(np.arange(E, dtype=f)[None, :], (P, E)).copy(),
    }


def build(nc, a, out, stages=99):
    with ExitStack() as ctx:
        def sb(name, shape, dt=F32):
            return ctx.enter_context(nc.sbuf_tensor(name, shape, dt))

        s = Semaphores(*[ctx.enter_context(nc.semaphore(n)) for n in SEMS])
        B = [ctx.enter_context(nc.psum_tensor(f"bank{n}", [P, 512], F32)) for n in range(8)]

        X = sb("X", [P, NT, D])
        U = sb("U", [P, NT, D])
        uT = sb("uT", [P, NT * P])
        ident = sb("ident_sb", [P, P])
        shift = sb("shift_sb", [P, 2, P])
        rot = sb("rot_sb", [P, 4, 2, LD])
        band = sb("band_sb", [P, 640])
        band_of = [band[:, 0:128], band[:, 256:448]]
        dist = sb("dist_sb", [P, 2, SEQ])
        headmask = sb("headmask_sb", [P, AH])
        causal = sb("causal_sb", [P, 384])
        iota = sb("iota_sb", [P, E])
        vec_rows = sb("vec_rows", [P, P])
        vec = sb("vec", [P, V_N])
        mhalf = sb("mhalf", [P, 16])
        ebase = sb("ebase", [P, CT])
        qs_row = sb("qs_row", [P, DEPTH, 2, LD])
        ks_row = sb("ks_row", [P, DEPTH, 2, LD])
        b2_row = sb("b2_row", [P, DEPTH, D])
        bs2_row = sb("bs2_row", [P, D])
        ob_row = sb("ob_row", [P, D])
        bv_row = sb("bv_row", [P, D])
        lbv_row = sb("lbv_row", [P, D])
        lbp_row = sb("lbp_row", [P, D])
        alpha = sb("alpha", [P, AH])
        alpha_w = sb("alpha_w", [P, 3, AH])
        wqkv = sb("wqkv", [P, DEPTH, 3 * INNER])
        wo = sb("wo", [P, DEPTH, 4, D])
        w1 = sb("w1", [P, 2 * HID])
        w2 = sb("w2", [P, DEPTH, 3, D])
        rtab = sb("rtab", [P, DEPTH, 4, 2, LD])
        aw_rows = sb("aw_rows", [P, 4, D])
        awT = sb("awT", [P, 4, D])
        nqkv = sb("nqkv", [P, 3 * D])
        ngate = sb("ngate", [P, D])
        nproj = sb("nproj", [P, D])
        ws1 = sb("ws1", [P, 2 * HS])
        ws2 = sb("ws2", [P, 2, D])
        wr = sb("wr", [P, E])
        br_col = sb("br_col", [E, 2])
        be2 = sb("be2", [E, D])
        wts = sb("wts", [P, NT, E])
        arena = sb("arena", [P, ARENA])

        def cut(start, *shape):
            n = int(np.prod(shape))
            assert start + n <= ARENA
            v = arena[:, start:start + n]
            names = "abc"[:len(shape)]
            if len(shape) > 1:
                sizes = dict(zip(names[1:], shape[1:]))
                v = v.rearrange(f"p ({' '.join(names)}) -> p {' '.join(names)}", **sizes)
            return v

        st6 = sb("st6", [P, CT, 6])
        mv = sb("mv", [P, CT, 2])
        rs = sb("rs", [P, 5, CT])
        stg = sb("stg", [P, CT, D])
        stg_flat = stg[:, :, :].rearrange("p t d -> p (t d)")
        hT = sb("hT", [P, SEQ])
        kT = [cut(n * 2048, 4, 2, SEQ) for n in range(2)]
        qT = [cut(4096 + n * 1024, 4, SEQ) for n in range(2)]
        vv = [cut(6144 + n * 1024, 2, INNER) for n in range(2)]
        rab = cut(8192, 4, INNER)
        sq = cut(10240, 2 * INNER)
        qr = cut(11264, INNER)
        kadd = cut(11776, INNER)
        kr = cut(12288, INNER)
        ss = sb("ss", [P, 2, 16])
        rn = sb("rn", [P, 4, 3, 8])
        rnp = sb("rnp", [P, 16])
        sm = [sb(f"sm{n}", [P, 2, SEQ]) for n in range(2)]
        mx = sb("mx", [P, 2, 2])
        nb = sb("nb", [P, 2, 2])
        den = sb("den", [P, 2, 2])
        rden = sb("rden", [P, 2, 2])
        pA = [sb(f"pA{n}", [P, 2, SEQ]) for n in range(2)]
        pB = [sb(f"pB{n}", [P, 2, SEQ]) for n in range(2)]
        pT = [sb(f"pT{n}", [P, 512]) for n in range(2)]
        oT = sb("oT", [P, 4, P])
        hn = sb("hn", [P, SEQ])
        hT2 = sb("hT2", [P, SEQ])
        gl = sb("gl", [P, 3, CH])
        act_b = sb("act_b", [P, 3, CH])
        x1b = sb("x1b", [P, SEQ])
        xs = sb("xs", [P, SEQ])
        mrs = sb("mrs", [P, 2, 2])
        dbias = cut(0, AH, 2, SEQ)
        VM_AT = 8192
        vm = cut(VM_AT, 2, AH, P)
        qTa = cut(12288, NT * P)
        kTa = cut(14336, NT * P)
        va = cut(16384, NT, D)
        qm = [sb(f"qm{n}", [P, SEQ]) for n in range(2)]
        oTa = sb("oTa", [P, SEQ])
        lgT = sb("lgT", [E, CH])
        lg = sb("lg", [P, CT, E])
        top = sb("top", [P, CT, 8])
        idx = sb("idx", [P, CT, 8], U32)
        idf = sb("idf", [P, CT, 2])
        rw = sb("rw", [P, CT, 4])
        wtmp = sb("wtmp", [P, CT, E])
        wst = sb("wst", [P, CT, E])
        wT = sb("wT", [E, CH])
        we1 = [cut(n * 1152, 2 * HR) for n in range(2)]
        we2 = [cut(n * 1152 + 768, 3, D) for n in range(2)]
        xn = sb("xn", [P, CH])
        qf, kf, z0, z1, z2, noT = (cut(2304 + n * CH, CH) for n in range(6))
        vA = cut(5376, CT, D + 1)
        am = [cut(5892 + n * 384, 384) for n in range(2)]
        osb = cut(6660, CT, D)
        ndr = sb("ndr", [P, 2, CT])

        block = ctx.enter_context(nc.Block())
        engines = ("pe", "act", "dve", "pool")
        done = {"pe": s.ph_pe, "act": s.ph_act, "dve": s.ph_dve, "pool": s.ph_pool}

        def phase_end(eng, me, k):
            eng.drain().then_inc(done[me], 1)
            for other in engines:
                if other != me:
                    eng.wait_ge(done[other], k)
            eng.sem_inc(s.passed, 1)

        def wait_apart(eng, sem, count):
            eng.wait_ge(sem, count)
            eng.sem_inc(s.passed, 1)

        def bc(ap, shape):
            return ap.broadcast_to(shape)

        def heads(ap):
            return ap.rearrange("p (h d) -> p h d", h=LH)

        def flipped(ap):
            return ap.rearrange("p (h a d) -> p h a d", h=LH, a=2)[:, :, ::-1, :]

        N_FIRST, N_VEC, N_ROWS, N_LATE = 10, 21, 13, 14

        def setup_sync(sp):
            def row(ap, n):
                return ap.rearrange("(o n) -> o n", o=1).broadcast_to([P, n])
            first = [(X[:, :, :], a["L0_attn_x"].rearrange("b (t p) d -> p (b t) d", p=P)),
                     (ident[:, :], a["ident"]), (rot[:, :, :, :], a["rot"]), (band[:, :], a["band"]),
                     (wqkv[:, :, :], a["L0_ffn_wqkv"].rearrange("l k n -> k l n")),
                     (wo[:, :, :, :], a["L0_ffn_wo"].rearrange("l (c k) n -> k l c n", k=P)),
                     (shift[:, :, :], a["shift"].rearrange("p (a b) -> p a b", a=2)),
                     (w2[:, 0, 0:2, :], a["L0_ffn_w2"][0, 0:256, :].rearrange("(c k) n -> k c n", k=P)),
                     (w2[:, 1, 0:2, :], a["L0_ffn_w2"][1, 0:256, :].rearrange("(c k) n -> k c n", k=P)),
                     (w2[0:HCH[2][1], :, 2, :], a["L0_ffn_w2"][:, 256:HID, :].rearrange("l k n -> k l n"))]
            assert len(first) == N_FIRST
            for dst, src in first:
                sp.dma_start(dst, src).then_inc(s.ld_first, 16)
            sp.wait_ge(s.vec_zero, 1)
            b1 = a["L0_ffn_b1"]
            vec_loads = [(vec_rows[V_BE1:V_BE1 + 72, :], a["L1_ffn_be1"].rearrange("e (c k) -> (e c) k", k=P)),
                         (vec_rows[V_BS1:V_BS1 + 4, :], a["L1_ffn_bs1"].rearrange("(c k) -> c k", k=P)),
                         (vec_rows[V_LG:V_LG + 2, :], a["L0_ffn_ln_g"]), (vec_rows[V_LB:V_LB + 2, :], a["L0_ffn_ln_b"]),
                         (vec_rows[V_QKVB:V_QKVB + 3, :], a["L0_attn_qkv_b"].rearrange("(c k) -> c k", k=P)),
                         (vec_rows[V_LQKVB:V_LQKVB + 3, :], a["L1_attn_b_qkv"].rearrange("(c k) -> c k", k=P)),
                         (vec_rows[V_LGATE:V_LGATE + 1, :], a["L1_attn_b_gate"].rearrange("(c k) -> c k", k=P)),
                         (vec_rows[V_LNG:V_LNG + 1, :], a["L1_attn_ln_g"].rearrange("(c k) -> c k", k=P)),
                         (vec_rows[V_LNB:V_LNB + 1, :], a["L1_attn_ln_b"].rearrange("(c k) -> c k", k=P))]
            for l in range(DEPTH):
                for g in range(2):
                    for c, (h0, hn_) in enumerate(HCH):
                        r = V_B1 + l * 6 + g * 3 + c
                        vec_loads.append((vec_rows[r:r + 1, 0:hn_], b1[l:l + 1, g * HID + h0:g * HID + h0 + hn_]))
            assert len(vec_loads) == N_VEC
            for dst, src in vec_loads:
                sp.dma_start(dst, src).then_inc(s.ld_vec, 16)
            qs, ks = a["L0_ffn_q_scale"], a["L0_ffn_k_scale"]
            rows = []
            for t, src in ((qs_row, qs), (ks_row, ks)):
                v = src.rearrange("(o l) d -> o l d", o=1)
                rows.append((t[:, :, 0, :], v.broadcast_to([P, DEPTH, LD])))
                for h in range(2):
                    rows.append((t[:, :, 1, 32 * h:32 * h + 32],
                                 v[:, :, 32 - 32 * h:64 - 32 * h].broadcast_to([P, DEPTH, 32])))
            rows += [(b2_row[:, :, :], a["L0_ffn_b2"].rearrange("(o l) d -> o l d", o=1).broadcast_to([P, DEPTH, D])),
                     (bs2_row[:, :], row(a["L1_ffn_bs2"], D)), (ob_row[:, :], row(a["L0_attn_out_b"], D)),
                     (bv_row[:, :], row(a["L0_attn_qkv_b"][2 * D:3 * D], D)),
                     (lbv_row[:, :], row(a["L1_attn_b_qkv"][2 * D:3 * D], D)),
                     (lbp_row[:, :], row(a["L1_attn_b_proj"], D)),
                     (alpha[:, :], row(a["L0_attn_decay_alpha"], AH))]
            assert len(rows) == N_ROWS
            for dst, src in rows:
                sp.dma_start(dst, src).then_inc(s.ld_rows, 16)
            late = [(aw_rows[:, 0:3, :], a["L0_attn_qkv_w"].rearrange("(c p) k -> p c k", p=P)),
                    (aw_rows[:, 3, :], a["L0_attn_out_w"]), (dist[:, :, :], a["dist"]),
                    (headmask[:, :], a["headmask"]), (causal[:, :], a["causal"]), (iota[:, :], a["iota"]),
                    (nqkv[:, :], a["L1_attn_w_qkv"]), (ngate[:, :], a["L1_attn_w_gate"]),
                    (nproj[:, :], a["L1_attn_w_proj"]), (ws1[:, :], a["L1_ffn_Ws1"]),
                    (ws2[:, :, :], a["L1_ffn_Ws2"].rearrange("(c k) n -> k c n", k=P)),
                    (wr[:, :], a["L1_ffn_Wr"]), (br_col[:, 0:1], a["L1_ffn_br"].rearrange("(e o) -> e o", o=1)),
                    (be2[:, :], a["L1_ffn_be2"])]
            assert len(late) == N_LATE
            for dst, src in late:
                sp.dma_start(dst, src).then_inc(s.ld_late, 16)

        def setup_pool(pool):
            pool.memset(vec_rows[:, :], 0.0).then_inc(s.vec_zero, 1)
            zeros = [hT[:, :]]
            for n in range(2):
                zeros += [kT[n][:, :, :, :], pB[n][:, :, :]]
            for z in zeros:
                pool.memset(z, 0.0).then_inc(s.zeros_set, 1)
            pool.memset(mhalf[:, :], -0.5).then_inc(s.zeros_set, 1)
            pool.memset(ebase[:, :], float(np.e)).then_inc(s.zeros_set, 1)
            phase_end(pool, "pool", 1)

        def setup_pe(pe):
            pe.wait_ge(s.ld_first, 16 * N_FIRST)
            pe.wait_ge(s.ld_vec, 16 * N_VEC)
            pe.transpose(B[0][:, 0:P], vec_rows[:, :], ident[:, :]).then_inc(s.vec_ps, 1)
            pe.wait_ge(s.ld_late, 16 * N_LATE)
            for c in range(4):
                t = pe.transpose(B[1][:, c * P:(c + 1) * P], aw_rows[:, c, :], ident[:, :])
            t.then_inc(s.wt_ps, 1)
            phase_end(pe, "pe", 1)

        def setup_act(act):
            act.wait_ge(s.ld_rows, 16 * N_ROWS)
            act.wait_ge(s.alpha_ready, 1)
            act.activation(alpha_w[:, 1, :], alpha_w[:, 0, :], ACT.Exp).then_inc(s.alpha_ready, 1)
            act.wait_ge(s.alpha_ready, 2)
            act.activation(alpha_w[:, 2, :], alpha_w[:, 1, :], ACT.Ln, bias=1.0).then_inc(s.alpha_ready, 1)
            phase_end(act, "act", 1)

        def setup_dve(dve):
            dve.wait_ge(s.ld_first, 16 * N_FIRST)
            dve.wait_ge(s.ld_rows, 16 * N_ROWS)
            dve.scalar_tensor_tensor(alpha_w[:, 0, :], alpha[:, :], -1.0, alpha[:, :], ALU.mult, ALU.min)\
                .then_inc(s.alpha_ready, 1)
            for l in range(DEPTH):
                for kind in range(4):
                    row_ = (qs_row, ks_row)[kind // 2][:, l, kind % 2, :]
                    dve.tensor_tensor(rtab[:, l, kind, :, :], rot[:, kind, :, :],
                                      bc(row_.unsqueeze(1), [P, 2, LD]), ALU.mult).then_inc(s.tab_ready, 1)
            dve.wait_ge(s.vec_ps, 1)
            dve.tensor_copy(vec[:, :], B[0][:, 0:V_N]).then_inc(s.vec_ready, 1)
            dve.wait_ge(s.wt_ps, 1)
            dve.tensor_copy(awT[:, :, :].rearrange("p c d -> p (c d)"), B[1][:, :]).then_inc(s.wt_ready, 1)
            dve.wait_ge(s.ld_late, 16 * N_LATE)
            dve.tensor_scalar(br_col[:, 1:2], br_col[:, 0:1], 1.0 / TAU, None, ALU.mult).then_inc(s.vec_ready, 1)
            dve.wait_ge(s.vec_ready, 2)
            dve.tensor_scalar(vec[:, V_QKVB:V_QKVB + 1], vec[:, V_QKVB:V_QKVB + 1], AD ** -0.5, None, ALU.mult)\
                .then_inc(s.vec_ready, 1)
            dve.wait_ge(s.alpha_ready, 3)
            dve.scalar_tensor_tensor(alpha[:, :], alpha[:, :], 0.0, alpha_w[:, 2, :], ALU.max, ALU.add)\
                .then_inc(s.alpha_ready, 1)
            phase_end(dve, "dve", 1)

        def tr_dve(dve, n, coef, ph):
            with dve.Fori(0, NCH) as c:
                k = c + n * NCH
                xc = X[:, bass.ts(c, CT), :]
                if n:
                    dve.scalar_tensor_tensor(xc, U[:, bass.ts(c, CT), :], coef, xc, ALU.mult, ALU.add)\
                        .then_inc(s.x_new, 1)
                    wait_apart(dve, s.x_new, k - NCH + 1)
                for j in range(CT):
                    dve.bn_stats(st6[:, j, :], X[:, bass.ds(c * CT + j, 1), :].rearrange("p o d -> p (o d)"))\
                        .then_inc(s.stats_raw, 1)
                wait_apart(dve, s.stats_raw, k * CT + CT)
                for j in range(CT):
                    m = dve.bn_aggr(mv[:, j, :], st6[:, j, :])
                m.then_inc(s.stats_ready, 1)
                dve.wait_ge(s.rs_ready, k + 1)
                for j in range(CT):
                    if j == 0:
                        pass
                    m = dve.tensor_scalar(stg[:, j, :], X[:, bass.ds(c * CT + j, 1), :].rearrange("p o d -> p (o d)"),
                                          mv[:, j, 0:1], rs[:, 1, j:j + 1], ALU.subtract, ALU.mult)
                m.then_inc(s.ln_done, 1)
                dve.wait_ge(s.ln_T, k + 1)
                dve.wait_ge(s.u_copied, k + 1)
            phase_end(dve, "dve", ph)

        def vm_zeros(pool):
            pool.memset(vm[:, :, :, :], 0.0).then_inc(s.vm_zero, 1)

        def kT_zeros(pool):
            for n in range(2):
                pool.memset(kT[n][:, :, :, :], 0.0).then_inc(s.zeros_set, 1)

        def vA_ones(pool):
            pool.memset(vA[:, :, D:D + 1], 1.0).then_inc(s.zeros_set, 1)

        def tr_pool(pool, n, ph, extra=None, twice=False):
            if extra:
                extra(pool)
            with pool.Fori(0, NCH) as c:
                k = c + n * NCH
                wait_apart(pool, s.stats_ready, k + 1)
                pool.tensor_scalar(rs[:, 0, :], mv[:, :, 1], LN_EPS, 0.0, ALU.add, ALU.add).then_inc(s.rs_var, 1)
                wait_apart(pool, s.rs_var, k + 1)
                if not twice:
                    pool.tensor_tensor(rs[:, 1, :], rs[:, 0, :], mhalf[:, 0:CT], ALU.pow).then_inc(s.rs_ready, 1)
                else:
                    pool.tensor_tensor(rs[:, 2, :], rs[:, 0, :], mhalf[:, 0:CT], ALU.pow).then_inc(s.rs_self, 1)
                    wait_apart(pool, s.rs_self, 5 * c + 1)
                    pool.tensor_tensor(rs[:, 3, :], rs[:, 2, :], rs[:, 2, :], ALU.mult).then_inc(s.rs_self, 1)
                    wait_apart(pool, s.rs_self, 5 * c + 2)
                    pool.tensor_tensor(rs[:, 4, :], rs[:, 3, :], mv[:, :, 1], ALU.mult).then_inc(s.rs_self, 1)
                    wait_apart(pool, s.rs_self, 5 * c + 3)
                    pool.tensor_scalar(rs[:, 3, :], rs[:, 4, :], LN_EPS, 0.0, ALU.add, ALU.add).then_inc(s.rs_self, 1)
                    wait_apart(pool, s.rs_self, 5 * c + 4)
                    pool.tensor_tensor(rs[:, 4, :], rs[:, 3, :], mhalf[:, 0:CT], ALU.pow).then_inc(s.rs_self, 1)
                    wait_apart(pool, s.rs_self, 5 * c + 5)
                    pool.tensor_tensor(rs[:, 1, :], rs[:, 2, :], rs[:, 4, :], ALU.mult).then_inc(s.rs_ready, 1)
            phase_end(pool, "pool", ph)

        def tr_pe(pe, n, ph):
            with pe.Fori(0, NCH) as c:
                k = c + n * NCH
                pe.wait_ge(s.ln_done, k + 1)
                for j in range(CT):
                    m = pe.transpose(B[0][:, j * P:(j + 1) * P], stg[:, j, :], ident[:, :])
                m.then_inc(s.ln_ps, 1)
                pe.wait_ge(s.ln_T, k + 1)
            phase_end(pe, "pe", ph)

        def tr_act(act, n, ph):
            act.preload_act_table(ACT.Exp)
            with act.Fori(0, NCH) as c:
                k = c + n * NCH
                wait_apart(act, s.ln_done, k + 1)
                act.activation(U[:, bass.ts(c, CT), :], stg[:, :, :], ACT.Copy).then_inc(s.u_copied, 1)
                wait_apart(act, s.ln_ps, k + 1)
                act.activation(uT[:, bass.ts(c, CH)], B[0][:, :], ACT.Copy).then_inc(s.ln_T, 1)
            phase_end(act, "act", ph)

        BQ, BK, BV, BT, BS, BP, BO = B[0], B[1], B[2], B[3], (B[4], B[5]), B[6], B[7]

        def steps(eng, step):
            for q in (1, 2, 3):
                step(-1, q, Step(q - 4))
            for q in range(4):
                step(0, q, Step(q))
            with eng.Fori(1, NT // 4 - 1) as i:
                for q in range(4):
                    f = Step()
                    f.hv = q % 2 == 1
                    step(i, q, f)
            for q in range(4):
                step(NT // 4 - 1, q, Step(NT - 4 + q))
            step(NT // 4, 0, Step(NT))

        def geometry(q):
            t = q % 2
            return (q // 2) % 2, t, (P if t == 0 else 192), (0 if t == 0 else 64)

        def probs(q, par):
            return (pA if q % 2 == 0 else pB)[par]

        def lo_pe(pe, l, pb, ph):
            tb, qb, hb = pb * NT, pb * NT * 4, pb * NBATCH

            def sim(i, q, u, banks_used):
                c, t, nk, k0 = geometry(q % 4)
                Q = 4 * i + q
                if u == 0:
                    pe.wait_ge(s.kT_ready, tb + Q + 1)
                if banks_used:
                    pe.wait_ge(s.smax_ready, qb + 4 * Q + u - 1)
                pe.matmul(BS[u % 2][:, 0:2 * nk], qT[c][:, u, t * P:(t + 1) * P], kT[c][:, u, :, k0:k0 + nk],
                          start=True, stop=True).then_inc(s.sim_ready, 1)

            def turn(i, q, u, bank_used):
                c, t, nk, k0 = geometry(q)
                n = qb + 4 * (4 * i + q) + u
                pe.wait_ge(s.probs_ready, n + 1)
                if bank_used:
                    pe.wait_ge(s.pT_ready, n)
                pr = probs(q, u % 2)
                for j in range(1 + t):
                    for x in range(2):
                        m = pe.transpose(BP[:, (2 * j + x) * P:(2 * j + x + 1) * P], pr[:, x, j * P:(j + 1) * P],
                                         ident[:, :])
                m.then_inc(s.pT_ps, 1)

            def pv(i, q, u, bank_used):
                c, t, nk, k0 = geometry(q)
                n = qb + 4 * (4 * i + q) + u
                pe.wait_ge(s.pT_ready, n + 1)
                if u == 0 and bank_used:
                    pe.wait_ge(s.o_ready, tb + 4 * i + q)
                if u == 0:
                    pe.wait_ge(s.v_ready, tb + 4 * i + q + 1)
                for x in range(2):
                    h = 2 * u + x
                    for j in range(1 + t):
                        m = pe.matmul(BO[64 * x:64 * x + 64, u * P:(u + 1) * P], vv[c][:, j, h * LD:(h + 1) * LD],
                                      pT[u % 2][:, (2 * j + x) * P:(2 * j + x + 1) * P], start=(j == 0), stop=(j == t))
                m.then_inc(s.pv_done, 1)

            def step(i, q, f):
                Q = 4 * i + q
                r = Q + 2
                tr_ = (q + 2) % 2
                for u in range(4):
                    if u < 3:
                        if f.att:
                            sim(i, q, u + 1, f.after(2, u + 1))
                    elif f.nx:
                        sim(i, q + 1, 0, not f.first)
                    if u > 0:
                        if f.att:
                            turn(i, q, u - 1, f.after(1, u - 1))
                    elif f.prev:
                        turn(i if q else i - 1, (q - 1) % 4, 3, True)
                    if u == 0 and f.rv:
                        pe.wait_ge(s.hT_ready, hb + 2 * i + (q + 2) // 2 + 1)
                        if f.r1:
                            pe.wait_ge(s.rq_ab, tb + r)
                        pe.matmul(BQ[:, :], hT[:, tr_ * P:(tr_ + 1) * P], wqkv_l(l, 0), start=True, stop=True)\
                            .then_inc(s.q_ps, 1)
                        if f.r1:
                            pe.wait_ge(s.rk_ab, tb + r)
                        pe.matmul(BK[:, :], hT[:, tr_ * P:(tr_ + 1) * P], wqkv_l(l, 1), start=True, stop=True)\
                            .then_inc(s.k_ps, 1)
                    if u == 1 and f.nx:
                        pe.wait_ge(s.qr_ready, tb + Q + 2)
                        if not f.first:
                            pe.wait_ge(s.kT_ready, tb + Q + 1)
                        for w in range(4):
                            m = pe.transpose(BT[:, w * P:(w + 1) * P], qr[:, w * P:(w + 1) * P], ident[:, :])
                        m.then_inc(s.qT_ps, 1)
                    if u == 1 and f.rv:
                        if f.prev2:
                            pe.wait_ge(s.x1_done, tb + Q - 1)
                        elif f.r1:
                            pe.wait_ge(s.v_ready, tb + r)
                        pe.matmul(BV[:, :], hT[:, tr_ * P:(tr_ + 1) * P], wqkv_l(l, 2), start=True, stop=True)\
                            .then_inc(s.v_ps, 1)
                    if u == 2 and f.nx:
                        pe.wait_ge(s.kr_ready, tb + Q + 2)
                        pe.wait_ge(s.qT_ready, tb + Q + 2)
                        for w in range(4):
                            m = pe.transpose(BT[:, w * P:(w + 1) * P], kr[:, w * P:(w + 1) * P], ident[:, :])
                        m.then_inc(s.kT_ps, 1)
                    if u == 3 and f.prev:
                        pe.wait_ge(s.o_ready, tb + Q)
                        if f.rv:
                            pe.wait_ge(s.v_ready, tb + r + 1)
                        elif f.prev2:
                            pe.wait_ge(s.x1_done, tb + Q - 1)
                        for w in range(4):
                            m = pe.matmul(BV[:, 0:D], oT[:, w, :], wo_l(l, w), start=(w == 0), stop=(w == 3))
                        m.then_inc(s.y_ps, 1)
                    if u >= 2:
                        if f.att:
                            pv(i, q, u - 2, f.prev)
                    elif f.prev:
                        pv(i if q else i - 1, (q - 1) % 4, u + 2, True)

            steps(pe, step)
            phase_end(pe, "pe", ph)

        def wqkv_l(l, k):
            return wqkv[:, bass.ds(l, 1), k * INNER:(k + 1) * INNER].rearrange("p o n -> p (o n)")

        def wo_l(l, w):
            return wo[:, bass.ds(l, 1), w, :].rearrange("p o n -> p (o n)")

        def lo_dve(dve, l, pb, ph):
            tb, qb = pb * NT, pb * NT * 4
            hb = pb * NBATCH

            def table(kind, t):
                v = rtab[:, bass.ds(l, 1), kind, t, :]
                return v

            def step(i, q, f):
                c, t, nk, k0 = geometry(q)
                Q = 4 * i + q
                r = Q + 2
                tr_ = (q + 2) % 2
                for u in range(4):
                    par = u % 2
                    n = qb + 4 * Q + u
                    if f.att:
                        wait_apart(dve, s.sim_ready, n + 1)
                        for x in range(2):
                            m = dve.tensor_tensor_reduce(sm[par][:, x, 0:nk], BS[par][:, x * nk:(x + 1) * nk], band_of[t],
                                                         1.0, -3e38, ALU.add, ALU.max, mx[:, par, x:x + 1])
                        m.then_inc(s.mx_ready, 1)
                        dve.wait_ge(s.mx_ready, n + 1)
                        dve.tensor_tensor(nb[:, par, :], mx[:, par, :], rn[:, q, 2, 2 * u:2 * u + 2], ALU.mult)\
                            .then_inc(s.smax_ready, 1)
                    back = (q, u - 1) if u else ((q - 1) % 4, 3)
                    if (f.att if u else f.prev):
                        bp, nkb, k0b = back[1] % 2, geometry(back[0])[2], geometry(back[0])[3]
                        dve.wait_ge(s.exp_done, n)
                        dve.reciprocal(rden[:, bp, :], den[:, bp, :]).then_inc(s.rden_ready, 1)
                        dve.wait_ge(s.rden_ready, n)
                        pr = probs(back[0], bp)
                        for x in range(2):
                            v = pr[:, x, k0b:k0b + nkb]
                            m = dve.tensor_scalar(v, v, rden[:, bp, x:x + 1], None, ALU.mult)
                        m.then_inc(s.probs_ready, 1)
                    if u == 0 and f.nx:
                        dve.wait_ge(s.rn_ready, tb + Q + 2)
                        dve.wait_ge(s.kadd_ready, tb + Q + 2)
                        if not f.first:
                            dve.wait_ge(s.kT_ps, tb + Q + 1)
                        dve.tensor_tensor(heads(kr[:, :]), heads(kadd[:, :]),
                                          bc(rn[:, (q + 1) % 4, 0, :].unsqueeze(2), [P, LH, LD]), ALU.mult)\
                            .then_inc(s.kr_ready, 1)
                    if u == 1 and f.rv:
                        dve.wait_ge(s.sq_done, tb + r + 1)
                        if f.r1:
                            dve.wait_ge(s.rn_ready, tb + r)
                        dve.tensor_reduce(ss[:, 0, :], sq[:, :].rearrange("p (h d) -> p h d", d=LD), AX_X, ALU.add)\
                            .then_inc(s.ss_raw, 1)
                        dve.wait_ge(s.ss_raw, tb + r + 1)
                        dve.tensor_scalar(ss[:, 1, :], ss[:, 0, :], 1e-24, None, ALU.max).then_inc(s.ss_ready, 1)
                    if f.rv and u in (1, 2, 3):
                        for kind in {1: (0,), 2: (1, 2), 3: (3,)}[u]:
                            bank = BQ if kind < 2 else BK
                            if kind == 0 and f.r1:
                                dve.wait_ge(s.qr_ready, tb + r)
                            if kind == 2 and f.r1:
                                dve.wait_ge(s.kadd_ready, tb + r)
                            if kind % 2 == 0:
                                m = dve.tensor_tensor(heads(rab[:, kind, :]), heads(bank[:, :]),
                                                      bc(table(kind, tr_), [P, LH, LD]), ALU.mult)
                            else:
                                tb_ = table(kind, tr_).rearrange("p o (a d) -> p o a d", a=2)
                                m = dve.tensor_tensor(rab[:, kind, :].rearrange("p (h a d) -> p h a d", h=LH, a=2),
                                                      flipped(bank[:, :]), bc(tb_, [P, LH, 2, LD // 2]), ALU.mult)
                                m.then_inc(s.rq_ab if kind == 1 else s.rk_ab, 1)
                    if u == 3 and f.hv:
                        if f.rv and not (f.first and not f.rv):
                            dve.wait_ge(s.v_ps, tb + r + 1)
                        b = 2 * i + (q + 3) // 2
                        src = uT[:, bass.ts(b, SEQ)]
                        dve.tensor_copy(hT[0:64, :], src[0:64, :])
                        dve.tensor_copy(hT[64:128, 1:SEQ], src[64:128, 0:SEQ - 1]).then_inc(s.hT_ready, 1)
                    if u == 3 and f.prev:
                        dve.wait_ge(s.y_ps, tb + Q)
                        ut = U[:, bass.ds(Q - 1, 1), :].rearrange("p o d -> p (o d)")
                        dve.tensor_tensor(ut, BV[:, 0:D], ut, ALU.add).then_inc(s.x1_done, 1)

            steps(dve, step)
            phase_end(dve, "dve", ph)

        def lo_act(act, l, pb, ph):
            tb, qb = pb * NT, pb * NT * 4
            act.preload_act_table(ACT.Exp)

            def pt_evac(q, u, n):
                act.wait_ge(s.pT_ps, n)
                cols = 256 * (1 + q % 2)
                act.activation(pT[u % 2][:, 0:cols], BP[:, 0:cols], ACT.Copy).then_inc(s.pT_ready, 1)

            def step(i, q, f):
                c, t, nk, k0 = geometry(q)
                Q = 4 * i + q
                r = Q + 2
                for u in range(4):
                    par = u % 2
                    n = qb + 4 * Q + u
                    if f.att:
                        act.wait_ge(s.smax_ready, n + 1)
                        pr = probs(q, par)
                        for x in range(2):
                            m = act.activation(pr[:, x, k0:k0 + nk], sm[par][:, x, 0:nk], ACT.Exp,
                                               bias=nb[:, par, x:x + 1], scale=rn[:, q, 1, 2 * u + x:2 * u + x + 1],
                                               accum_out=den[:, par, x:x + 1])
                        m.then_inc(s.exp_done, 1)
                    bq, bu = (q, u - 1) if u else ((q - 1) % 4, 3)
                    if (f.att if u else f.prev):
                        if f.after(3, u):
                            act.wait_ge(s.pv_done, n - 2)
                        pt_evac(bq, bu, n)
                    if u == 0 and f.rv:
                        act.wait_ge(s.q_ps, tb + r + 1)
                        if f.r1:
                            act.wait_ge(s.ss_raw, tb + r)
                        act.activation(sq[:, 0:INNER], BQ[:, :], ACT.Square)
                        act.wait_ge(s.k_ps, tb + r + 1)
                        act.activation(sq[:, INNER:], BK[:, :], ACT.Square).then_inc(s.sq_done, 1)
                    if u == 1 and f.nx:
                        c1, t1, _, _ = geometry((q + 1) % 4)
                        act.wait_ge(s.qT_ps, tb + Q + 2)
                        act.activation(qT[c1][:, :, t1 * P:(t1 + 1) * P], BT[:, :].rearrange("p (w t) -> p w t", w=4),
                                       ACT.Copy).then_inc(s.qT_ready, 1)
                    if u == 2 and f.prev:
                        act.wait_ge(s.pv_done, qb + 4 * Q)
                        if f.prev2:
                            act.wait_ge(s.y_ps, tb + Q - 1)
                        act.activation(oT[:, :, :].rearrange("p w t -> p (w t)"), BO[:, :], ACT.Copy)\
                            .then_inc(s.o_ready, 1)
                    if u == 2 and f.nx:
                        act.wait_ge(s.kT_ps, tb + Q + 2)
                        for x in range(2):
                            m = act.activation(kT[c1][64 * x:64 * x + 64, :, x, t1 * P:(t1 + 1) * P],
                                               BT[64 * x:64 * x + 64, :].rearrange("p (w t) -> p w t", w=4), ACT.Copy)
                        m.then_inc(s.kT_ready, 1)
                    if u == 2 and f.rv:
                        cr, trr, _, _ = geometry((q + 2) % 4)
                        act.wait_ge(s.v_ps, tb + r + 1)
                        act.activation(vv[cr][:, trr, :], BV[:, :], ACT.Copy).then_inc(s.v_ready, 1)

            steps(act, step)
            phase_end(act, "act", ph)

        def lo_pool(pool, l, pb, ph):
            tb, qb = pb * NT, pb * NT * 4

            def step(i, q, f):
                Q = 4 * i + q
                r = Q + 2
                rq = (q + 2) % 4
                if f.rv:
                    wait_apart(pool, s.ss_ready, tb + r + 1)
                    pool.tensor_tensor(rnp[:, :], ss[:, 1, :], mhalf[:, :], ALU.pow).then_inc(s.rn_self, 1)
                    wait_apart(pool, s.rn_self, tb + r + 1)
                    pool.tensor_scalar(rn[:, rq, 1, :], rnp[:, 0:8], QK_SCALE, 1.0, ALU.mult, ALU.mult)
                    pool.tensor_scalar(rn[:, rq, 2, :], rnp[:, 0:8], -QK_SCALE, 1.0, ALU.mult, ALU.mult)
                    pool.tensor_scalar(rn[:, rq, 0, :], rnp[:, 8:16], 1.0, 1.0, ALU.mult, ALU.mult)\
                        .then_inc(s.rn_ready, 1)
                    wait_apart(pool, s.rq_ab, tb + r + 1)
                    if f.r1:
                        wait_apart(pool, s.qT_ps, tb + r)
                    pool.tensor_tensor(qr[:, :], rab[:, 0, :], rab[:, 1, :], ALU.add).then_inc(s.qr_ready, 1)
                    wait_apart(pool, s.rk_ab, tb + r + 1)
                    if f.r1:
                        wait_apart(pool, s.kr_ready, tb + r)
                    pool.tensor_tensor(kadd[:, :], rab[:, 2, :], rab[:, 3, :], ALU.add).then_inc(s.kadd_ready, 1)

            steps(pool, step)
            phase_end(pool, "pool", ph)

        MH, MT, MG, MY, MX = B[0], B[1], (B[2], B[3], B[4]), B[5], B[6]

        def over_batches(eng, head, body, tail):
            head(0)
            body(0, True, True)
            with eng.Fori(1, NBATCH - 1) as b:
                body(b, False, True)
            body(NBATCH - 1, False, False)
            tail(NBATCH)

        def ff_pe(pe, l, pb, ph):
            hb = pb * NBATCH

            def shifted(b):
                if isinstance(b, int) and b == 0:
                    pass
                else:
                    pe.wait_ge(s.hn_ready, hb + b)
                h3 = MH[:, 0:SEQ].rearrange("p (t d) -> p t d", t=2)
                ub = U[:, bass.ts(b, 2), :]
                pe.matmul(h3[:, :, 0:64], ident[:, :], ub[:, :, 0:64], start=True, stop=True)
                pe.matmul(h3[:, :, 64:128], shift[:, 0, :], ub[:, :, 64:128], start=True, stop=False,
                          skip_group_check=True)
                pe.matmul(h3[:, 1, 64:128], shift[:, 1, :], ub[:, 0, 64:128], start=False, stop=True,
                          skip_group_check=True).then_inc(s.h_ps, 1)

            def turned(b):
                pe.wait_ge(s.hn_ready, hb + b + 1)
                for t in range(2):
                    m = pe.transpose(MT[:, t * P:(t + 1) * P], hn[:, t * P:(t + 1) * P], ident[:, :])
                m.then_inc(s.hnT_ps, 1)

            def x_turned(b):
                pe.wait_ge(s.x2_ready, hb + b)
                if not (isinstance(b, int) and b == 1):
                    pe.wait_ge(s.xT_done, hb + b - 1)
                for t in range(2):
                    m = pe.transpose(MX[:, t * P:(t + 1) * P], xs[:, t * P:(t + 1) * P], ident[:, :])
                m.then_inc(s.xT_ps, 1)

            def head(b):
                shifted(b)
                turned(b)

            def body(b, is_first, more):
                if more:
                    shifted(b + 1)
                pe.wait_ge(s.hT2_ready, hb + b + 1)
                for c, (h0, n) in enumerate(HCH):
                    if c == 0 and not is_first:
                        pe.wait_ge(s.act_ready, 3 * (hb + b))
                    for g in range(2):
                        m = pe.matmul(MG[c][0:n, g * SEQ:(g + 1) * SEQ], w1[:, g * HID + h0:g * HID + h0 + n], hT2[:, :],
                                      start=True, stop=True)
                    m.then_inc(s.up_ps, 1)
                if more:
                    turned(b + 1)
                if not is_first:
                    x_turned(b)
                pe.wait_ge(s.act_ready, 3 * (hb + b) + 3)
                for t in range(2):
                    for c, (h0, n) in enumerate(HCH):
                        m = pe.matmul(MY[:, t * P:(t + 1) * P], act_b[0:n, c, t * P:(t + 1) * P],
                                      w2[0:n, bass.ds(l, 1), c, :].rearrange("p o d -> p (o d)"),
                                      start=(c == 0), stop=(c == 2))
                m.then_inc(s.dn_ps, 1)

            pe.wait_ge(s.ld_w1, 16 * (pb + 1))
            over_batches(pe, head, body, x_turned)
            phase_end(pe, "pe", ph)

        def ff_dve(dve, l, pb, ph):
            hb = pb * NBATCH

            def stats(b):
                dve.wait_ge(s.h_ps, hb + b + 1)
                for t in range(2):
                    dve.bn_stats(st6[:, t, :], MH[:, t * P:(t + 1) * P]).then_inc(s.m_raw, 1)
                wait_apart(dve, s.m_raw, 2 * (hb + b) + 2)
                for t in range(2):
                    m = dve.bn_aggr(mv[:, t, :], st6[:, t, :])
                m.then_inc(s.m_stats, 1)

            def normed(b, is_first=False):
                dve.wait_ge(s.m_rs, hb + b + 1)
                if not is_first:
                    dve.wait_ge(s.hnT_ps, hb + b)
                for t in range(2):
                    m = dve.tensor_scalar(hn[:, t * P:(t + 1) * P], MH[:, t * P:(t + 1) * P], mv[:, t, 0:1],
                                          mrs[:, 1, t:t + 1], ALU.subtract, ALU.mult)
                m.then_inc(s.hn_ready, 1)

            def head(b):
                stats(b)
                normed(b, True)

            def body(b, is_first, more):
                if more:
                    stats(b + 1)
                for c, (h0, n) in enumerate(HCH):
                    dve.wait_ge(s.gelu_done, 3 * (hb + b) + c + 1)
                    if c == 0 and not is_first:
                        dve.wait_ge(s.dn_ps, hb + b)
                    row_a = V_B1 + c
                    ba = vec[0:n, bass.ds(l * 6 + row_a, 1)]
                    dve.scalar_tensor_tensor(act_b[0:n, c, 0:SEQ], MG[c][0:n, 0:SEQ], ba, gl[0:n, c, 0:SEQ],
                                             ALU.add, ALU.mult).then_inc(s.act_ready, 1)
                    if c == 0 and more:
                        normed(b + 1)
                dve.wait_ge(s.dn_ps, hb + b + 1)
                dve.wait_ge(s.x1b_ready, hb + b + 1)
                if not is_first:
                    dve.wait_ge(s.xT_ps, hb + b)
                    dve.wait_ge(s.x2_copied, hb + b)
                dve.tensor_tensor(xs[:, :], MY[:, 0:SEQ], x1b[:, :], ALU.add).then_inc(s.x2_ready, 1)

            over_batches(dve, head, body, lambda b: None)
            phase_end(dve, "dve", ph)

        def ff_act(act, l, pb, ph):
            hb = pb * NBATCH
            act.preload_act_table(ACT.Gelu)

            def head(b):
                wait_apart(act, s.hnT_ps, hb + b + 1)
                act.activation(hT2[:, :], MT[:, 0:SEQ], ACT.Identity, bias=vec[:, bass.ds(l + V_LB, 1)],
                               scale=vec[:, bass.ds(l + V_LG, 1)]).then_inc(s.hT2_ready, 1)

            def x_out(b):
                wait_apart(act, s.xT_ps, hb + b)
                act.activation(uT[:, bass.ts(b - 1, SEQ)], MX[:, 0:SEQ], ACT.Copy).then_inc(s.xT_done, 1)

            def body(b, is_first, more):
                for c, (h0, n) in enumerate(HCH):
                    wait_apart(act, s.up_ps, 3 * (hb + b) + c + 1)
                    act.activation(gl[0:n, c, 0:SEQ], MG[c][0:n, SEQ:2 * SEQ], ACT.Gelu,
                                   bias=vec[0:n, bass.ds(l * 6 + V_B1 + 3 + c, 1)]).then_inc(s.gelu_done, 1)
                if more:
                    head(b + 1)
                if not is_first:
                    x_out(b)

            over_batches(act, head, body, x_out)
            phase_end(act, "act", ph)

        def ff_pool(pool, l, pb, ph):
            hb = pb * NBATCH

            def head(b):
                wait_apart(pool, s.m_stats, hb + b + 1)
                pool.tensor_scalar(mrs[:, 0, :], mv[:, 0:2, 1], LN_EPS, 0.0, ALU.add, ALU.add).then_inc(s.m_var, 1)
                wait_apart(pool, s.m_var, hb + b + 1)
                pool.tensor_tensor(mrs[:, 1, :], mrs[:, 0, :], mhalf[:, 0:2], ALU.pow).then_inc(s.m_rs, 1)

            def body(b, is_first, more):
                if not is_first:
                    wait_apart(pool, s.x2_ready, hb + b)
                pool.tensor_tensor(x1b[:, :].rearrange("p (t d) -> p t d", t=2), U[:, bass.ts(b, 2), :],
                                   bc(b2_row[:, bass.ds(l, 1), :], [P, 2, D]), ALU.add).then_inc(s.x1b_ready, 1)
                if more:
                    head(b + 1)
                wait_apart(pool, s.x2_ready, hb + b + 1)
                wait_apart(pool, s.h_ps, hb + b + 1)
                pool.tensor_copy(U[:, bass.ts(b, 2), :], xs[:, :].rearrange("p (t d) -> p t d", t=2))\
                    .then_inc(s.x2_copied, 1)

            over_batches(pool, head, body, lambda b: None)
            phase_end(pool, "pool", ph)

        def ffn_sync(sp, site, ph0):
            with sp.Fori(0, DEPTH) as l:
                pb = l + site * DEPTH
                sp.wait_ge(s.ph_pe, ph0 + 2 * l)
                sp.dma_start(w1[:, :], a["L0_ffn_w1"][bass.ds(l, 1), :, :].rearrange("o k n -> (o k) n"))\
                    .then_inc(s.ld_w1, 16)

        def ffn(eng, name, site, ph0):
            parts = {"pe": (lo_pe, ff_pe), "act": (lo_act, ff_act), "dve": (lo_dve, ff_dve),
                     "pool": (lo_pool, ff_pool)}[name]
            with eng.Fori(0, DEPTH) as l:
                pb = l + site * DEPTH
                parts[0](eng, l, pb, ph0 + 1 + 2 * l)
                parts[1](eng, l, pb, ph0 + 2 + 2 * l)

        def ap_pe(pe, ph):
            with pe.Fori(0, NCH) as c:
                for k in range(2):
                    m = pe.matmul(B[k][:, :], awT[:, k, :], uT[:, bass.ts(c, CH)], start=True, stop=True)
                m.then_inc(s.aq_ps, 1)
                pe.wait_ge(s.ustg_ready, c + 1)
                for j in range(CT):
                    m = pe.matmul(B[2][:, j * P:(j + 1) * P], xn[:, j * P:(j + 1) * P], awT[:, 2, :],
                                  start=True, stop=True)
                m.then_inc(s.av_ps, 1)
                pe.wait_ge(s.aq_ready, c + 1)
                pe.wait_ge(s.av_ready, c + 1)
            phase_end(pe, "pe", ph)

        def ap_act(act, ph):
            act.preload_act_table(ACT.Exp)
            with act.Fori(0, NCH) as c:
                act.wait_ge(s.aq_ps, c + 1)
                act.activation(qTa[:, bass.ts(c, CH)], B[0][:, :], ACT.Identity, bias=vec[:, V_QKVB:V_QKVB + 1],
                               scale=AD ** -0.5)
                act.activation(kTa[:, bass.ts(c, CH)], B[1][:, :], ACT.Identity,
                               bias=vec[:, V_QKVB + 1:V_QKVB + 2]).then_inc(s.aq_ready, 1)
            phase_end(act, "act", ph)

        def ap_dve(dve, ph):
            dve.wait_ge(s.alpha_ready, 4)
            for h in range(AH):
                dve.tensor_scalar(dbias[:, h, :, :], dist[:, :, :], alpha[:, h:h + 1], -1.0, ALU.mult, ALU.mult)\
                    .then_inc(s.bias_ready, 1)
            with dve.Fori(0, NCH) as c:
                dve.tensor_copy(xn[:, :], uT[:, bass.ts(c, CH)]).then_inc(s.ustg_ready, 1)
                dve.wait_ge(s.av_ps, c + 1)
                dve.tensor_tensor(va[:, bass.ts(c, CT), :], B[2][:, :].rearrange("p (t d) -> p t d", t=CT),
                                  bc(bv_row[:, :].unsqueeze(1), [P, CT, D]), ALU.add).then_inc(s.av_ready, 1)
            phase_end(dve, "dve", ph)

        AS, AP_, AO, AY = (B[4], B[5]), (B[6], B[3]), B[7], B[2]

        def over_sequences(eng, body, tail):
            body(0, True, False)
            with eng.Fori(1, NBATCH - 1) as b:
                body(b, False, False)
            body(NBATCH - 1, False, True)
            tail(NBATCH)

        def aa_pe(pe, ph):
            def sim(b, h):
                n = b * AH + h
                pe.wait_ge(s.a_qm, n + 1)
                if not (isinstance(n, int) and n < 2):
                    pe.wait_ge(s.a_max, n - 1)
                for t in range(2):
                    m = pe.matmul(AS[h % 2][:, t * SEQ:(t + 1) * SEQ], qm[h % 2][:, t * P:(t + 1) * P],
                                  kTa[:, bass.ts(b, SEQ)], start=True, stop=True)
                m.then_inc(s.a_sim, 1)

            def turn(b, h):
                n = b * AH + h
                pe.wait_ge(s.a_prob, n + 1)
                if not (isinstance(n, int) and n < 2):
                    pe.wait_ge(s.a_Tready, n - 1)
                for j in range(2):
                    for t in range(2):
                        m = pe.transpose(AP_[h % 2][:, (2 * j + t) * P:(2 * j + t + 1) * P],
                                         pA[h % 2][:, t, j * P:(j + 1) * P], ident[:, :])
                m.then_inc(s.a_Tps, 1)

            def pv(b, h):
                n = b * AH + h
                pe.wait_ge(s.a_Tready, n + 1)
                if h == 0:
                    pe.wait_ge(s.vm_ready, b + 1)
                    if not (isinstance(b, int) and b == 0):
                        pe.wait_ge(s.a_o, b)
                for j in range(2):
                    m = pe.matmul(AO[:, 0:SEQ], vm[:, j, h, :], pT[h % 2][:, j * SEQ:(j + 1) * SEQ],
                                  start=(h == 0 and j == 0), stop=(h == AH - 1 and j == 1))
                m.then_inc(s.a_pv, 1)

            def out_proj(b):
                pe.wait_ge(s.a_o, b)
                if not (isinstance(b, int) and b == 1):
                    pe.wait_ge(s.a_out, b - 1)
                for t in range(2):
                    m = pe.matmul(AY[:, t * P:(t + 1) * P], oTa[:, t * P:(t + 1) * P], awT[:, 3, :],
                                  start=True, stop=True)
                m.then_inc(s.a_yps, 1)

            def body(b, is_first, is_last):
                for h in range(AH):
                    if h + 1 < AH:
                        sim(b, h + 1)
                    elif not is_last:
                        sim(b + 1, 0)
                    if h >= 1:
                        turn(b, h - 1)
                    elif not is_first:
                        turn(b - 1, AH - 1)
                    if h >= 2:
                        pv(b, h - 2)
                    elif not is_first:
                        pv(b - 1, AH - 2 + h)
                    if h == 3 and not is_first:
                        out_proj(b)

            def tail(b):
                turn(b - 1, AH - 1)
                pv(b - 1, AH - 2)
                pv(b - 1, AH - 1)
                out_proj(b)

            sim(0, 0)
            over_sequences(pe, body, tail)
            phase_end(pe, "pe", ph)

        def aa_dve(dve, ph):
            def masked(b, h):
                dve.tensor_scalar(qm[h % 2][:, :], qTa[:, bass.ts(b, SEQ)], headmask[:, h:h + 1], None, ALU.mult)\
                    .then_inc(s.a_qm, 1)

            def scaled(n, par):
                dve.wait_ge(s.a_exp, n)
                dve.reciprocal(rden[:, par, :], den[:, par, :]).then_inc(s.a_rd, 1)
                dve.wait_ge(s.a_rd, n)
                for t in range(2):
                    m = dve.tensor_scalar(pA[par][:, t, :], pA[par][:, t, :], rden[:, par, t:t + 1], None, ALU.mult)
                m.then_inc(s.a_prob, 1)

            def result(b):
                dve.wait_ge(s.a_yps, b)
                dve.tensor_tensor(U[:, bass.ts(b - 1, 2), :], AY[:, 0:SEQ].rearrange("p (t d) -> p t d", t=2),
                                  bc(ob_row[:, :].unsqueeze(1), [P, 2, D]), ALU.add).then_inc(s.a_out, 1)

            def body(b, is_first, is_last):
                for h in range(AH):
                    n = b * AH + h
                    par = h % 2
                    wait_apart(dve, s.a_sim, n + 1)
                    for t in range(2):
                        m = dve.tensor_tensor_reduce(sm[par][:, t, :], AS[par][:, t * SEQ:(t + 1) * SEQ],
                                                     dbias[:, h, t, :], 1.0, -3e38, ALU.add, ALU.max,
                                                     mx[:, par, t:t + 1])
                    m.then_inc(s.a_mx, 1)
                    dve.wait_ge(s.a_mx, n + 1)
                    dve.tensor_scalar(nb[:, par, :], mx[:, par, :], -1.0, None, ALU.mult).then_inc(s.a_max, 1)
                    if h + 2 < AH:
                        masked(b, h + 2)
                    elif not is_last:
                        masked(b + 1, h + 2 - AH)
                    if not (is_first and h == 0):
                        scaled(n, 1 - par)
                    if h == 5 and not is_first:
                        result(b)

            def tail(b):
                scaled(AH * b, 1)
                result(b)

            masked(0, 0)
            masked(0, 1)
            over_sequences(dve, body, tail)
            phase_end(dve, "dve", ph)

        def aa_act(act, ph):
            act.preload_act_table(ACT.Exp)

            def evac(n, par, back_ok):
                act.wait_ge(s.a_Tps, n)
                if back_ok:
                    act.wait_ge(s.a_pv, n - 2)
                act.activation(pT[par][:, :], AP_[par][:, :], ACT.Copy).then_inc(s.a_Tready, 1)

            def outs(b):
                act.wait_ge(s.a_pv, AH * b)
                if not (isinstance(b, int) and b == 1):
                    act.wait_ge(s.a_yps, b - 1)
                act.activation(oTa[:, :], AO[:, 0:SEQ], ACT.Copy).then_inc(s.a_o, 1)

            def body(b, is_first, is_last):
                for h in range(AH):
                    n = b * AH + h
                    par = h % 2
                    act.wait_ge(s.a_max, n + 1)
                    for t in range(2):
                        m = act.activation(pA[par][:, t, :], sm[par][:, t, :], ACT.Exp, bias=nb[:, par, t:t + 1],
                                           accum_out=den[:, par, t:t + 1])
                    m.then_inc(s.a_exp, 1)
                    if not (is_first and h == 0):
                        evac(n, 1 - par, not (is_first and h < 3))
                    if h == 1 and not is_first:
                        outs(b)

            def tail(b):
                evac(AH * b, 1, True)
                outs(b)

            over_sequences(act, body, tail)
            phase_end(act, "act", ph)

        def aa_pool(pool, ph):
            pool.wait_ge(s.vm_zero, 1)

            def spread(b):
                for t in range(2):
                    blocks = bass.AP(tensor=arena, offset=VM_AT + t * AH * P, ap=[[ARENA, P], [P + AD, AH], [1, AD]])
                    m = pool.tensor_copy(blocks, va[:, bass.ds(b * 2 + t, 1), :]
                                         .rearrange("p o (h d) -> p (o h) d", h=AH))
                m.then_inc(s.vm_ready, 1)

            spread(0)
            with pool.Fori(1, NBATCH) as b:
                wait_apart(pool, s.a_pv, AH * b)
                spread(b)
            phase_end(pool, "pool", ph)

        def mr_pe(pe, k0, ph):
            with pe.Fori(0, NCH) as c:
                k = c + k0 * NCH
                uc = uT[:, bass.ts(c, CH)]
                pe.matmul(B[0][0:E, :], wr[:, :], uc, start=True, stop=True).then_inc(s.r_lps, 1)
                for g in range(2):
                    for half in range(2):
                        m = pe.matmul(B[1 + 2 * g + half][:, :], ws1[:, (2 * half + g) * P:(2 * half + g + 1) * P], uc,
                                      start=True, stop=True)
                    m.then_inc(s.s_up, 1)
                wait_apart(pe, s.r_lsb, k + 1)
                for j in range(CT):
                    m = pe.transpose(B[0][:, j * E:(j + 1) * E], lgT[:, j * P:(j + 1) * P], ident[0:E, 0:E])
                m.then_inc(s.r_ltps, 1)
                pe.wait_ge(s.r_w, 3 * k + 3)
                for j in range(CT):
                    m = pe.transpose(B[6][0:E, j * P:(j + 1) * P], wst[:, j, :], ident[:, :])
                m.then_inc(s.r_wps, 1)
                pe.wait_ge(s.r_wT, k + 1)
                pe.wait_ge(s.s_act, 2 * k + 2)
                for j in range(CT):
                    js = slice(j * P, (j + 1) * P)
                    pe.matmul(B[5][:, js], act_b[:, 0, js], ws2[:, 0, :], start=True, stop=False)
                    pe.matmul(B[5][:, js], act_b[:, 1, js], ws2[:, 1, :], start=False, stop=False)
                    m = pe.matmul(B[5][:, js], wT[:, js], be2[:, :], start=False, stop=True)
                m.then_inc(s.s_dn, 1)
                pe.wait_ge(s.s_out, k + 1)
            phase_end(pe, "pe", ph)

        def mr_act(act, k0, ph):
            act.preload_act_table(ACT.Gelu)
            with act.Fori(0, NCH) as c:
                k = c + k0 * NCH
                wait_apart(act, s.r_lps, k + 1)
                act.activation(lgT[:, :], B[0][0:E, :], ACT.Identity, bias=br_col[:, 1:2], scale=1.0 / TAU)\
                    .then_inc(s.r_lsb, 1)
                for g in range(2):
                    wait_apart(act, s.s_up, 2 * k + g + 1)
                    act.activation(gl[:, g, :], B[2 + 2 * g][:, :], ACT.Gelu, bias=vec[:, V_BS1 + 2 + g:V_BS1 + 3 + g])\
                        .then_inc(s.s_gelu, 1)
                wait_apart(act, s.r_wps, k + 1)
                act.activation(wT[:, :], B[6][0:E, :], ACT.Copy).then_inc(s.r_wT, 1)
            phase_end(act, "act", ph)

        def mr_dve(dve, k0, ph):
            with dve.Fori(0, NCH) as c:
                k = c + k0 * NCH
                dve.wait_ge(s.r_ltps, k + 1)
                dve.tensor_copy(lg[:, :, :].rearrange("p t e -> p (t e)"), B[0][:, 0:CT * E]).then_inc(s.r_max, 1)
                wait_apart(dve, s.r_max, 2 * k + 1)
                for j in range(CT):
                    m = dve.max(top[:, j, :], lg[:, j, :])
                m.then_inc(s.r_max, 1)
                wait_apart(dve, s.r_max, 2 * k + 2)
                for j in range(CT):
                    m = dve.max_index(idx[:, j, :], top[:, j, :], lg[:, j, :])
                m.then_inc(s.r_idx, 1)
                dve.tensor_tensor(rw[:, :, 0], top[:, :, 1], top[:, :, 0], ALU.subtract).then_inc(s.r_m12, 1)
                for g in range(2):
                    dve.wait_ge(s.s_gelu, 2 * k + g + 1)
                    dve.scalar_tensor_tensor(act_b[:, g, :], B[1 + 2 * g][:, :], vec[:, V_BS1 + g:V_BS1 + g + 1],
                                             gl[:, g, :], ALU.add, ALU.mult).then_inc(s.s_act, 1)
                wait_apart(dve, s.r_idx, k + 1)
                dve.tensor_copy(idf[:, :, :], idx[:, :, 0:2]).then_inc(s.r_self, 1)
                dve.wait_ge(s.r_e, k + 1)
                dve.tensor_scalar(rw[:, :, 0], rw[:, :, 1], 1.0, None, ALU.add).then_inc(s.r_self, 1)
                dve.wait_ge(s.r_self, 5 * k + 2)
                dve.reciprocal(rw[:, :, 2], rw[:, :, 0]).then_inc(s.r_self, 1)
                dve.wait_ge(s.r_self, 5 * k + 3)
                dve.tensor_tensor(rw[:, :, 3], rw[:, :, 1], rw[:, :, 2], ALU.mult).then_inc(s.r_self, 1)
                dve.wait_ge(s.r_self, 5 * k + 4)
                for j in range(CT):
                    dve.tensor_scalar(wtmp[:, j, :], iota[:, :], idf[:, j, 0:1], rw[:, j, 2:3], ALU.is_equal, ALU.mult)
                    m = dve.tensor_scalar(wst[:, j, :], iota[:, :], idf[:, j, 1:2], rw[:, j, 3:4], ALU.is_equal, ALU.mult)
                m.then_inc(s.r_w, 1)
                dve.wait_ge(s.r_w, 3 * k + 1)
                dve.tensor_tensor(wst[:, :, :], wst[:, :, :], wtmp[:, :, :], ALU.add).then_inc(s.r_w, 1)
                dve.wait_ge(s.r_w, 3 * k + 2)
                dve.tensor_copy(wts[:, bass.ts(c, CT), :], wst[:, :, :]).then_inc(s.r_w, 1)
                dve.wait_ge(s.s_dn, k + 1)
                dve.tensor_tensor(U[:, bass.ts(c, CT), :], B[5][:, :].rearrange("p (t d) -> p t d", t=CT),
                                  bc(bs2_row[:, :].unsqueeze(1), [P, CT, D]), ALU.add).then_inc(s.s_out, 1)
                dve.sem_inc(s.r_self, 1)
            phase_end(dve, "dve", ph)

        def mr_pool(pool, k0, ph):
            with pool.Fori(0, NCH) as c:
                k = c + k0 * NCH
                wait_apart(pool, s.r_m12, k + 1)
                pool.tensor_tensor(rw[:, :, 1], ebase[:, :], rw[:, :, 0], ALU.pow).then_inc(s.r_e, 1)
            phase_end(pool, "pool", ph)

        def me_pe(pe, k0, ph):
            base = k0 * E * NCH

            def up(e, sl, c, i, wait):
                if wait:
                    pe.wait_ge(s.e_act, (base + e * NCH + c) * 3 - 2 + i)
                for half in range(2):
                    m = pe.matmul(B[2 * i + half][:, :], we1[sl][:, (3 * half + i) * P:(3 * half + i + 1) * P],
                                  uT[:, bass.ts(c, CH)], start=True, stop=True)
                m.then_inc(s.e_up, 1)

            def down(e, sl, c):
                n = base + e * NCH + c
                pe.wait_ge(s.e_act, n * 3 + 3)
                pe.wait_ge(s.e_acc, n + 1)
                for j in range(CT):
                    for i in range(3):
                        m = pe.matmul(B[6][:, j * P:(j + 1) * P], act_b[:, i, j * P:(j + 1) * P], we2[sl][:, i, :],
                                      start=(i == 0), stop=(i == 2))
                m.then_inc(s.e_dn, 1)

            def first(e, sl):
                for i in range(3):
                    up(e, sl, 0, i, False)

            def rest(e, sl, c):
                up(e, sl, c, 0, True)
                down(e, sl, c - 1)
                up(e, sl, c, 1, True)
                up(e, sl, c, 2, True)

            with pe.Fori(0, E // 2) as ep:
                for sl in range(2):
                    e = ep * 2 + sl
                    pe.wait_ge((s.ld_e0, s.ld_e1)[sl], (ep + 1 + k0 * (E // 2)) * 32)
                    first(e, sl)
                    with pe.Fori(1, NCH) as c:
                        rest(e, sl, c)
                    down(e, sl, NCH - 1)
            phase_end(pe, "pe", ph)

        def me_act(act, k0, ph):
            act.preload_act_table(ACT.Gelu)
            base = k0 * E * NCH
            with act.Fori(0, E) as e:
                with act.Fori(0, NCH) as c:
                    n = base + e * NCH + c
                    for i in range(3):
                        wait_apart(act, s.e_up, n * 3 + i + 1)
                        act.activation(gl[:, i, :], B[2 * i + 1][:, :], ACT.Gelu, bias=vec[:, bass.ds(e * 6 + 3 + i, 1)])\
                            .then_inc(s.e_gelu, 1)
            phase_end(act, "act", ph)

        def me_dve(dve, k0, ph):
            base = k0 * E * NCH
            wflat = wts[:, :, :].rearrange("p t e -> p (t e)")

            def acts(e, n):
                for i in range(3):
                    dve.wait_ge(s.e_gelu, n * 3 + i + 1)
                    dve.scalar_tensor_tensor(act_b[:, i, :], B[2 * i][:, :], vec[:, bass.ds(e * 6 + i, 1)], gl[:, i, :],
                                             ALU.add, ALU.mult).then_inc(s.e_act, 1)

            def add(e, c):
                dve.wait_ge(s.e_dn, base + e * NCH + c + 1)
                for j in range(CT):
                    ut = U[:, bass.ds(c * CT + j, 1), :].rearrange("p o d -> p (o d)")
                    m = dve.scalar_tensor_tensor(ut, B[6][:, j * P:(j + 1) * P],
                                                 wflat[:, bass.ds((c * CT + j) * E + e, 1)], ut, ALU.mult, ALU.add)
                m.then_inc(s.e_acc, 1)

            if not k0:
                dve.sem_inc(s.e_acc, 1)
            with dve.Fori(0, E) as e:
                acts(e, base + e * NCH)
                with dve.Fori(1, NCH) as c:
                    add(e, c - 1)
                    acts(e, base + e * NCH + c)
                add(e, NCH - 1)
            phase_end(dve, "dve", ph)

        def me_sync(sp, k0, ph_before):
            base = k0 * E * NCH

            def load(ep, sl):
                ld = (s.ld_e0, s.ld_e1)[sl]
                e = ep * 2 + sl
                sp.dma_start(we1[sl][:, :], a["L1_ffn_We1"][bass.ds(e, 1), :, :].rearrange("o k n -> (o k) n"))\
                    .then_inc(ld, 16)
                sp.dma_start(we2[sl][:, :, :], a["L1_ffn_We2"][bass.ds(e, 1), :, :]
                             .rearrange("o (c k) n -> k (o c) n", k=P)).then_inc(ld, 16)

            sp.wait_ge(s.ph_pe, ph_before)
            for sl in range(2):
                load(0, sl)
            with sp.Fori(1, E // 2) as ep:
                for sl in range(2):
                    sp.wait_ge(s.e_dn, base + ep * 2 * NCH + (sl - 1) * NCH)
                    load(ep, sl)

        def la_pe(pe, ph):
            with pe.Fori(0, NCH) as c:
                pe.wait_ge(s.n_xn, c + 1)
                for k, w in ((0, nqkv[:, 0:D]), (1, nqkv[:, D:2 * D]), (2, ngate[:, :])):
                    pe.matmul(B[k][:, :], w, xn[:, :], start=True, stop=True).then_inc(s.n_proj, 1)
                for j in range(CT):
                    m = pe.matmul(B[3][:, j * P:(j + 1) * P], xn[:, j * P:(j + 1) * P], nqkv[:, 2 * D:3 * D],
                                  start=True, stop=True)
                m.then_inc(s.n_proj, 1)
                pe.wait_ge(s.n_feat, 2 * c + 2)
                for b in range(2):
                    q0 = b * SEQ
                    pe.matmul(B[4 + b][:, 0:SEQ], kf[:, q0:q0 + P], qf[:, q0:q0 + SEQ], start=True, stop=True)
                    pe.matmul(B[4 + b][:, SEQ:384], kf[:, q0 + P:q0 + SEQ], qf[:, q0 + P:q0 + SEQ],
                              start=True, stop=True).then_inc(s.n_att, 1)
                for b in range(2):
                    pe.wait_ge(s.n_am, 2 * c + b + 1)
                    if b == 0:
                        pe.wait_ge(s.n_v, c + 1)
                    w = D + 1
                    pe.matmul(B[6 + b][:, 0:w], am[b][:, 0:P], vA[:, 2 * b, :], start=True, stop=True)
                    pe.matmul(B[6 + b][:, w:2 * w], am[b][:, P:SEQ], vA[:, 2 * b, :], start=True, stop=False)
                    pe.matmul(B[6 + b][:, w:2 * w], am[b][:, SEQ:384], vA[:, 2 * b + 1, :], start=False, stop=True)\
                        .then_inc(s.n_num, 1)
                pe.wait_ge(s.n_o, c + 1)
                for j in range(CT):
                    m = pe.transpose(B[4][:, j * P:(j + 1) * P], osb[:, j, :], ident[:, :])
                m.then_inc(s.n_oT_ps, 1)
                pe.wait_ge(s.n_oT, c + 1)
                for j in range(CT):
                    m = pe.matmul(B[5][:, j * P:(j + 1) * P], noT[:, j * P:(j + 1) * P], nproj[:, :],
                                  start=True, stop=True)
                m.then_inc(s.n_yps, 1)
                pe.wait_ge(s.n_out, c + 2)
            phase_end(pe, "pe", ph)

        def la_act(act, ph):
            act.preload_act_table(ACT.Exp)
            with act.Fori(0, NCH) as c:
                wait_apart(act, s.n_out, c + 1)
                act.activation(xn[:, :], uT[:, bass.ts(c, CH)], ACT.Identity, bias=vec[:, V_LNB:V_LNB + 1],
                               scale=vec[:, V_LNG:V_LNG + 1]).then_inc(s.n_xn, 1)
                wait_apart(act, s.n_g, c + 1)
                act.activation(z2[:, :], z2[:, :], ACT.Exp, scale=-1.0).then_inc(s.n_gexp, 1)
                for k in range(2):
                    wait_apart(act, s.n_min, 2 * c + k + 1)
                    z = (z0, z1)[k]
                    act.activation(z[:, :], z[:, :], ACT.Exp).then_inc(s.n_exp, 1)
                wait_apart(act, s.n_oT_ps, c + 1)
                act.activation(noT[:, :], B[4][:, :], ACT.Copy).then_inc(s.n_oT, 1)
            phase_end(act, "act", ph)

        def la_dve(dve, ph):
            bq, bk = (vec[:, V_LQKVB + k:V_LQKVB + k + 1] for k in range(2))
            dve.sem_inc(s.n_out, 1)
            with dve.Fori(0, NCH) as c:
                dve.wait_ge(s.n_proj, 4 * c + 1)
                dve.tensor_scalar(z0[:, :], B[0][:, :], bq, 0.0, ALU.add, ALU.min).then_inc(s.n_min, 1)
                dve.tensor_scalar(qf[:, :], B[0][:, :], bq, 0.0, ALU.add, ALU.max).then_inc(s.n_gd, 1)
                dve.wait_ge(s.n_proj, 4 * c + 3)
                dve.tensor_scalar(z2[:, :], B[2][:, :], vec[:, V_LGATE:V_LGATE + 1], -80.0, ALU.add, ALU.max)\
                    .then_inc(s.n_g, 1)
                dve.wait_ge(s.n_gexp, c + 1)
                dve.tensor_scalar(z2[:, :], z2[:, :], 1.0, None, ALU.add).then_inc(s.n_gd, 1)
                dve.wait_ge(s.n_gd, 4 * c + 2)
                dve.reciprocal(z2[:, :], z2[:, :]).then_inc(s.n_gd, 1)
                dve.wait_ge(s.n_gd, 4 * c + 3)
                dve.scalar_tensor_tensor(kf[:, :], B[1][:, :], bk, z2[:, :], ALU.add, ALU.mult).then_inc(s.n_gd, 1)
                dve.wait_ge(s.n_gd, 4 * c + 4)
                dve.tensor_scalar(z1[:, :], kf[:, :], 0.0, None, ALU.min).then_inc(s.n_min, 1)
                dve.wait_ge(s.n_exp, 2 * c + 1)
                dve.tensor_tensor(qf[:, :], qf[:, :], z0[:, :], ALU.add).then_inc(s.n_feat, 1)
                dve.wait_ge(s.n_exp, 2 * c + 2)
                dve.scalar_tensor_tensor(kf[:, :], kf[:, :], 0.0, z1[:, :], ALU.max, ALU.add).then_inc(s.n_feat, 1)
                dve.wait_ge(s.n_proj, 4 * c + 4)
                dve.tensor_tensor(vA[:, :, 0:D], B[3][:, :].rearrange("p (t d) -> p t d", t=CT),
                                  bc(lbv_row[:, :].unsqueeze(1), [P, CT, D]), ALU.add).then_inc(s.n_v, 1)
                for b in range(2):
                    dve.wait_ge(s.n_att, 2 * c + b + 1)
                    dve.tensor_tensor(am[b][:, :], B[4 + b][:, 0:384], causal[:, :], ALU.mult).then_inc(s.n_am, 1)
                for b in range(2):
                    dve.wait_ge(s.n_num, 2 * c + b + 1)
                    dve.tensor_scalar(ndr[:, 0, 2 * b:2 * b + 2],
                                      B[6 + b][:, 0:2 * (D + 1)].rearrange("p (t d) -> p t d", t=2)[:, :, D],
                                      DEN_EPS, None, ALU.add).then_inc(s.n_den, 1)
                dve.wait_ge(s.n_den, 2 * c + 2)
                dve.reciprocal(ndr[:, 1, :], ndr[:, 0, :]).then_inc(s.n_rec, 1)
                dve.wait_ge(s.n_rec, c + 1)
                for j in range(CT):
                    o0 = (j % 2) * (D + 1)
                    m = dve.tensor_scalar(osb[:, j, :], B[6 + j // 2][:, o0:o0 + D], ndr[:, 1, j:j + 1], None, ALU.mult)
                m.then_inc(s.n_o, 1)
                dve.wait_ge(s.n_yps, c + 1)
                dve.tensor_tensor(U[:, bass.ts(c, CT), :], B[5][:, :].rearrange("p (t d) -> p t d", t=CT),
                                  bc(lbp_row[:, :].unsqueeze(1), [P, CT, D]), ALU.add).then_inc(s.n_out, 1)
            phase_end(dve, "dve", ph)

        def fin_dve(dve, coef):
            with dve.Fori(0, NCH) as c:
                xc = X[:, bass.ts(c, CT), :]
                dve.scalar_tensor_tensor(xc, U[:, bass.ts(c, CT), :], coef, xc, ALU.mult, ALU.add).then_inc(s.fin_x, 1)

        def fin_sync(sp):
            per_seq = out.rearrange("b (t p) d -> p (b t) d", p=P)
            for c in range(NCH):
                sp.wait_ge(s.fin_x, c + 1)
                sp.dma_start(per_seq[:, c * CT:(c + 1) * CT, :], X[:, c * CT:(c + 1) * CT, :]).then_inc(s.out_done, 16)
            sp.wait_ge(s.out_done, 16 * NCH)

        def nothing(eng, me, ph):
            phase_end(eng, me, ph)

        COEF = [0.0, 0.5, 1.0, 0.5, 0.5, 1.0, 0.5]

        @block.sync
        def _(sp):
            setup_sync(sp)
            if stages >= 1:
                ffn_sync(sp, 0, 2)
            if stages >= 3:
                ffn_sync(sp, 1, 10)
            if stages >= 4:
                me_sync(sp, 0, 16)
            if stages >= 6:
                me_sync(sp, 1, 21)
            fin_sync(sp)

        @block.tensor
        def _(pe):
            setup_pe(pe)
            tr_pe(pe, 0, 2)
            if stages >= 1:
                ffn(pe, "pe", 0, 2)
            if stages >= 2:
                tr_pe(pe, 1, 7)
                ap_pe(pe, 8)
                aa_pe(pe, 9)
            if stages >= 3:
                tr_pe(pe, 2, 10)
                ffn(pe, "pe", 1, 10)
            if stages >= 4:
                tr_pe(pe, 3, 15)
                mr_pe(pe, 0, 16)
                me_pe(pe, 0, 17)
            if stages >= 5:
                tr_pe(pe, 4, 18)
                la_pe(pe, 19)
            if stages >= 6:
                tr_pe(pe, 5, 20)
                mr_pe(pe, 1, 21)
                me_pe(pe, 1, 22)

        @block.scalar
        def _(act):
            setup_act(act)
            tr_act(act, 0, 2)
            if stages >= 1:
                ffn(act, "act", 0, 2)
            if stages >= 2:
                tr_act(act, 1, 7)
                ap_act(act, 8)
                aa_act(act, 9)
            if stages >= 3:
                tr_act(act, 2, 10)
                ffn(act, "act", 1, 10)
            if stages >= 4:
                tr_act(act, 3, 15)
                mr_act(act, 0, 16)
                me_act(act, 0, 17)
            if stages >= 5:
                tr_act(act, 4, 18)
                la_act(act, 19)
            if stages >= 6:
                tr_act(act, 5, 20)
                mr_act(act, 1, 21)
                me_act(act, 1, 22)

        @block.vector
        def _(dve):
            setup_dve(dve)
            tr_dve(dve, 0, 0.0, 2)
            if stages >= 1:
                ffn(dve, "dve", 0, 2)
            if stages >= 2:
                tr_dve(dve, 1, COEF[1], 7)
                ap_dve(dve, 8)
                aa_dve(dve, 9)
            if stages >= 3:
                tr_dve(dve, 2, COEF[2], 10)
                ffn(dve, "dve", 1, 10)
            if stages >= 4:
                tr_dve(dve, 3, COEF[3], 15)
                mr_dve(dve, 0, 16)
                me_dve(dve, 0, 17)
            if stages >= 5:
                tr_dve(dve, 4, COEF[4], 18)
                la_dve(dve, 19)
            if stages >= 6:
                tr_dve(dve, 5, COEF[5], 20)
                mr_dve(dve, 1, 21)
                me_dve(dve, 1, 22)
            fin_dve(dve, COEF[min(stages, 6)])

        @block.gpsimd
        def _(pool):
            setup_pool(pool)
            tr_pool(pool, 0, 2)
            if stages >= 1:
                ffn(pool, "pool", 0, 2)
            if stages >= 2:
                tr_pool(pool, 1, 7)
                vm_zeros(pool)
                nothing(pool, "pool", 8)
                aa_pool(pool, 9)
            if stages >= 3:
                tr_pool(pool, 2, 10, kT_zeros)
                ffn(pool, "pool", 1, 10)
            if stages >= 4:
                tr_pool(pool, 3, 15)
                mr_pool(pool, 0, 16)
                nothing(pool, "pool", 17)
            if stages >= 5:
                tr_pool(pool, 4, 18, vA_ones, twice=True)
                nothing(pool, "pool", 19)
            if stages >= 6:
                tr_pool(pool, 5, 20)
                mr_pool(pool, 1, 21)
                nothing(pool, "pool", 22)


_INS = ["L0_attn_x", "L0_attn_qkv_w", "L0_attn_qkv_b", "L0_attn_out_w", "L0_attn_out_b", "L0_attn_decay_alpha",
        "L0_ffn_wqkv", "L0_ffn_q_scale", "L0_ffn_k_scale", "L0_ffn_wo", "L0_ffn_ln_g", "L0_ffn_ln_b", "L0_ffn_w1",
        "L0_ffn_b1", "L0_ffn_w2", "L0_ffn_b2", "L1_attn_w_qkv", "L1_attn_b_qkv", "L1_attn_w_gate", "L1_attn_b_gate",
        "L1_attn_w_proj", "L1_attn_b_proj", "L1_attn_ln_g", "L1_attn_ln_b", "L1_ffn_Ws1", "L1_ffn_bs1", "L1_ffn_Ws2",
        "L1_ffn_bs2", "L1_ffn_We1", "L1_ffn_be1", "L1_ffn_We2", "L1_ffn_be2", "L1_ffn_Wr", "L1_ffn_br"]


def kernel(**inputs):
    import concourse.bacc as bacc
    from concourse.bass_utils import run_bass_kernel_spmd

    nc = bacc.Bacc("TRN2", target_bir_lowering=False, num_devices=1)
    arrays, aps = {}, {}
    for name in _INS:
        arrays[f"in_{name}"] = np.ascontiguousarray(inputs[name])
    for name, value in constants().items():
        arrays[f"in_{name}"] = np.ascontiguousarray(value.reshape(value.shape))
    for name, value in arrays.items():
        aps[name[3:]] = nc.dram_tensor(name, value.shape, mybir.dt.from_np(value.dtype), kind="ExternalInput").ap()
    out = nc.dram_tensor("out_0", (NBATCH, SEQ, D), F32, kind="ExternalOutput").ap()
    build(nc, aps, out)
    r = run_bass_kernel_spmd(nc, [arrays], core_ids=[0])
    return r.results[0]["out_0"]
```

```python
from collections import namedtuple
from contextlib import ExitStack

import concourse.bass as bass
import numpy as np
from concourse import mybir

F32 = mybir.dt.float32
U32 = mybir.dt.uint32
ALU = mybir.AluOpType
ACT = mybir.ActivationFunctionType
AX_X = mybir.AxisListType.X

P = 128
D = 128
NBATCH, SEQ = 8, 256
NT = NBATCH * SEQ // P
CH = 512
NCH = NT * P // CH
CT = CH // P
DEPTH, LH, LD, WIN = 2, 8, 64, 64
INNER = LH * LD
HID = int(D * 4 * 2 / 3)
HCH = [(0, 128), (128, 128), (256, HID - 256)]
QK_SCALE = 8.0
AH, AD = 16, 8
E, HS, HR, TAU = 12, 2 * D, 3 * D, 1.5
NEG = -1e25
LN_EPS, DEN_EPS = 1e-5, 1e-6
ARENA = 25002
NXT = (2 * NT * P) // P + E
NXG = NXT // 4

V_BE1, V_BS1, V_B1, V_LG, V_LB, V_QKVB, V_LQKVB, V_LGATE, V_LNG, V_LNB, V_N = (
    0, 72, 76, 88, 90, 92, 95, 98, 99, 100, 101)

SEMS = """
ld_first ld_vec ld_rows ld_late ld_w1 vec_zero vec_ps vec_ready wt_ps ph_pe ph_act ph_dve ph_pool x_new
stats_raw stats_ready rs_var rs_ready ln_done ln_ps hT_ready q_ps k_ps v_ps sqq_done sqk_done rq_ab rk_ab
qr_ready kadd_ready ssq_raw ssk_raw ss_ready rn_ready rn_self kr_ready qT_ps qT_ready kT_ps kT_ready v_ready
sim_ready mx_ready smax_ready exp_done rden_ready probs_ready pT_ps pT_ready pv_done o_ready y_ps x1_done h_ps
m_stats m_raw m_var m_rs hn_ready hnT_ps hT2_ready up_ps gelu_done act_ready dn_ps x1b_ready x2_ready xT_ps
xT_done x2_copied ustg_ready aq_ps av_ps aq_ready av_ready a_qm a_sim a_mx a_max a_exp a_rd a_prob a_Tps
a_Tready a_pv a_o a_yps a_out vm_ready alpha_ready r_lg r_self r_m12 r_e r_both r_cum r_pos r_te r_wst r_wps
r_wT s_up s_gelu s_act s_dn s_tmp xn_zero x_filled ld_ew scattered ld_x0 ld_x1 st_y0 st_y1 x_ps x_T x_up_g
x_up_a x_gb x_ab x_gl x_act x_Tps x_actT x_dn x_y gat0 gat1 gat2 gat3 x_sum n_xn n_proj n_min n_exp n_feat
n_gexp n_g n_gd n_v n_att n_am n_num n_den n_rec n_o n_oT_ps n_oT n_yps n_out out_done fin_x vm_zero rs_self
passed
""".split()

Semaphores = namedtuple("Semaphores", SEMS)


class Step:

    def __init__(self, q, Q=None):
        self.Q, self.inner = Q, Q is None
        self.opens = q % 2 == 0 and self.has(4)

    def has(self, d):
        return self.inner or 0 <= self.Q + d < NT

    def second(self, d):
        return self.inner or self.Q + d >= 1

    def after(self, n, u):
        return self.inner or 4 * self.Q + u >= n


def rotary_tables():
    f = np.float32
    half = np.arange(0, LD, 2, dtype=f)
    inv = f(1.0) / np.power(f(10000.0), half / f(LD)).astype(f)
    t = np.arange(SEQ, dtype=f)
    fr = (t[:, None] * inv[None, :]).astype(f)
    fr = np.concatenate([fr, fr], -1)
    base = ((half + f(0.4 * LD)) / f(1.4 * LD)).astype(f)
    power = ((t - SEQ // 2) / f(WIN // 2)).astype(f)
    sc = np.power(base[None, :].astype(f), power[:, None]).astype(f)
    sc = np.concatenate([sc, sc], -1)
    sign = np.concatenate([-np.ones(LD // 2, f), np.ones(LD // 2, f)])
    cos, sin = np.cos(fr).astype(f), np.sin(fr).astype(f) * sign
    tabs = np.stack([cos * sc, sin * sc, cos / sc, sin / sc]).astype(f)
    return np.ascontiguousarray(tabs.reshape(4, 2, P, LD).transpose(2, 0, 1, 3))


def constants():
    i, j = np.arange(P)[:, None], np.arange(P)[None, :]
    f = np.float32
    j1 = np.arange(64, SEQ)[None, :]
    band0 = np.where((j <= i) & (i - j <= WIN), 0, NEG).astype(f)
    band1 = np.where((j1 <= i + P) & (i + P - j1 <= WIN), 0, NEG).astype(f)
    jj = np.arange(SEQ)[None, :]
    dist = np.stack([np.abs(jj - i), np.abs(jj - i - P)], 1).astype(f)
    tri = (i <= j).astype(f)
    return {
        "ident": np.eye(P, dtype=f),
        "shift": np.concatenate([(j == i + 1), (i == P - 1) & (j == 0)], 1).astype(f),
        "rot": rotary_tables(),
        "band": np.concatenate([band0, band0, band1, band1], 1),
        "dist": dist,
        "headmask": (i // AD == np.arange(AH)[None, :]).astype(f),
        "causal": np.concatenate([tri, np.ones((P, P), f), tri], 1),
        "strict": (i < j).astype(f),
        "iota": np.broadcast_to(np.concatenate([np.arange(E), np.arange(NXT), P * np.arange(NT)]).astype(f)[None, :],
                                (P, E + NXT + NT)).copy(),
    }


def build(nc, a, out, stages=6):
    with ExitStack() as ctx:
        def sb(name, shape, dt=F32):
            return ctx.enter_context(nc.sbuf_tensor(name, shape, dt))

        s = Semaphores(*[ctx.enter_context(nc.semaphore(n)) for n in SEMS])
        B = [ctx.enter_context(nc.psum_tensor(f"bank{n}", [P, 512], F32)) for n in range(8)]

        X = sb("X", [P, NT, D])
        U = sb("U", [P, NT, D])
        uT = sb("uT", [P, NT * P])
        ident = sb("ident_sb", [P, P])
        shift = sb("shift_sb", [P, 2, P])
        rot = sb("rot_sb", [P, 4, 2, LD])
        band = sb("band_sb", [P, 640])
        band_of = [band[:, 0:128], band[:, 256:448]]
        dist = sb("dist_sb", [P, 2, SEQ])
        headmask = sb("headmask_sb", [P, AH])
        causal = sb("causal_sb", [P, 384])
        iota = sb("iota_sb", [P, E + NXT + NT])
        vec_rows = sb("vec_rows", [P, P])
        vec = sb("vec", [P, V_N])
        mhalf = sb("mhalf", [P, NT])
        ebase = sb("ebase", [P, NT])
        qs_row = sb("qs_row", [P, DEPTH, 2, LD])
        ks_row = sb("ks_row", [P, DEPTH, 2, LD])
        b2_row = sb("b2_row", [P, DEPTH, D])
        bs2_row = sb("bs2_row", [P, D])
        ob_row = sb("ob_row", [P, D])
        bv_row = sb("bv_row", [P, D])
        lbv_row = sb("lbv_row", [P, D])
        lbp_row = sb("lbp_row", [P, D])
        alpha = sb("alpha", [P, AH])
        alpha_w = sb("alpha_w", [P, 3, AH])
        aw_rows = sb("aw_rows", [P, 4, D])
        awT = sb("awT", [P, 4, D])
        nqkv = sb("nqkv", [P, 3 * D])
        ngate = sb("ngate", [P, D])
        nproj = sb("nproj", [P, D])
        ws1 = sb("ws1", [P, 2 * HS])
        ws2 = sb("ws2", [P, 2, D])
        wr = sb("wr", [P, E])
        be2 = sb("be2", [E, D])
        wts = sb("wts", [P, NT, E])
        arena = sb("arena", [P, ARENA])

        def cut(start, *shape):
            n = int(np.prod(shape))
            assert start + n <= ARENA
            v = arena[:, start:start + n]
            names = "abcd"[:len(shape)]
            if len(shape) > 1:
                sizes = dict(zip(names[1:], shape[1:]))
                v = v.rearrange(f"p ({' '.join(names)}) -> p {' '.join(names)}", **sizes)
            return v

        wqkv = cut(18432, DEPTH, 3 * INNER)
        wo = cut(21504, DEPTH, 4, D)
        w1 = cut(22528, 2 * HID)
        w2 = cut(23210, DEPTH, 3, D)
        rtab = cut(23978, DEPTH, 4, 2, LD)
        st6 = sb("st6", [P, NT, 6])
        mv = sb("mv", [P, NT, 2])
        rs = sb("rs", [P, 5, NT])
        stg = sb("stg", [P, CT, D])
        stg_flat = stg[:, :, :].rearrange("p t d -> p (t d)")
        hT = [sb(f"hT{n}", [P, SEQ]) for n in range(2)]
        kT = [cut(n * 2048, 4, 2, SEQ) for n in range(2)]
        qT = [cut(4096 + n * 1024, 4, SEQ) for n in range(2)]
        vv = [cut(6144 + n * 1024, 2, INNER) for n in range(2)]
        rab = cut(8192, 4, INNER)
        sq = cut(10240, 2 * INNER)
        qr = cut(11264, INNER)
        kadd = cut(11776, INNER)
        kr = cut(12288, INNER)
        ss = sb("ss", [P, 2, 16])
        rn = sb("rn", [P, 4, 3, 8])
        rnp = sb("rnp", [P, 16])
        sm = [sb(f"sm{n}", [P, 2, SEQ]) for n in range(2)]
        mx = sb("mx", [P, 2, 2])
        nb = sb("nb", [P, 2, 2])
        den = sb("den", [P, 2, 2])
        rden = sb("rden", [P, 2, 2])
        pA = [sb(f"pA{n}", [P, 2, SEQ]) for n in range(2)]
        pB = [sb(f"pB{n}", [P, 2, SEQ]) for n in range(2)]
        pT = [sb(f"pT{n}", [P, 512]) for n in range(2)]
        oT = sb("oT", [P, 4, P])
        hn = sb("hn", [P, SEQ])
        hT2 = sb("hT2", [P, SEQ])
        gl = sb("gl", [P, 3, CH])
        act_b = sb("act_b", [P, 3, CH])
        x1b = sb("x1b", [P, SEQ])
        xs = sb("xs", [P, SEQ])
        mrs = sb("mrs", [P, 2, 2])
        dbias = cut(0, AH, 2, SEQ)
        VM_AT = 8192
        vm = cut(VM_AT, 2, AH, P)
        qTa = cut(12288, NT * P)
        kTa = cut(14336, NT * P)
        va = cut(16384, NT, D)
        qm = [sb(f"qm{n}", [P, SEQ]) for n in range(2)]
        oTa = sb("oTa", [P, SEQ])
        def flat(t):
            return t[:, :, :].rearrange("p a b -> p (a b)")

        def halves(t):
            return [t[:, n * NT * E:(n + 1) * NT * E].rearrange("p (t e) -> p t e", e=E) for n in range(2)]
        oh = halves(flat(pA[0]))
        both, lg = halves(flat(pA[1]))
        tot, pre0 = halves(flat(pB[0]))
        pre1, place = halves(flat(pB[1]))
        prod, wtmp = halves(pT[0])
        need = pT[1][:, 0:E * NT].rearrange("p (e t) -> p e t", e=E)
        top = sb("top", [P, NT, 8])
        idx = sb("idx", [P, NT, 8], U32)
        idf = sb("idf", [P, NT, 2])
        rw = sb("rw", [P, NT, 4])
        wc = sb("wc", [P, 2, NT])
        wst = sb("wst", [P, CT, E])
        wT = sb("wT", [E, CH])
        ntile = sb("ntile", [P, E])
        etile = sb("etile", [P, 2, E])
        ecmp = sb("ecmp", [P, NXT, E])
        tef = sb("tef", [P, 2, NXT])
        te = sb("te", [P, NXT], U32)
        posf = sb("posf", [P, 2, NT])
        pos = sb("pos", [P, 2, NT], U32)
        strict = sb("strict_sb", [P, P])
        ones = sb("ones", [P, P])
        br_row = sb("br_row", [P, E])
        xg = sm[0][:, :, :].rearrange("p a (b d) -> p (a b) d", d=P)
        yb = stg
        xT = [pT[0][:, n * P:(n + 1) * P] for n in range(2)]
        gl_flat, act_flat = flat(gl), flat(act_b)
        xgate = [gl_flat[:, n * HR:(n + 1) * HR] for n in range(2)]
        xgelu = [gl_flat[:, (2 + n) * HR:(3 + n) * HR] for n in range(2)]
        xa = [act_flat[:, n * HR:(n + 1) * HR] for n in range(2)]
        xact = [act_flat[:, (2 + n) * HR:(3 + n) * HR] for n in range(2)]
        xactT = [flat(pA[n])[:, 0:HR] for n in range(2)]
        we1 = cut(0, E * 2 * HR)
        we2 = cut(E * 2 * HR, E * HR)
        be1_row = cut(E * 3 * HR, E * 2 * HR)
        xn = sb("xn", [P, CH])
        qf, kf, z0, z1 = flat(pA[0]), flat(pA[1]), flat(pB[0]), flat(pB[1])
        z2, noT = pT[0][:, :], pT[1][:, :]
        osb = sm[0][:, :, :].rearrange("p a (b d) -> p (a b) d", d=P)
        vA = cut(E * 5 * HR, CT, D + 1)
        am = [flat(sm[1])[:, 0:384], cut(E * 5 * HR + 516, 384)]
        ndr = sb("ndr", [P, 2, CT])

        x_sorted = nc.dram_tensor("x_sorted", [NXT * P, D], F32, kind="Internal").ap()
        y_sorted = nc.dram_tensor("y_sorted", [NXT * P, D], F32, kind="Internal").ap()

        block = ctx.enter_context(nc.Block())
        engines = ("pe", "act", "dve", "pool")
        done = {"pe": s.ph_pe, "act": s.ph_act, "dve": s.ph_dve, "pool": s.ph_pool}

        def phase_end(eng, me, k):
            eng.drain().then_inc(done[me], 1)
            for other in engines:
                if other != me:
                    eng.wait_ge(done[other], k)
            eng.sem_inc(s.passed, 1)

        def wait_apart(eng, sem, count):
            eng.wait_ge(sem, count)
            eng.sem_inc(s.passed, 1)

        def bc(ap, shape):
            return ap.broadcast_to(shape)

        def heads(ap):
            return ap.rearrange("p (h d) -> p h d", h=LH)

        def flipped(ap):
            return ap.rearrange("p (h a d) -> p h a d", h=LH, a=2)[:, :, ::-1, :]

        N_FIRST, N_VEC, N_ROWS, N_LATE = 10, 21, 13, 15

        def setup_sync(sp):
            def row(ap, n):
                return ap.rearrange("(o n) -> o n", o=1).broadcast_to([P, n])
            first = [(X[:, :, :], a["L0_attn_x"].rearrange("b (t p) d -> p (b t) d", p=P)),
                     (ident[:, :], a["ident"]), (rot[:, :, :, :], a["rot"]), (band[:, :], a["band"]),
                     (wqkv[:, :, :], a["L0_ffn_wqkv"].rearrange("l k n -> k l n")),
                     (wo[:, :, :, :], a["L0_ffn_wo"].rearrange("l (c k) n -> k l c n", k=P)),
                     (shift[:, :, :], a["shift"].rearrange("p (a b) -> p a b", a=2)),
                     (w2[:, 0, 0:2, :], a["L0_ffn_w2"][0, 0:256, :].rearrange("(c k) n -> k c n", k=P)),
                     (w2[:, 1, 0:2, :], a["L0_ffn_w2"][1, 0:256, :].rearrange("(c k) n -> k c n", k=P)),
                     (w2[0:HCH[2][1], :, 2, :], a["L0_ffn_w2"][:, 256:HID, :].rearrange("l k n -> k l n"))]
            assert len(first) == N_FIRST
            for dst, src in first:
                sp.dma_start(dst, src).then_inc(s.ld_first, 16)
            sp.wait_ge(s.vec_zero, 1)
            b1 = a["L0_ffn_b1"]
            vec_loads = [(vec_rows[V_BE1:V_BE1 + 72, :], a["L1_ffn_be1"].rearrange("e (c k) -> (e c) k", k=P)),
                         (vec_rows[V_BS1:V_BS1 + 4, :], a["L1_ffn_bs1"].rearrange("(c k) -> c k", k=P)),
                         (vec_rows[V_LG:V_LG + 2, :], a["L0_ffn_ln_g"]), (vec_rows[V_LB:V_LB + 2, :], a["L0_ffn_ln_b"]),
                         (vec_rows[V_QKVB:V_QKVB + 3, :], a["L0_attn_qkv_b"].rearrange("(c k) -> c k", k=P)),
                         (vec_rows[V_LQKVB:V_LQKVB + 3, :], a["L1_attn_b_qkv"].rearrange("(c k) -> c k", k=P)),
                         (vec_rows[V_LGATE:V_LGATE + 1, :], a["L1_attn_b_gate"].rearrange("(c k) -> c k", k=P)),
                         (vec_rows[V_LNG:V_LNG + 1, :], a["L1_attn_ln_g"].rearrange("(c k) -> c k", k=P)),
                         (vec_rows[V_LNB:V_LNB + 1, :], a["L1_attn_ln_b"].rearrange("(c k) -> c k", k=P))]
            for l in range(DEPTH):
                for g in range(2):
                    for c, (h0, hn_) in enumerate(HCH):
                        r = V_B1 + l * 6 + g * 3 + c
                        vec_loads.append((vec_rows[r:r + 1, 0:hn_], b1[l:l + 1, g * HID + h0:g * HID + h0 + hn_]))
            assert len(vec_loads) == N_VEC
            for dst, src in vec_loads:
                sp.dma_start(dst, src).then_inc(s.ld_vec, 16)
            qs, ks = a["L0_ffn_q_scale"], a["L0_ffn_k_scale"]
            rows = []
            for t, src in ((qs_row, qs), (ks_row, ks)):
                v = src.rearrange("(o l) d -> o l d", o=1)
                rows.append((t[:, :, 0, :], v.broadcast_to([P, DEPTH, LD])))
                for h in range(2):
                    rows.append((t[:, :, 1, 32 * h:32 * h + 32],
                                 v[:, :, 32 - 32 * h:64 - 32 * h].broadcast_to([P, DEPTH, 32])))
            rows += [(b2_row[:, :, :], a["L0_ffn_b2"].rearrange("(o l) d -> o l d", o=1).broadcast_to([P, DEPTH, D])),
                     (bs2_row[:, :], row(a["L1_ffn_bs2"], D)), (ob_row[:, :], row(a["L0_attn_out_b"], D)),
                     (bv_row[:, :], row(a["L0_attn_qkv_b"][2 * D:3 * D], D)),
                     (lbv_row[:, :], row(a["L1_attn_b_qkv"][2 * D:3 * D], D)),
                     (lbp_row[:, :], row(a["L1_attn_b_proj"], D)),
                     (alpha[:, :], row(a["L0_attn_decay_alpha"], AH))]
            assert len(rows) == N_ROWS
            for dst, src in rows:
                sp.dma_start(dst, src).then_inc(s.ld_rows, 16)
            late = [(aw_rows[:, 0:3, :], a["L0_attn_qkv_w"].rearrange("(c p) k -> p c k", p=P)),
                    (aw_rows[:, 3, :], a["L0_attn_out_w"]), (dist[:, :, :], a["dist"]),
                    (headmask[:, :], a["headmask"]), (causal[:, :], a["causal"]), (iota[:, :], a["iota"]),
                    (nqkv[:, :], a["L1_attn_w_qkv"]), (ngate[:, :], a["L1_attn_w_gate"]),
                    (nproj[:, :], a["L1_attn_w_proj"]), (ws1[:, :], a["L1_ffn_Ws1"]),
                    (ws2[:, :, :], a["L1_ffn_Ws2"].rearrange("(c k) n -> k c n", k=P)),
                    (wr[:, :], a["L1_ffn_Wr"]), (br_row[:, :], row(a["L1_ffn_br"], E)), (strict[:, :], a["strict"]),
                    (be2[:, :], a["L1_ffn_be2"])]
            assert len(late) == N_LATE
            for dst, src in late:
                sp.dma_start(dst, src).then_inc(s.ld_late, 16)
            sp.wait_ge(s.xn_zero, 1)
            for g in range(NXG):
                sp.dma_start(x_sorted[4 * g * P:4 * (g + 1) * P, :].rearrange("(t p) d -> p t d", p=P),
                             xn[:, :].rearrange("p (t d) -> p t d", d=D)).then_inc(s.x_filled, 16)

        def setup_pool(pool):
            pool.memset(vec_rows[:, :], 0.0).then_inc(s.vec_zero, 1)
            zeros = [hT[n][:, :] for n in range(2)]
            for n in range(2):
                zeros += [kT[n][:, :, :, :], pB[n][:, :, :]]
            for z in zeros:
                pool.memset(z, 0.0)
            pool.memset(xn[:, :], 0.0).then_inc(s.xn_zero, 1)
            pool.memset(ones[:, :], 1.0)
            pool.memset(mhalf[:, :], -0.5)
            pool.memset(ebase[:, :], float(np.e))
            phase_end(pool, "pool", 1)

        def setup_pe(pe):
            pe.wait_ge(s.ld_first, 16 * N_FIRST)
            pe.wait_ge(s.ld_vec, 16 * N_VEC)
            pe.transpose(B[0][:, 0:P], vec_rows[:, :], ident[:, :]).then_inc(s.vec_ps, 1)
            pe.wait_ge(s.ld_late, 16 * N_LATE)
            for c in range(4):
                t = pe.transpose(B[1][:, c * P:(c + 1) * P], aw_rows[:, c, :], ident[:, :])
            t.then_inc(s.wt_ps, 1)
            phase_end(pe, "pe", 1)

        def setup_act(act):
            act.wait_ge(s.ld_rows, 16 * N_ROWS)
            act.wait_ge(s.alpha_ready, 1)
            act.activation(alpha_w[:, 1, :], alpha_w[:, 0, :], ACT.Exp).then_inc(s.alpha_ready, 1)
            act.wait_ge(s.alpha_ready, 2)
            act.activation(alpha_w[:, 2, :], alpha_w[:, 1, :], ACT.Ln, bias=1.0).then_inc(s.alpha_ready, 1)
            phase_end(act, "act", 1)

        def setup_dve(dve):
            dve.wait_ge(s.ld_first, 16 * N_FIRST)
            dve.wait_ge(s.ld_rows, 16 * N_ROWS)
            dve.scalar_tensor_tensor(alpha_w[:, 0, :], alpha[:, :], -1.0, alpha[:, :], ALU.mult, ALU.min)\
                .then_inc(s.alpha_ready, 1)
            for l in range(DEPTH):
                for kind in range(4):
                    row_ = (qs_row, ks_row)[kind // 2][:, l, kind % 2, :]
                    dve.tensor_tensor(rtab[:, l, kind, :, :], rot[:, kind, :, :],
                                      bc(row_.unsqueeze(1), [P, 2, LD]), ALU.mult)
            dve.wait_ge(s.vec_ps, 1)
            dve.tensor_copy(vec[:, :], B[0][:, 0:V_N]).then_inc(s.vec_ready, 1)
            dve.wait_ge(s.wt_ps, 1)
            dve.tensor_copy(awT[:, :, :].rearrange("p c d -> p (c d)"), B[1][:, :])
            dve.wait_ge(s.ld_late, 16 * N_LATE)
            dve.wait_ge(s.vec_ready, 1)
            dve.tensor_scalar(vec[:, V_QKVB:V_QKVB + 1], vec[:, V_QKVB:V_QKVB + 1], AD ** -0.5, None, ALU.mult)\
                .then_inc(s.vec_ready, 1)
            dve.wait_ge(s.alpha_ready, 3)
            dve.scalar_tensor_tensor(alpha[:, :], alpha[:, :], 0.0, alpha_w[:, 2, :], ALU.max, ALU.add)\
                .then_inc(s.alpha_ready, 1)
            phase_end(dve, "dve", 1)

        HALF = NT // 2

        def tr_dve(dve, n, coef, ph, added=False):
            adds = n and not added
            first_x = (n - 1 - n // 5) * NCH

            def x_chunk(c):
                ts = slice(c * CT, (c + 1) * CT)
                dve.scalar_tensor_tensor(X[:, ts, :], U[:, ts, :], coef, X[:, ts, :], ALU.mult, ALU.add)\
                    .then_inc(s.x_new, 1)

            if adds:
                x_chunk(0)
            for c in range(NCH):
                if added:
                    add_experts(dve, 0, c)
                    dve.wait_ge(s.x_sum, 2 * (c + 1) * CT)
                if adds:
                    if c + 1 < NCH:
                        x_chunk(c + 1)
                    dve.wait_ge(s.x_new, first_x + c + 1)
                for t in range(c * CT, (c + 1) * CT):
                    m = dve.bn_stats(st6[:, t, :], X[:, t, :])
                m.then_inc(s.stats_raw, 1)
                if c % 2:
                    dve.wait_ge(s.stats_raw, n * NCH + c + 1)
                    for t in range(c * CT - CT, (c + 1) * CT):
                        m = dve.bn_aggr(mv[:, t, :], st6[:, t, :])
                    m.then_inc(s.stats_ready, 1)
            for c in range(NCH):
                if c % 2 == 0:
                    dve.wait_ge(s.rs_ready, n * 2 + c // 2 + 1)
                    dve.wait_ge(s.stats_ready, n * 2 + c // 2 + 1)
                for t in range(c * CT, (c + 1) * CT):
                    m = dve.tensor_scalar(U[:, t, :], X[:, t, :], mv[:, t, 0:1], rs[:, 1, t:t + 1],
                                          ALU.subtract, ALU.mult)
                m.then_inc(s.ln_done, 1)
            phase_end(dve, "dve", ph)

        def tr_pe(pe, n, ph):
            for c in range(NCH):
                pe.wait_ge(s.ln_done, n * NCH + c + 1)
                for j in range(CT):
                    m = pe.transpose(B[c][:, j * P:(j + 1) * P], U[:, c * CT + j, :], ident[:, :])
                m.then_inc(s.ln_ps, 1)
            phase_end(pe, "pe", ph)

        def tr_act(act, n, ph):
            act.preload_act_table(ACT.Exp)
            for c in range(NCH):
                act.wait_ge(s.ln_ps, n * NCH + c + 1)
                act.activation(uT[:, c * CH:(c + 1) * CH], B[c][:, :], ACT.Copy)
            phase_end(act, "act", ph)

        def vm_zeros(pool):
            pool.memset(vm[:, :, :, :], 0.0).then_inc(s.vm_zero, 1)

        def kT_zeros(pool):
            for n in range(2):
                pool.memset(kT[n][:, :, :, :], 0.0)

        def vA_ones(pool):
            pool.memset(vA[:, :, D:D + 1], 1.0)

        def tr_pool(pool, n, ph, extra=None, twice=False):
            if extra:
                extra(pool)
            for h in range(2):
                def part(k):
                    return rs[:, k, h * HALF:(h + 1) * HALF]

                def then_own(m, k):
                    m.then_inc(s.rs_self, 1)
                    pool.wait_ge(s.rs_self, 5 * h + k)

                power = mhalf[:, 0:HALF]
                pool.wait_ge(s.stats_ready, 2 * n + h + 1)
                var = mv[:, h * HALF:(h + 1) * HALF, 1]
                pool.tensor_scalar(part(0), var, LN_EPS, 0.0, ALU.add, ALU.add).then_inc(s.rs_var, 1)
                pool.wait_ge(s.rs_var, 2 * n + h + 1)
                if not twice:
                    pool.tensor_tensor(part(1), part(0), power, ALU.pow).then_inc(s.rs_ready, 1)
                else:
                    then_own(pool.tensor_tensor(part(2), part(0), power, ALU.pow), 1)
                    then_own(pool.tensor_tensor(part(3), part(2), part(2), ALU.mult), 2)
                    then_own(pool.tensor_tensor(part(4), part(3), var, ALU.mult), 3)
                    then_own(pool.tensor_scalar(part(3), part(4), LN_EPS, 0.0, ALU.add, ALU.add), 4)
                    then_own(pool.tensor_tensor(part(4), part(3), power, ALU.pow), 5)
                    pool.tensor_tensor(part(1), part(2), part(4), ALU.mult).then_inc(s.rs_ready, 1)
            phase_end(pool, "pool", ph)

        BQ, BK, BV, BT, BS, BP, BO = B[0], B[1], B[2], B[3], (B[4], B[5]), B[6], B[7]

        def steps(eng, step):
            for q in range(4):
                step(-1, q, Step(q, q - 4))
            for q in range(4):
                step(0, q, Step(q, q))
            with eng.Fori(1, NT // 4 - 1) as i:
                for q in range(4):
                    step(i, q, Step(q))
            for q in range(4):
                step(NT // 4 - 1, q, Step(q, NT - 4 + q))
            for q in (0, 1):
                step(NT // 4, q, Step(q, NT + q))

        def geometry(q):
            t = q % 2
            return (q // 2) % 2, t, (P if t == 0 else 192), (0 if t == 0 else 64)

        def probs(q, par):
            return (pA if q % 2 == 0 else pB)[par]

        def lo_pe(pe, l, pb, ph):
            tb, qb, hb = pb * NT, pb * NT * 4, pb * NBATCH

            def sim(i, q, u, banks_used):
                c, t, nk, k0 = geometry(q % 4)
                Q = 4 * i + q
                if u == 0:
                    pe.wait_ge(s.kT_ready, tb + Q + 1)
                if banks_used:
                    pe.wait_ge(s.smax_ready, qb + 4 * Q + u - 1)
                pe.matmul(BS[u % 2][:, 0:2 * nk], qT[c][:, u, t * P:(t + 1) * P], kT[c][:, u, :, k0:k0 + nk],
                          start=True, stop=True).then_inc(s.sim_ready, 1)

            def turn(i, q, u, bank_used):
                c, t, nk, k0 = geometry(q)
                n = qb + 4 * (4 * i + q) + u
                pe.wait_ge(s.probs_ready, n + 1)
                if bank_used:
                    pe.wait_ge(s.pT_ready, n)
                pr = probs(q, u % 2)
                for j in range(1 + t):
                    for x in range(2):
                        m = pe.transpose(BP[:, (2 * j + x) * P:(2 * j + x + 1) * P], pr[:, x, j * P:(j + 1) * P],
                                         ident[:, :])
                m.then_inc(s.pT_ps, 1)

            def pv(i, q, u, bank_used):
                c, t, nk, k0 = geometry(q)
                n = qb + 4 * (4 * i + q) + u
                pe.wait_ge(s.pT_ready, n + 1)
                if u == 0 and bank_used:
                    pe.wait_ge(s.o_ready, tb + 4 * i + q)
                if u == 0:
                    pe.wait_ge(s.v_ready, tb + 4 * i + q + 1)
                for x in range(2):
                    h = 2 * u + x
                    for j in range(1 + t):
                        m = pe.matmul(BO[64 * x:64 * x + 64, u * P:(u + 1) * P], vv[c][:, j, h * LD:(h + 1) * LD],
                                      pT[u % 2][:, (2 * j + x) * P:(2 * j + x + 1) * P], start=(j == 0), stop=(j == t))
                m.then_inc(s.pv_done, 1)

            def hT_of(q):
                return hT[(q // 2) % 2][:, (q % 2) * P:(q % 2 + 1) * P]

            def step(i, q, f):
                Q = 4 * i + q
                for u in range(4):
                    if u < 3:
                        if f.has(0):
                            sim(i, q, u + 1, f.after(2, u + 1))
                    elif f.has(1):
                        sim(i, q + 1, 0, f.second(1))
                    if u > 0:
                        if f.has(0):
                            turn(i, q, u - 1, f.after(1, u - 1))
                    elif f.has(-1):
                        turn(i if q else i - 1, (q - 1) % 4, 3, True)
                    if u == 0 and f.has(1):
                        pe.wait_ge(s.qr_ready, tb + Q + 2)
                        if f.second(1):
                            pe.wait_ge(s.kT_ready, tb + Q + 1)
                        for w in range(4):
                            m = pe.transpose(BT[:, w * P:(w + 1) * P], qr[:, w * P:(w + 1) * P], ident[:, :])
                        m.then_inc(s.qT_ps, 1)
                    if u == 0 and f.has(-2):
                        pe.wait_ge(s.o_ready, tb + Q - 1)
                        if f.has(1):
                            pe.wait_ge(s.v_ready, tb + Q + 2)
                        else:
                            pe.wait_ge(s.x1_done, tb + Q - 2)
                        for w in range(4):
                            m = pe.matmul(BV[:, 0:D], oT[:, w, :], wo_l(l, w), start=(w == 0), stop=(w == 3))
                        m.then_inc(s.y_ps, 1)
                    if u == 1 and f.has(1):
                        pe.wait_ge(s.kr_ready, tb + Q + 2)
                        pe.wait_ge(s.qT_ready, tb + Q + 2)
                        for w in range(4):
                            m = pe.transpose(BT[:, w * P:(w + 1) * P], kr[:, w * P:(w + 1) * P], ident[:, :])
                        m.then_inc(s.kT_ps, 1)
                    if u == 2 and f.has(3):
                        pe.wait_ge(s.hT_ready, hb + 2 * i + (q + 3) // 2 + 1)
                        if f.second(3):
                            pe.wait_ge(s.rq_ab, tb + Q + 3)
                        pe.matmul(BQ[:, :], hT_of(q + 3), wqkv_l(l, 0), start=True, stop=True).then_inc(s.q_ps, 1)
                    if u == 3 and f.has(3):
                        if f.second(3):
                            pe.wait_ge(s.rk_ab, tb + Q + 3)
                        pe.matmul(BK[:, :], hT_of(q + 3), wqkv_l(l, 1), start=True, stop=True).then_inc(s.k_ps, 1)
                    if u == 3 and f.has(2):
                        if f.has(-2):
                            pe.wait_ge(s.x1_done, tb + Q - 1)
                        elif f.second(2):
                            pe.wait_ge(s.v_ready, tb + Q + 2)
                        pe.matmul(BV[:, :], hT_of(q + 2), wqkv_l(l, 2), start=True, stop=True).then_inc(s.v_ps, 1)
                    if u >= 2:
                        if f.has(0):
                            pv(i, q, u - 2, f.has(-1))
                    elif f.has(-1):
                        pv(i if q else i - 1, (q - 1) % 4, u + 2, True)

            steps(pe, step)
            phase_end(pe, "pe", ph)

        def wqkv_l(l, k):
            return wqkv[:, bass.ds(l, 1), k * INNER:(k + 1) * INNER].rearrange("p o n -> p (o n)")

        def wo_l(l, w):
            return wo[:, bass.ds(l, 1), w, :].rearrange("p o n -> p (o n)")

        def lo_dve(dve, l, pb, ph):
            tb, qb = pb * NT, pb * NT * 4
            hb = pb * NBATCH

            def table(kind, t):
                v = rtab[:, bass.ds(l, 1), kind, t, :]
                return v

            def step(i, q, f):
                c, t, nk, k0 = geometry(q)
                Q = 4 * i + q
                r = Q + 2
                tr_ = (q + 2) % 2
                for u in range(4):
                    par = u % 2
                    n = qb + 4 * Q + u
                    if f.has(0):
                        wait_apart(dve, s.sim_ready, n + 1)
                        for x in range(2):
                            m = dve.tensor_tensor_reduce(sm[par][:, x, 0:nk], BS[par][:, x * nk:(x + 1) * nk], band_of[t],
                                                         1.0, -3e38, ALU.add, ALU.max, mx[:, par, x:x + 1])
                        m.then_inc(s.mx_ready, 1)
                        dve.wait_ge(s.mx_ready, n + 1)
                        dve.tensor_tensor(nb[:, par, :], mx[:, par, :], rn[:, q, 2, 2 * u:2 * u + 2], ALU.mult)\
                            .then_inc(s.smax_ready, 1)
                    back = (q, u - 1) if u else ((q - 1) % 4, 3)
                    if f.has(0 if u else -1):
                        bp, nkb, k0b = back[1] % 2, geometry(back[0])[2], geometry(back[0])[3]
                        dve.wait_ge(s.exp_done, n)
                        dve.reciprocal(rden[:, bp, :], den[:, bp, :]).then_inc(s.rden_ready, 1)
                        dve.wait_ge(s.rden_ready, n)
                        pr = probs(back[0], bp)
                        for x in range(2):
                            v = pr[:, x, k0b:k0b + nkb]
                            m = dve.tensor_scalar(v, v, rden[:, bp, x:x + 1], None, ALU.mult)
                        m.then_inc(s.probs_ready, 1)
                    if u == 3 and f.has(3):
                        dve.wait_ge(s.sqq_done, tb + Q + 4)
                        if f.second(3):
                            dve.wait_ge(s.ss_ready, tb + Q + 3)
                        dve.tensor_reduce(ss[:, 0, 0:8], heads(sq[:, 0:INNER]), AX_X, ALU.add).then_inc(s.ssq_raw, 1)
                    if u == 1 and f.has(2):
                        dve.wait_ge(s.sqk_done, tb + r + 1)
                        dve.tensor_reduce(ss[:, 0, 8:16], heads(sq[:, INNER:]), AX_X, ALU.add).then_inc(s.ssk_raw, 1)
                        dve.wait_ge(s.ssq_raw, tb + r + 1)
                        dve.wait_ge(s.ssk_raw, tb + r + 1)
                        if f.second(2):
                            dve.wait_ge(s.rn_ready, tb + r)
                        dve.tensor_scalar(ss[:, 1, :], ss[:, 0, :], 1e-24, None, ALU.max).then_inc(s.ss_ready, 1)
                    if f.has(2) and u < 3:
                        for kind in ((0, 1), (2,), (3,))[u]:
                            bank = BQ if kind < 2 else BK
                            if kind == 0 and f.second(2):
                                dve.wait_ge(s.qr_ready, tb + r)
                            if kind == 2 and f.second(2):
                                dve.wait_ge(s.kadd_ready, tb + r)
                            if kind % 2 == 0:
                                m = dve.tensor_tensor(heads(rab[:, kind, :]), heads(bank[:, :]),
                                                      bc(table(kind, tr_), [P, LH, LD]), ALU.mult)
                            else:
                                tb_ = table(kind, tr_).rearrange("p o (a d) -> p o a d", a=2)
                                m = dve.tensor_tensor(rab[:, kind, :].rearrange("p (h a d) -> p h a d", h=LH, a=2),
                                                      flipped(bank[:, :]), bc(tb_, [P, LH, 2, LD // 2]), ALU.mult)
                                m.then_inc(s.rq_ab if kind == 1 else s.rk_ab, 1)
                    if u == 1 and f.has(-2):
                        dve.wait_ge(s.y_ps, tb + Q - 1)
                        ut = U[:, bass.ds(Q - 2, 1), :].rearrange("p o d -> p (o d)")
                        dve.tensor_tensor(ut, BV[:, 0:D], ut, ALU.add).then_inc(s.x1_done, 1)
                    if u == 3 and f.opens:
                        h = hT[((q + 4) // 2) % 2]
                        b = 2 * i + (q + 4) // 2
                        src = uT[:, bass.ts(b, SEQ)]
                        if f.inner or Q >= 0:
                            dve.wait_ge(s.v_ps, tb + Q + 1)
                        dve.tensor_copy(h[0:64, :], src[0:64, :])
                        dve.tensor_copy(h[64:128, 1:SEQ], src[64:128, 0:SEQ - 1]).then_inc(s.hT_ready, 1)

            steps(dve, step)
            phase_end(dve, "dve", ph)

        def lo_act(act, l, pb, ph):
            tb, qb = pb * NT, pb * NT * 4
            act.preload_act_table(ACT.Exp)

            def pt_evac(q, u, n):
                act.wait_ge(s.pT_ps, n)
                cols = 256 * (1 + q % 2)
                act.activation(pT[u % 2][:, 0:cols], BP[:, 0:cols], ACT.Copy).then_inc(s.pT_ready, 1)

            def step(i, q, f):
                c, t, nk, k0 = geometry(q)
                Q = 4 * i + q
                for u in range(4):
                    par = u % 2
                    n = qb + 4 * Q + u
                    if u == 2 and f.has(-1):
                        act.wait_ge(s.pv_done, qb + 4 * Q)
                        if f.has(-2):
                            act.wait_ge(s.y_ps, tb + Q - 1)
                        act.activation(oT[:, :, :].rearrange("p w t -> p (w t)"), BO[:, :], ACT.Copy)\
                            .then_inc(s.o_ready, 1)
                    if f.has(0):
                        act.wait_ge(s.smax_ready, n + 1)
                        pr = probs(q, par)
                        for x in range(2):
                            m = act.activation(pr[:, x, k0:k0 + nk], sm[par][:, x, 0:nk], ACT.Exp,
                                               bias=nb[:, par, x:x + 1], scale=rn[:, q, 1, 2 * u + x:2 * u + x + 1],
                                               accum_out=den[:, par, x:x + 1])
                        m.then_inc(s.exp_done, 1)
                    bq, bu = (q, u - 1) if u else ((q - 1) % 4, 3)
                    if f.has(0 if u else -1):
                        if f.after(3, u):
                            act.wait_ge(s.pv_done, n - 2)
                        pt_evac(bq, bu, n)
                    c1, t1, _, _ = geometry((q + 1) % 4)
                    if u == 0 and f.has(1):
                        act.wait_ge(s.qT_ps, tb + Q + 2)
                        act.activation(qT[c1][:, :, t1 * P:(t1 + 1) * P], BT[:, :].rearrange("p (w t) -> p w t", w=4),
                                       ACT.Copy).then_inc(s.qT_ready, 1)
                    if u == 1 and f.has(1):
                        act.wait_ge(s.kT_ps, tb + Q + 2)
                        for x in range(2):
                            m = act.activation(kT[c1][64 * x:64 * x + 64, :, x, t1 * P:(t1 + 1) * P],
                                               BT[64 * x:64 * x + 64, :].rearrange("p (w t) -> p w t", w=4), ACT.Copy)
                        m.then_inc(s.kT_ready, 1)
                    if u == 3 and f.has(2):
                        cr, trr, _, _ = geometry((q + 2) % 4)
                        act.wait_ge(s.v_ps, tb + Q + 3)
                        act.activation(vv[cr][:, trr, :], BV[:, :], ACT.Copy).then_inc(s.v_ready, 1)
                    if u == 2 and f.has(3):
                        act.wait_ge(s.q_ps, tb + Q + 4)
                        if f.second(3):
                            act.wait_ge(s.ssq_raw, tb + Q + 3)
                        act.activation(sq[:, 0:INNER], BQ[:, :], ACT.Square).then_inc(s.sqq_done, 1)
                    if u == 3 and f.has(3):
                        act.wait_ge(s.k_ps, tb + Q + 4)
                        if f.second(3):
                            act.wait_ge(s.ssk_raw, tb + Q + 3)
                        act.activation(sq[:, INNER:], BK[:, :], ACT.Square).then_inc(s.sqk_done, 1)

            steps(act, step)
            phase_end(act, "act", ph)

        def lo_pool(pool, l, pb, ph):
            tb, qb = pb * NT, pb * NT * 4

            def step(i, q, f):
                Q = 4 * i + q
                r = Q + 2
                rq = (q + 2) % 4
                if f.has(2):
                    wait_apart(pool, s.rq_ab, tb + r + 1)
                    if f.second(2):
                        wait_apart(pool, s.qT_ps, tb + r)
                    pool.tensor_tensor(qr[:, :], rab[:, 0, :], rab[:, 1, :], ALU.add).then_inc(s.qr_ready, 1)
                    wait_apart(pool, s.ss_ready, tb + r + 1)
                    pool.tensor_tensor(rnp[:, :], ss[:, 1, :], mhalf[:, :], ALU.pow).then_inc(s.rn_self, 1)
                    wait_apart(pool, s.rn_self, tb + r + 1)
                    pool.tensor_scalar(rn[:, rq, 1, :], rnp[:, 0:8], QK_SCALE, 1.0, ALU.mult, ALU.mult)
                    pool.tensor_scalar(rn[:, rq, 2, :], rnp[:, 0:8], -QK_SCALE, 1.0, ALU.mult, ALU.mult)
                    pool.tensor_scalar(rn[:, rq, 0, :], rnp[:, 8:16], 1.0, 1.0, ALU.mult, ALU.mult)\
                        .then_inc(s.rn_ready, 1)
                    wait_apart(pool, s.rk_ab, tb + r + 1)
                    if f.second(2):
                        wait_apart(pool, s.kr_ready, tb + r)
                    pool.tensor_tensor(kadd[:, :], rab[:, 2, :], rab[:, 3, :], ALU.add).then_inc(s.kadd_ready, 1)
                    wait_apart(pool, s.kadd_ready, tb + r + 1)
                    if f.second(2):
                        wait_apart(pool, s.kT_ps, tb + r)
                    pool.tensor_tensor(heads(kr[:, :]), heads(kadd[:, :]),
                                       bc(rn[:, rq, 0, :].unsqueeze(2), [P, LH, LD]), ALU.mult)\
                        .then_inc(s.kr_ready, 1)

            steps(pool, step)
            phase_end(pool, "pool", ph)

        MH, MT, MG, MY, MX = B[0], B[1], (B[2], B[3], B[4]), B[5], B[6]

        def over_batches(eng, head, body, tail):
            head(0)
            body(0, True, True)
            with eng.Fori(1, NBATCH - 1) as b:
                body(b, False, True)
            body(NBATCH - 1, False, False)
            tail(NBATCH)

        def ff_pe(pe, l, pb, ph):
            hb = pb * NBATCH

            def shifted(b):
                if isinstance(b, int) and b == 0:
                    pass
                else:
                    pe.wait_ge(s.hn_ready, hb + b)
                h3 = MH[:, 0:SEQ].rearrange("p (t d) -> p t d", t=2)
                ub = U[:, bass.ts(b, 2), :]
                pe.matmul(h3[:, :, 0:64], ident[:, :], ub[:, :, 0:64], start=True, stop=True)
                pe.matmul(h3[:, :, 64:128], shift[:, 0, :], ub[:, :, 64:128], start=True, stop=False,
                          skip_group_check=True)
                pe.matmul(h3[:, 1, 64:128], shift[:, 1, :], ub[:, 0, 64:128], start=False, stop=True,
                          skip_group_check=True).then_inc(s.h_ps, 1)

            def turned(b):
                pe.wait_ge(s.hn_ready, hb + b + 1)
                for t in range(2):
                    m = pe.transpose(MT[:, t * P:(t + 1) * P], hn[:, t * P:(t + 1) * P], ident[:, :])
                m.then_inc(s.hnT_ps, 1)

            def x_turned(b):
                pe.wait_ge(s.x2_ready, hb + b)
                if not (isinstance(b, int) and b == 1):
                    pe.wait_ge(s.xT_done, hb + b - 1)
                for t in range(2):
                    m = pe.transpose(MX[:, t * P:(t + 1) * P], xs[:, t * P:(t + 1) * P], ident[:, :])
                m.then_inc(s.xT_ps, 1)

            def head(b):
                shifted(b)
                turned(b)

            def body(b, is_first, more):
                if more:
                    shifted(b + 1)
                pe.wait_ge(s.hT2_ready, hb + b + 1)
                for c, (h0, n) in enumerate(HCH):
                    if c == 0 and not is_first:
                        pe.wait_ge(s.act_ready, 3 * (hb + b))
                    for g in range(2):
                        m = pe.matmul(MG[c][0:n, g * SEQ:(g + 1) * SEQ], w1[:, g * HID + h0:g * HID + h0 + n], hT2[:, :],
                                      start=True, stop=True)
                    m.then_inc(s.up_ps, 1)
                if more:
                    turned(b + 1)
                if not is_first:
                    x_turned(b)
                pe.wait_ge(s.act_ready, 3 * (hb + b) + 3)
                for t in range(2):
                    for c, (h0, n) in enumerate(HCH):
                        m = pe.matmul(MY[:, t * P:(t + 1) * P], act_b[0:n, c, t * P:(t + 1) * P],
                                      w2[0:n, bass.ds(l, 1), c, :].rearrange("p o d -> p (o d)"),
                                      start=(c == 0), stop=(c == 2))
                m.then_inc(s.dn_ps, 1)

            pe.wait_ge(s.ld_w1, 16 * (pb + 1))
            over_batches(pe, head, body, x_turned)
            phase_end(pe, "pe", ph)

        def ff_dve(dve, l, pb, ph):
            hb = pb * NBATCH

            def stats(b):
                dve.wait_ge(s.h_ps, hb + b + 1)
                for t in range(2):
                    dve.bn_stats(st6[:, t, :], MH[:, t * P:(t + 1) * P]).then_inc(s.m_raw, 1)
                wait_apart(dve, s.m_raw, 2 * (hb + b) + 2)
                for t in range(2):
                    m = dve.bn_aggr(mv[:, t, :], st6[:, t, :])
                m.then_inc(s.m_stats, 1)

            def normed(b, is_first=False):
                dve.wait_ge(s.m_rs, hb + b + 1)
                if not is_first:
                    dve.wait_ge(s.hnT_ps, hb + b)
                for t in range(2):
                    m = dve.tensor_scalar(hn[:, t * P:(t + 1) * P], MH[:, t * P:(t + 1) * P], mv[:, t, 0:1],
                                          mrs[:, 1, t:t + 1], ALU.subtract, ALU.mult)
                m.then_inc(s.hn_ready, 1)

            def head(b):
                stats(b)
                normed(b, True)

            def body(b, is_first, more):
                if more:
                    stats(b + 1)
                for c, (h0, n) in enumerate(HCH):
                    dve.wait_ge(s.gelu_done, 3 * (hb + b) + c + 1)
                    if c == 0 and not is_first:
                        dve.wait_ge(s.dn_ps, hb + b)
                    row_a = V_B1 + c
                    ba = vec[0:n, bass.ds(l * 6 + row_a, 1)]
                    dve.scalar_tensor_tensor(act_b[0:n, c, 0:SEQ], MG[c][0:n, 0:SEQ], ba, gl[0:n, c, 0:SEQ],
                                             ALU.add, ALU.mult).then_inc(s.act_ready, 1)
                    if c == 0 and more:
                        normed(b + 1)
                dve.wait_ge(s.dn_ps, hb + b + 1)
                dve.wait_ge(s.x1b_ready, hb + b + 1)
                if not is_first:
                    dve.wait_ge(s.xT_ps, hb + b)
                    dve.wait_ge(s.x2_copied, hb + b)
                dve.tensor_tensor(xs[:, :], MY[:, 0:SEQ], x1b[:, :], ALU.add).then_inc(s.x2_ready, 1)

            over_batches(dve, head, body, lambda b: None)
            phase_end(dve, "dve", ph)

        def ff_act(act, l, pb, ph):
            hb = pb * NBATCH
            act.preload_act_table(ACT.Gelu)

            def head(b):
                wait_apart(act, s.hnT_ps, hb + b + 1)
                act.activation(hT2[:, :], MT[:, 0:SEQ], ACT.Identity, bias=vec[:, bass.ds(l + V_LB, 1)],
                               scale=vec[:, bass.ds(l + V_LG, 1)]).then_inc(s.hT2_ready, 1)

            def x_out(b):
                wait_apart(act, s.xT_ps, hb + b)
                act.activation(uT[:, bass.ts(b - 1, SEQ)], MX[:, 0:SEQ], ACT.Copy).then_inc(s.xT_done, 1)

            def body(b, is_first, more):
                for c, (h0, n) in enumerate(HCH):
                    wait_apart(act, s.up_ps, 3 * (hb + b) + c + 1)
                    act.activation(gl[0:n, c, 0:SEQ], MG[c][0:n, SEQ:2 * SEQ], ACT.Gelu,
                                   bias=vec[0:n, bass.ds(l * 6 + V_B1 + 3 + c, 1)]).then_inc(s.gelu_done, 1)
                if more:
                    head(b + 1)
                if not is_first:
                    x_out(b)

            over_batches(act, head, body, x_out)
            phase_end(act, "act", ph)

        def ff_pool(pool, l, pb, ph):
            hb = pb * NBATCH

            def head(b):
                wait_apart(pool, s.m_stats, hb + b + 1)
                pool.tensor_scalar(mrs[:, 0, :], mv[:, 0:2, 1], LN_EPS, 0.0, ALU.add, ALU.add).then_inc(s.m_var, 1)
                wait_apart(pool, s.m_var, hb + b + 1)
                pool.tensor_tensor(mrs[:, 1, :], mrs[:, 0, :], mhalf[:, 0:2], ALU.pow).then_inc(s.m_rs, 1)

            def body(b, is_first, more):
                if more:
                    head(b + 1)
                if not is_first:
                    wait_apart(pool, s.x2_ready, hb + b)
                pool.tensor_tensor(x1b[:, :].rearrange("p (t d) -> p t d", t=2), U[:, bass.ts(b, 2), :],
                                   bc(b2_row[:, bass.ds(l, 1), :], [P, 2, D]), ALU.add).then_inc(s.x1b_ready, 1)
                wait_apart(pool, s.x2_ready, hb + b + 1)
                wait_apart(pool, s.h_ps, hb + b + 1)
                pool.tensor_copy(U[:, bass.ts(b, 2), :], xs[:, :].rearrange("p (t d) -> p t d", t=2))\
                    .then_inc(s.x2_copied, 1)

            over_batches(pool, head, body, lambda b: None)
            phase_end(pool, "pool", ph)

        def ffn_sync(sp, site, ph0):
            with sp.Fori(0, DEPTH) as l:
                pb = l + site * DEPTH
                sp.wait_ge(s.ph_pe, ph0 + 2 * l)
                sp.dma_start(w1[:, :], a["L0_ffn_w1"][bass.ds(l, 1), :, :].rearrange("o k n -> (o k) n"))\
                    .then_inc(s.ld_w1, 16)

        def ffn(eng, name, site, ph0):
            parts = {"pe": (lo_pe, ff_pe), "act": (lo_act, ff_act), "dve": (lo_dve, ff_dve),
                     "pool": (lo_pool, ff_pool)}[name]
            with eng.Fori(0, DEPTH) as l:
                pb = l + site * DEPTH
                parts[0](eng, l, pb, ph0 + 1 + 2 * l)
                parts[1](eng, l, pb, ph0 + 2 + 2 * l)

        def ap_pe(pe, ph):
            with pe.Fori(0, NCH) as c:
                for k in range(2):
                    m = pe.matmul(B[k][:, :], awT[:, k, :], uT[:, bass.ts(c, CH)], start=True, stop=True)
                m.then_inc(s.aq_ps, 1)
                pe.wait_ge(s.ustg_ready, c + 1)
                for j in range(CT):
                    m = pe.matmul(B[2][:, j * P:(j + 1) * P], xn[:, j * P:(j + 1) * P], awT[:, 2, :],
                                  start=True, stop=True)
                m.then_inc(s.av_ps, 1)
                pe.wait_ge(s.aq_ready, c + 1)
                pe.wait_ge(s.av_ready, c + 1)
            phase_end(pe, "pe", ph)

        def ap_act(act, ph):
            act.preload_act_table(ACT.Exp)
            with act.Fori(0, NCH) as c:
                act.wait_ge(s.aq_ps, c + 1)
                act.activation(qTa[:, bass.ts(c, CH)], B[0][:, :], ACT.Identity, bias=vec[:, V_QKVB:V_QKVB + 1],
                               scale=AD ** -0.5)
                act.activation(kTa[:, bass.ts(c, CH)], B[1][:, :], ACT.Identity,
                               bias=vec[:, V_QKVB + 1:V_QKVB + 2]).then_inc(s.aq_ready, 1)
            phase_end(act, "act", ph)

        def ap_dve(dve, ph):
            dve.wait_ge(s.alpha_ready, 4)
            for h in range(AH):
                dve.tensor_scalar(dbias[:, h, :, :], dist[:, :, :], alpha[:, h:h + 1], -1.0, ALU.mult, ALU.mult)
            dve.wait_ge(s.x_filled, 16 * NXG)
            with dve.Fori(0, NCH) as c:
                dve.tensor_copy(xn[:, :], uT[:, bass.ts(c, CH)]).then_inc(s.ustg_ready, 1)
                dve.wait_ge(s.av_ps, c + 1)
                dve.tensor_tensor(va[:, bass.ts(c, CT), :], B[2][:, :].rearrange("p (t d) -> p t d", t=CT),
                                  bc(bv_row[:, :].unsqueeze(1), [P, CT, D]), ALU.add).then_inc(s.av_ready, 1)
            phase_end(dve, "dve", ph)

        AS, AP_, AO, AY = (B[4], B[5]), (B[6], B[3]), B[7], B[2]

        def over_sequences(eng, body, tail):
            body(0, True, False)
            with eng.Fori(1, NBATCH - 1) as b:
                body(b, False, False)
            body(NBATCH - 1, False, True)
            tail(NBATCH)

        def aa_pe(pe, ph):
            def sim(b, h):
                n = b * AH + h
                pe.wait_ge(s.a_qm, n + 1)
                if not (isinstance(n, int) and n < 2):
                    pe.wait_ge(s.a_max, n - 1)
                for t in range(2):
                    m = pe.matmul(AS[h % 2][:, t * SEQ:(t + 1) * SEQ], qm[h % 2][:, t * P:(t + 1) * P],
                                  kTa[:, bass.ts(b, SEQ)], start=True, stop=True)
                m.then_inc(s.a_sim, 1)

            def turn(b, h):
                n = b * AH + h
                pe.wait_ge(s.a_prob, n + 1)
                if not (isinstance(n, int) and n < 2):
                    pe.wait_ge(s.a_Tready, n - 1)
                for j in range(2):
                    for t in range(2):
                        m = pe.transpose(AP_[h % 2][:, (2 * j + t) * P:(2 * j + t + 1) * P],
                                         pA[h % 2][:, t, j * P:(j + 1) * P], ident[:, :])
                m.then_inc(s.a_Tps, 1)

            def pv(b, h):
                n = b * AH + h
                pe.wait_ge(s.a_Tready, n + 1)
                if h == 0:
                    pe.wait_ge(s.vm_ready, b + 1)
                    if not (isinstance(b, int) and b == 0):
                        pe.wait_ge(s.a_o, b)
                for j in range(2):
                    m = pe.matmul(AO[:, 0:SEQ], vm[:, j, h, :], pT[h % 2][:, j * SEQ:(j + 1) * SEQ],
                                  start=(h == 0 and j == 0), stop=(h == AH - 1 and j == 1))
                m.then_inc(s.a_pv, 1)

            def out_proj(b):
                pe.wait_ge(s.a_o, b)
                if not (isinstance(b, int) and b == 1):
                    pe.wait_ge(s.a_out, b - 1)
                for t in range(2):
                    m = pe.matmul(AY[:, t * P:(t + 1) * P], oTa[:, t * P:(t + 1) * P], awT[:, 3, :],
                                  start=True, stop=True)
                m.then_inc(s.a_yps, 1)

            def body(b, is_first, is_last):
                for h in range(AH):
                    if h + 1 < AH:
                        sim(b, h + 1)
                    elif not is_last:
                        sim(b + 1, 0)
                    if h >= 1:
                        turn(b, h - 1)
                    elif not is_first:
                        turn(b - 1, AH - 1)
                    if h >= 2:
                        pv(b, h - 2)
                    elif not is_first:
                        pv(b - 1, AH - 2 + h)
                    if h == 3 and not is_first:
                        out_proj(b)

            def tail(b):
                turn(b - 1, AH - 1)
                pv(b - 1, AH - 2)
                pv(b - 1, AH - 1)
                out_proj(b)

            sim(0, 0)
            over_sequences(pe, body, tail)
            phase_end(pe, "pe", ph)

        def aa_dve(dve, ph):
            def masked(b, h):
                dve.tensor_scalar(qm[h % 2][:, :], qTa[:, bass.ts(b, SEQ)], headmask[:, h:h + 1], None, ALU.mult)\
                    .then_inc(s.a_qm, 1)

            def scaled(n, par):
                dve.wait_ge(s.a_exp, n)
                dve.reciprocal(rden[:, par, :], den[:, par, :]).then_inc(s.a_rd, 1)
                dve.wait_ge(s.a_rd, n)
                for t in range(2):
                    m = dve.tensor_scalar(pA[par][:, t, :], pA[par][:, t, :], rden[:, par, t:t + 1], None, ALU.mult)
                m.then_inc(s.a_prob, 1)

            def result(b):
                dve.wait_ge(s.a_yps, b)
                dve.tensor_tensor(U[:, bass.ts(b - 1, 2), :], AY[:, 0:SEQ].rearrange("p (t d) -> p t d", t=2),
                                  bc(ob_row[:, :].unsqueeze(1), [P, 2, D]), ALU.add).then_inc(s.a_out, 1)

            def body(b, is_first, is_last):
                for h in range(AH):
                    n = b * AH + h
                    par = h % 2
                    wait_apart(dve, s.a_sim, n + 1)
                    for t in range(2):
                        m = dve.tensor_tensor_reduce(sm[par][:, t, :], AS[par][:, t * SEQ:(t + 1) * SEQ],
                                                     dbias[:, h, t, :], 1.0, -3e38, ALU.add, ALU.max,
                                                     mx[:, par, t:t + 1])
                    m.then_inc(s.a_mx, 1)
                    dve.wait_ge(s.a_mx, n + 1)
                    dve.tensor_scalar(nb[:, par, :], mx[:, par, :], -1.0, None, ALU.mult).then_inc(s.a_max, 1)
                    if h + 2 < AH:
                        masked(b, h + 2)
                    elif not is_last:
                        masked(b + 1, h + 2 - AH)
                    if not (is_first and h == 0):
                        scaled(n, 1 - par)
                    if h == 5 and not is_first:
                        result(b)

            def tail(b):
                scaled(AH * b, 1)
                result(b)

            masked(0, 0)
            masked(0, 1)
            over_sequences(dve, body, tail)
            phase_end(dve, "dve", ph)

        def aa_act(act, ph):
            act.preload_act_table(ACT.Exp)

            def evac(n, par, back_ok):
                act.wait_ge(s.a_Tps, n)
                if back_ok:
                    act.wait_ge(s.a_pv, n - 2)
                act.activation(pT[par][:, :], AP_[par][:, :], ACT.Copy).then_inc(s.a_Tready, 1)

            def outs(b):
                act.wait_ge(s.a_pv, AH * b)
                if not (isinstance(b, int) and b == 1):
                    act.wait_ge(s.a_yps, b - 1)
                act.activation(oTa[:, :], AO[:, 0:SEQ], ACT.Copy).then_inc(s.a_o, 1)

            def body(b, is_first, is_last):
                for h in range(AH):
                    n = b * AH + h
                    par = h % 2
                    act.wait_ge(s.a_max, n + 1)
                    for t in range(2):
                        m = act.activation(pA[par][:, t, :], sm[par][:, t, :], ACT.Exp, bias=nb[:, par, t:t + 1],
                                           accum_out=den[:, par, t:t + 1])
                    m.then_inc(s.a_exp, 1)
                    if not (is_first and h == 0):
                        evac(n, 1 - par, not (is_first and h < 3))
                    if h == 1 and not is_first:
                        outs(b)

            def tail(b):
                evac(AH * b, 1, True)
                outs(b)

            over_sequences(act, body, tail)
            phase_end(act, "act", ph)

        def aa_pool(pool, ph):
            pool.wait_ge(s.vm_zero, 1)

            def spread(b):
                for t in range(2):
                    blocks = bass.AP(tensor=arena, offset=VM_AT + t * AH * P, ap=[[ARENA, P], [P + AD, AH], [1, AD]])
                    m = pool.tensor_copy(blocks, va[:, bass.ds(b * 2 + t, 1), :]
                                         .rearrange("p o (h d) -> p (o h) d", h=AH))
                m.then_inc(s.vm_ready, 1)

            spread(0)
            with pool.Fori(1, NBATCH) as b:
                wait_apart(pool, s.a_pv, AH * b)
                spread(b)
            phase_end(pool, "pool", ph)

        def mr_pe(pe, k0, ph):
            for t in range(NT):
                m = pe.matmul(B[0][:, t * E:(t + 1) * E], uT[:, t * P:(t + 1) * P], wr[:, :], start=True, stop=True)
            m.then_inc(s.r_lg, 1)

            def up(c, g, wait):
                if wait:
                    pe.wait_ge(s.s_act, 2 * (k0 * NCH + c) + g - 1)
                for half in range(2):
                    m = pe.matmul(B[1 + 2 * g + half][:, :], ws1[:, (2 * half + g) * P:(2 * half + g + 1) * P],
                                  uT[:, bass.ts(c, CH)], start=True, stop=True)
                m.then_inc(s.s_up, 1)

            def down(c):
                k = c + k0 * NCH
                pe.wait_ge(s.r_wst, k + 1)
                for j in range(CT):
                    m = pe.transpose(B[6][0:E, j * P:(j + 1) * P], wst[:, j, :], ident[:, :])
                m.then_inc(s.r_wps, 1)
                pe.wait_ge(s.s_act, 2 * k + 2)
                pe.wait_ge(s.s_tmp, 2 * k + 1)
                for j in range(CT):
                    js = slice(j * P, (j + 1) * P)
                    pe.matmul(B[5][:, js], act_b[:, 0, js], ws2[:, 0, :], start=True, stop=False)
                    pe.matmul(B[5][:, js], act_b[:, 1, js], ws2[:, 1, :], start=False, stop=False)
                    if j == 0:
                        pe.wait_ge(s.r_wT, k + 1)
                    m = pe.matmul(B[5][:, js], wT[:, js], be2[:, :], start=False, stop=True)
                m.then_inc(s.s_dn, 1)

            for g in range(2):
                up(0, g, False)
            pe.wait_ge(s.r_both, k0 + 1)
            flat_both = both.rearrange("p t e -> p (t e)")
            pe.matmul(B[7][:, 0:NT * E], strict[:, :], flat_both, start=True, stop=True)
            pe.matmul(B[7][:, 256:256 + NT * E], ones[:, :], flat_both, start=True, stop=True).then_inc(s.r_cum, 1)
            with pe.Fori(1, NCH) as c:
                for g in range(2):
                    up(c, g, True)
                down(c - 1)
            down(NCH - 1)
            phase_end(pe, "pe", ph)

        def mr_act(act, k0, ph):
            act.preload_act_table(ACT.Gelu)
            with act.Fori(0, NCH) as c:
                k = c + k0 * NCH
                for g in range(2):
                    wait_apart(act, s.s_up, 2 * k + g + 1)
                    act.activation(gl[:, g, :], B[2 + 2 * g][:, :], ACT.Gelu, bias=vec[:, V_BS1 + 2 + g:V_BS1 + 3 + g])\
                        .then_inc(s.s_gelu, 1)
                wait_apart(act, s.r_wps, k + 1)
                act.activation(wT[:, :], B[6][0:E, :], ACT.Copy).then_inc(s.r_wT, 1)
            phase_end(act, "act", ph)

        R_STEPS = 35

        def mr_dve(dve, k0, coef, ph):
            taken = [k0 * R_STEPS]

            def done_(m):
                m.then_inc(s.r_self, 1)
                taken[0] += 1

            def own():
                dve.wait_ge(s.r_self, taken[0])

            def tiles_bc(v):
                return bc(v.unsqueeze(1), [P, NT, E])

            def experts_bc(v):
                return bc(v.unsqueeze(2), [P, NT, E])

            def prefix(bufs, n, view):
                src, others = bufs[0], [bufs[1], bufs[2]]
                step, m = 1, 0
                while step < n:
                    dst = others[m % 2]
                    own()
                    dve.tensor_tensor(view(dst, step, n), view(src, step, n), view(src, 0, n - step), ALU.add)
                    done_(dve.tensor_copy(view(dst, 0, step), view(src, 0, step)))
                    src, step, m = dst, 2 * step, m + 1
                return src

            dve.wait_ge(s.r_lg, k0 + 1)
            done_(dve.tensor_tensor(lg, B[0][:, 0:NT * E].rearrange("p (t e) -> p t e", e=E), tiles_bc(br_row[:, :]),
                                    ALU.add))
            own()
            done_(dve.tensor_scalar(lg, lg, 1.0 / TAU, None, ALU.mult))
            own()
            for t in range(NT):
                m = dve.max(top[:, t, :], lg[:, t, :])
            done_(m)
            own()
            dve.tensor_tensor(rw[:, :, 0], top[:, :, 1], top[:, :, 0], ALU.subtract).then_inc(s.r_m12, 1)
            for t in range(NT):
                m = dve.max_index(idx[:, t, :], top[:, t, :], lg[:, t, :])
            done_(m)
            own()
            done_(dve.tensor_copy(idf[:, :, :], idx[:, :, 0:2]))
            own()
            for n in range(2):
                m = dve.tensor_tensor(oh[n], tiles_bc(iota[:, 0:E]), experts_bc(idf[:, :, n]), ALU.is_equal)
            done_(m)
            own()
            dve.tensor_tensor(both, oh[0], oh[1], ALU.add).then_inc(s.r_both, 1)
            dve.wait_ge(s.r_e, k0 + 1)
            done_(dve.tensor_scalar(rw[:, :, 0], rw[:, :, 1], 1.0, None, ALU.add))
            own()
            done_(dve.reciprocal(rw[:, :, 2], rw[:, :, 0]))
            own()
            done_(dve.tensor_tensor(rw[:, :, 3], rw[:, :, 1], rw[:, :, 2], ALU.mult))
            own()
            dve.wait_ge(s.r_cum, k0 + 1)
            done_(dve.tensor_copy(tot, B[7][:, 256:256 + NT * E].rearrange("p (t e) -> p t e", e=E)))
            incl = prefix([tot, pre0, pre1], NT, lambda v, a_, b_: v[:, a_:b_, :])
            own()
            done_(dve.tensor_tensor(need, bc(incl[:, NT - 1, :].unsqueeze(2), [P, E, NT]),
                                    bc(iota[:, E + NXT:].unsqueeze(1), [P, E, NT]), ALU.is_gt))
            own()
            done_(dve.tensor_reduce(ntile[:, :], need, AX_X, ALU.add))
            ends = prefix([ntile[:, :], etile[:, 0, :], etile[:, 1, :]], E, lambda v, a_, b_: v[:, a_:b_])
            own()
            done_(dve.tensor_tensor(ecmp[:, :, :], bc(ends.unsqueeze(1), [P, NXT, E]),
                                    bc(iota[:, E:E + NXT].unsqueeze(2), [P, NXT, E]), ALU.is_le))
            done_(dve.tensor_tensor(place, incl, tot, ALU.subtract))
            own()
            done_(dve.tensor_tensor(place, place, B[7][:, 0:NT * E].rearrange("p (t e) -> p t e", e=E), ALU.add))
            done_(dve.tensor_tensor(ntile[:, :], ends, ntile[:, :], ALU.subtract))
            own()
            done_(dve.scalar_tensor_tensor(place, tiles_bc(ntile[:, :]), float(P), place, ALU.mult, ALU.add))
            for n in range(2):
                own()
                done_(dve.tensor_tensor(prod, oh[n], place, ALU.mult))
                own()
                done_(dve.tensor_reduce(posf[:, n, :], prod, AX_X, ALU.add))
            own()
            dve.tensor_copy(pos[:, :, :], posf[:, :, :]).then_inc(s.r_pos, 1)
            done_(dve.tensor_reduce(tef[:, 0, :], ecmp[:, :, :], AX_X, ALU.add))
            own()
            done_(dve.tensor_scalar(tef[:, 1, :], tef[:, 0, :], float(E - 1), None, ALU.min))
            own()
            dve.tensor_copy(te[:, :], tef[:, 1, :]).then_inc(s.r_te, 1)
            done_(dve.tensor_tensor(wtmp, oh[0], experts_bc(rw[:, :, 2]), ALU.mult))
            done_(dve.tensor_tensor(wts[:, :, :], oh[1], experts_bc(rw[:, :, 3]), ALU.mult))
            own()
            done_(dve.tensor_tensor(wts[:, :, :], wts[:, :, :], wtmp, ALU.add))
            for n in range(2):
                m = dve.tensor_scalar(wc[:, n, :], rw[:, :, 2 + n], coef, None, ALU.mult)
            done_(m)
            own()
            assert taken[0] == (k0 + 1) * R_STEPS, taken

            def acts(c):
                k = c + k0 * NCH
                for g in range(2):
                    dve.wait_ge(s.s_gelu, 2 * k + g + 1)
                    if not (isinstance(c, int) and c == 0 and k0 == 0) and g == 0:
                        dve.wait_ge(s.s_dn, k)
                    dve.scalar_tensor_tensor(act_b[:, g, :], B[1 + 2 * g][:, :], vec[:, V_BS1 + g:V_BS1 + g + 1],
                                             gl[:, g, :], ALU.add, ALU.mult).then_inc(s.s_act, 1)

            def weights(c):
                k = c + k0 * NCH
                if not (isinstance(c, int) and c == 0 and k0 == 0):
                    dve.wait_ge(s.r_wps, k)
                dve.tensor_copy(wst[:, :, :], wts[:, bass.ts(c, CT), :]).then_inc(s.r_wst, 1)

            def result(c):
                k = c + k0 * NCH
                dve.wait_ge(s.s_dn, k + 1)
                dve.wait_ge(s.s_tmp, 2 * k + 2)
                xc = X[:, bass.ts(c, CT), :]
                dve.tensor_tensor(stg[:, :, :], B[5][:, :].rearrange("p (t d) -> p t d", t=CT),
                                  bc(bs2_row[:, :].unsqueeze(1), [P, CT, D]), ALU.add).then_inc(s.s_tmp, 1)
                dve.wait_ge(s.s_tmp, 2 * k + 3)
                dve.scalar_tensor_tensor(xc, stg[:, :, :], coef, xc, ALU.mult, ALU.add).then_inc(s.s_tmp, 1)

            if not k0:
                dve.sem_inc(s.s_tmp, 2)
            weights(0)
            acts(0)
            with dve.Fori(1, NCH) as c:
                weights(c)
                acts(c)
                result(c - 1)
            result(NCH - 1)
            phase_end(dve, "dve", ph)

        def mr_pool(pool, k0, ph):
            pool.wait_ge(s.r_m12, k0 + 1)
            pool.tensor_tensor(rw[:, :, 1], ebase[:, :], rw[:, :, 0], ALU.pow).then_inc(s.r_e, 1)
            pool.wait_ge(s.r_pos, k0 + 1)
            if not k0:
                pool.wait_ge(s.x_filled, 16 * NXG)
            for t in range(NT):
                for n in range(2):
                    pool.indirect_dma_start(x_sorted[:, :], bass.IndirectOffsetOnAxis(ap=pos[:, n, t:t + 1], axis=0),
                                            U[:, t, :], None).then_inc(s.scattered, 16)
            phase_end(pool, "pool", ph)

        XIN, XUP, XTA, XY = B[0], ((B[1], B[2]), (B[3], B[4])), B[5], B[6]

        def over_tiles(eng, step):
            for n in (-2, -1):
                step(-1, n + 4, lambda d, n=n: 0 <= n + d < NXT)
            for q in range(4):
                step(0, q, lambda d, n=q: 0 <= n + d < NXT)
            with eng.Fori(1, NXG - 1) as i:
                for q in range(4):
                    step(i, q, lambda d: True)
            for q in range(4):
                step(NXG - 1, q, lambda d, n=NXT - 4 + q: 0 <= n + d < NXT)
            step(NXG, 0, lambda d: NXT + d < NXT)

        def me_pe(pe, k0, ph):
            base = k0 * NXT

            def expert(n):
                return pe.value_load(te[0:1, bass.ds(n, 1)], min_val=0, max_val=E - 1)

            def step(i, q, has):
                n = 4 * i + q
                if has(1):
                    e = expert(n + 1)
                    pe.wait_ge(s.x_T, base + n + 2)
                    if has(-1) or k0:
                        pe.wait_ge(s.x_ab, base + n)
                    for half, sem in ((1, s.x_up_g), (0, s.x_up_a)):
                        pe.matmul(XUP[(q + 1) % 2][half][:, 0:HR], xT[(q + 1) % 2],
                                  we1[:, bass.ds(e * (2 * HR) + half * HR, HR)], start=True, stop=True).then_inc(sem, 1)
                if has(2):
                    q2 = (q + 2) % 4
                    i2 = i + (q + 2) // 4
                    if q2 % 2 == 0:
                        pe.wait_ge((s.ld_x0, s.ld_x1)[q2 // 2], 16 * (NXG * k0 + i2 + 1))
                    pe.transpose(XIN[:, 0:P], xg[:, q2, :], ident[:, :]).then_inc(s.x_ps, 1)
                if has(-1):
                    e = expert(n - 1)
                    pe.wait_ge(s.x_actT, base + n)
                    if has(-2) or k0:
                        pe.wait_ge(s.x_y, base + n - 1)
                    for j in range(3):
                        m = pe.matmul(XY[:, 0:D], xactT[(q + 1) % 2][:, j * P:(j + 1) * P],
                                      we2[:, bass.ds(e * HR + j * D, D)], start=(j == 0), stop=(j == 2))
                    m.then_inc(s.x_dn, 1)
                if has(0):
                    pe.wait_ge(s.x_act, base + n + 1)
                    for j in range(3):
                        m = pe.transpose(XTA[:, j * P:(j + 1) * P], xact[q % 2][:, j * P:(j + 1) * P], ident[:, :])
                    m.then_inc(s.x_Tps, 1)

            pe.wait_ge(s.ld_ew, 16 * N_EW)
            pe.wait_ge(s.r_te, k0 + 1)
            over_tiles(pe, step)
            phase_end(pe, "pe", ph)

        def me_act(act, k0, ph):
            base = k0 * NXT
            act.preload_act_table(ACT.Gelu)

            def step(i, q, has):
                n = 4 * i + q
                if has(1):
                    act.wait_ge(s.x_gb, base + n + 2)
                    act.activation(xgelu[(q + 1) % 2], xgate[(q + 1) % 2], ACT.Gelu).then_inc(s.x_gl, 1)
                if has(2):
                    act.wait_ge(s.x_ps, base + n + 3)
                    if has(0):
                        act.wait_ge(s.x_up_a, base + n + 1)
                    act.activation(xT[q % 2], XIN[:, 0:P], ACT.Copy).then_inc(s.x_T, 1)
                if has(-1):
                    q1 = (q - 1) % 4
                    i1 = i if q else i - 1
                    act.wait_ge(s.x_dn, base + n)
                    if q1 % 2 == 0 and not (isinstance(i1, int) and i1 + k0 == 0):
                        act.wait_ge((s.st_y0, s.st_y1)[q1 // 2], 16 * (NXG * k0 + i1))
                    act.activation(yb[:, q1, :], XY[:, 0:D], ACT.Copy).then_inc(s.x_y, 1)
                if has(0):
                    act.wait_ge(s.x_Tps, base + n + 1)
                    if has(-2):
                        act.wait_ge(s.x_dn, base + n - 1)
                    act.activation(xactT[q % 2], XTA[:, 0:HR], ACT.Copy).then_inc(s.x_actT, 1)

            over_tiles(act, step)
            phase_end(act, "act", ph)

        def me_dve(dve, k0, ph):
            base = k0 * NXT

            def step(i, q, has):
                n = 4 * i + q
                par = (q + 1) % 2
                if has(1):
                    e = dve.value_load(te[0:1, bass.ds(n + 1, 1)], min_val=0, max_val=E - 1)
                    dve.wait_ge(s.x_up_g, base + n + 2)
                    dve.tensor_tensor(xgate[par], XUP[par][1][:, 0:HR], be1_row[:, bass.ds(e * (2 * HR) + HR, HR)],
                                      ALU.add).then_inc(s.x_gb, 1)
                    dve.wait_ge(s.x_up_a, base + n + 2)
                    dve.tensor_tensor(xa[par], XUP[par][0][:, 0:HR], be1_row[:, bass.ds(e * (2 * HR), HR)],
                                      ALU.add).then_inc(s.x_ab, 1)
                    dve.wait_ge(s.x_gl, base + n + 2)
                    dve.wait_ge(s.x_ab, base + n + 2)
                    if has(-1):
                        dve.wait_ge(s.x_Tps, base + n)
                    dve.tensor_tensor(xact[par], xa[par], xgelu[par], ALU.mult).then_inc(s.x_act, 1)

            over_tiles(dve, step)
            phase_end(dve, "dve", ph)

        def add_experts(dve, k0, c):
            dve.wait_ge((s.gat0, s.gat1, s.gat2, s.gat3)[c], 16 * 8 * (k0 + 1))
            for t in range(c * CT, (c + 1) * CT):
                for n in range(2):
                    if n:
                        dve.wait_ge(s.x_sum, 2 * (k0 * NT + t) + 1)
                    src = (U[:, t, :], uT[:, t * P:(t + 1) * P])[n]
                    dve.scalar_tensor_tensor(X[:, t, :], src, wc[:, n, t:t + 1], X[:, t, :], ALU.mult, ALU.add)\
                        .then_inc(s.x_sum, 1)

        def me_pool(pool, k0, ph):
            phase_end(pool, "pool", ph)
            pool.wait_ge(s.st_y0, 16 * NXG * (k0 + 1))
            pool.wait_ge(s.st_y1, 16 * NXG * (k0 + 1))
            for t in range(NT):
                for n in range(2):
                    dst = (U[:, t, :], uT[:, t * P:(t + 1) * P])[n]
                    pool.indirect_dma_start(dst, None, y_sorted[:, :],
                                            bass.IndirectOffsetOnAxis(ap=pos[:, n, t:t + 1], axis=0))\
                        .then_inc((s.gat0, s.gat1, s.gat2, s.gat3)[t // 4], 16)

        N_EW = 9

        def me_sync(sp, k0):
            base = k0 * NXT
            if not k0:
                for sem in (s.ph_pe, s.ph_act, s.ph_dve, s.ph_pool):
                    sp.wait_ge(sem, 14)
                for n in range(3):
                    e0, e1 = 4 * n, 4 * n + 4
                    sp.dma_start(we1[:, e0 * 768:e1 * 768].rearrange("k (e n) -> k e n", e=4),
                                 a["L1_ffn_We1"][e0:e1].rearrange("e k n -> k e n")).then_inc(s.ld_ew, 16)
                    sp.dma_start(we2[:, e0 * HR:e1 * HR].rearrange("k (c n) -> k c n", n=D),
                                 a["L1_ffn_We2"][e0:e1].rearrange("e (c k) n -> k (e c) n", k=P)).then_inc(s.ld_ew, 16)
                    sp.dma_start(be1_row[:, e0 * 2 * HR:e1 * 2 * HR],
                                 a["L1_ffn_be1"][e0:e1].rearrange("(o e) n -> o (e n)", o=1)
                                 .broadcast_to([P, 8 * HR])).then_inc(s.ld_ew, 16)

            def rows(t, i, h):
                return t[bass.ds((4 * i + 2 * h) * P, 2 * P), :].rearrange("(t p) d -> p t d", p=P)

            def load(i, h):
                sp.dma_start(xg[:, 2 * h:2 * h + 2, :], rows(x_sorted, i, h)).then_inc((s.ld_x0, s.ld_x1)[h], 16)

            def store(i, h):
                sp.wait_ge(s.x_y, base + 4 * i + 2 * h + 2)
                sp.dma_start(rows(y_sorted, i, h), yb[:, 2 * h:2 * h + 2, :]).then_inc((s.st_y0, s.st_y1)[h], 16)

            def turn(i, after_two):
                for h in range(2):
                    sp.wait_ge(s.x_ps, base + 4 * (i - 1) + 2 * h + 2)
                    load(i, h)
                    if h == 0 and after_two:
                        store(i - 2, 1)
                    if h == 1:
                        store(i - 1, 0)

            sp.wait_ge(s.scattered, 16 * 2 * NT * (k0 + 1))
            load(0, 0)
            load(0, 1)
            turn(1, False)
            with sp.Fori(2, NXG) as i:
                turn(i, True)
            store(NXG - 2, 1)
            store(NXG - 1, 0)
            store(NXG - 1, 1)

        def la_pe(pe, ph):
            with pe.Fori(0, NCH) as c:
                pe.wait_ge(s.n_xn, c + 1)
                for k, w in ((0, nqkv[:, 0:D]), (1, nqkv[:, D:2 * D]), (2, ngate[:, :])):
                    pe.matmul(B[k][:, :], w, xn[:, :], start=True, stop=True).then_inc(s.n_proj, 1)
                for j in range(CT):
                    m = pe.matmul(B[3][:, j * P:(j + 1) * P], xn[:, j * P:(j + 1) * P], nqkv[:, 2 * D:3 * D],
                                  start=True, stop=True)
                m.then_inc(s.n_proj, 1)
                pe.wait_ge(s.n_feat, 2 * c + 2)
                for b in range(2):
                    q0 = b * SEQ
                    pe.matmul(B[4 + b][:, 0:SEQ], kf[:, q0:q0 + P], qf[:, q0:q0 + SEQ], start=True, stop=True)
                    pe.matmul(B[4 + b][:, SEQ:384], kf[:, q0 + P:q0 + SEQ], qf[:, q0 + P:q0 + SEQ],
                              start=True, stop=True).then_inc(s.n_att, 1)
                for b in range(2):
                    pe.wait_ge(s.n_am, 2 * c + b + 1)
                    if b == 0:
                        pe.wait_ge(s.n_v, c + 1)
                    w = D + 1
                    pe.matmul(B[6 + b][:, 0:w], am[b][:, 0:P], vA[:, 2 * b, :], start=True, stop=True)
                    pe.matmul(B[6 + b][:, w:2 * w], am[b][:, P:SEQ], vA[:, 2 * b, :], start=True, stop=False)
                    pe.matmul(B[6 + b][:, w:2 * w], am[b][:, SEQ:384], vA[:, 2 * b + 1, :], start=False, stop=True)\
                        .then_inc(s.n_num, 1)
                pe.wait_ge(s.n_o, c + 1)
                for j in range(CT):
                    m = pe.transpose(B[4][:, j * P:(j + 1) * P], osb[:, j, :], ident[:, :])
                m.then_inc(s.n_oT_ps, 1)
                pe.wait_ge(s.n_oT, c + 1)
                for j in range(CT):
                    m = pe.matmul(B[5][:, j * P:(j + 1) * P], noT[:, j * P:(j + 1) * P], nproj[:, :],
                                  start=True, stop=True)
                m.then_inc(s.n_yps, 1)
                pe.wait_ge(s.n_out, c + 2)
            phase_end(pe, "pe", ph)

        def la_act(act, ph):
            act.preload_act_table(ACT.Exp)
            with act.Fori(0, NCH) as c:
                wait_apart(act, s.n_out, c + 1)
                act.activation(xn[:, :], uT[:, bass.ts(c, CH)], ACT.Identity, bias=vec[:, V_LNB:V_LNB + 1],
                               scale=vec[:, V_LNG:V_LNG + 1]).then_inc(s.n_xn, 1)
                wait_apart(act, s.n_g, c + 1)
                act.activation(z2[:, :], z2[:, :], ACT.Exp, scale=-1.0).then_inc(s.n_gexp, 1)
                for k in range(2):
                    wait_apart(act, s.n_min, 2 * c + k + 1)
                    z = (z0, z1)[k]
                    act.activation(z[:, :], z[:, :], ACT.Exp).then_inc(s.n_exp, 1)
                wait_apart(act, s.n_oT_ps, c + 1)
                act.activation(noT[:, :], B[4][:, :], ACT.Copy).then_inc(s.n_oT, 1)
            phase_end(act, "act", ph)

        def la_dve(dve, ph):
            bq, bk = (vec[:, V_LQKVB + k:V_LQKVB + k + 1] for k in range(2))
            dve.sem_inc(s.n_out, 1)
            with dve.Fori(0, NCH) as c:
                dve.wait_ge(s.n_proj, 4 * c + 1)
                dve.tensor_scalar(z0[:, :], B[0][:, :], bq, 0.0, ALU.add, ALU.min).then_inc(s.n_min, 1)
                dve.tensor_scalar(qf[:, :], B[0][:, :], bq, 0.0, ALU.add, ALU.max).then_inc(s.n_gd, 1)
                dve.wait_ge(s.n_proj, 4 * c + 3)
                dve.tensor_scalar(z2[:, :], B[2][:, :], vec[:, V_LGATE:V_LGATE + 1], -80.0, ALU.add, ALU.max)\
                    .then_inc(s.n_g, 1)
                dve.wait_ge(s.n_gexp, c + 1)
                dve.tensor_scalar(z2[:, :], z2[:, :], 1.0, None, ALU.add).then_inc(s.n_gd, 1)
                dve.wait_ge(s.n_gd, 4 * c + 2)
                dve.reciprocal(z2[:, :], z2[:, :]).then_inc(s.n_gd, 1)
                dve.wait_ge(s.n_gd, 4 * c + 3)
                dve.scalar_tensor_tensor(kf[:, :], B[1][:, :], bk, z2[:, :], ALU.add, ALU.mult).then_inc(s.n_gd, 1)
                dve.wait_ge(s.n_gd, 4 * c + 4)
                dve.tensor_scalar(z1[:, :], kf[:, :], 0.0, None, ALU.min).then_inc(s.n_min, 1)
                dve.wait_ge(s.n_exp, 2 * c + 1)
                dve.tensor_tensor(qf[:, :], qf[:, :], z0[:, :], ALU.add).then_inc(s.n_feat, 1)
                dve.wait_ge(s.n_exp, 2 * c + 2)
                dve.scalar_tensor_tensor(kf[:, :], kf[:, :], 0.0, z1[:, :], ALU.max, ALU.add).then_inc(s.n_feat, 1)
                dve.wait_ge(s.n_proj, 4 * c + 4)
                dve.tensor_tensor(vA[:, :, 0:D], B[3][:, :].rearrange("p (t d) -> p t d", t=CT),
                                  bc(lbv_row[:, :].unsqueeze(1), [P, CT, D]), ALU.add).then_inc(s.n_v, 1)
                for b in range(2):
                    dve.wait_ge(s.n_att, 2 * c + b + 1)
                    dve.tensor_tensor(am[b][:, :], B[4 + b][:, 0:384], causal[:, :], ALU.mult).then_inc(s.n_am, 1)
                for b in range(2):
                    dve.wait_ge(s.n_num, 2 * c + b + 1)
                    dve.tensor_scalar(ndr[:, 0, 2 * b:2 * b + 2],
                                      B[6 + b][:, 0:2 * (D + 1)].rearrange("p (t d) -> p t d", t=2)[:, :, D],
                                      DEN_EPS, None, ALU.add).then_inc(s.n_den, 1)
                dve.wait_ge(s.n_den, 2 * c + 2)
                dve.reciprocal(ndr[:, 1, :], ndr[:, 0, :]).then_inc(s.n_rec, 1)
                dve.wait_ge(s.n_rec, c + 1)
                for j in range(CT):
                    o0 = (j % 2) * (D + 1)
                    m = dve.tensor_scalar(osb[:, j, :], B[6 + j // 2][:, o0:o0 + D], ndr[:, 1, j:j + 1], None, ALU.mult)
                m.then_inc(s.n_o, 1)
                dve.wait_ge(s.n_yps, c + 1)
                dve.tensor_tensor(U[:, bass.ts(c, CT), :], B[5][:, :].rearrange("p (t d) -> p t d", t=CT),
                                  bc(lbp_row[:, :].unsqueeze(1), [P, CT, D]), ALU.add).then_inc(s.n_out, 1)
            phase_end(dve, "dve", ph)

        def fin_dve(dve, coef, k0=None):
            if k0 is not None:
                for c in range(NCH):
                    add_experts(dve, k0, c)
                    dve.wait_ge(s.x_sum, 2 * (k0 * NT + (c + 1) * CT))
                    dve.sem_inc(s.fin_x, 1)
                return
            with dve.Fori(0, NCH) as c:
                xc = X[:, bass.ts(c, CT), :]
                dve.scalar_tensor_tensor(xc, U[:, bass.ts(c, CT), :], coef, xc, ALU.mult, ALU.add).then_inc(s.fin_x, 1)

        def fin_sync(sp):
            per_seq = out.rearrange("b (t p) d -> p (b t) d", p=P)
            for c in range(NCH):
                sp.wait_ge(s.fin_x, c + 1)
                sp.dma_start(per_seq[:, c * CT:(c + 1) * CT, :], X[:, c * CT:(c + 1) * CT, :]).then_inc(s.out_done, 16)
            sp.wait_ge(s.out_done, 16 * NCH)

        def nothing(eng, me, ph):
            phase_end(eng, me, ph)

        COEF = [0.0, 0.5, 1.0, 0.5, 0.5, 1.0, 0.5]

        @block.sync
        def _(sp):
            setup_sync(sp)
            if stages >= 1:
                ffn_sync(sp, 0, 2)
            if stages >= 3:
                ffn_sync(sp, 1, 10)
            if stages >= 4:
                me_sync(sp, 0)
            if stages >= 6:
                me_sync(sp, 1)
            fin_sync(sp)

        @block.tensor
        def _(pe):
            setup_pe(pe)
            tr_pe(pe, 0, 2)
            if stages >= 1:
                ffn(pe, "pe", 0, 2)
            if stages >= 2:
                tr_pe(pe, 1, 7)
                ap_pe(pe, 8)
                aa_pe(pe, 9)
            if stages >= 3:
                tr_pe(pe, 2, 10)
                ffn(pe, "pe", 1, 10)
            if stages >= 4:
                tr_pe(pe, 3, 15)
                mr_pe(pe, 0, 16)
                me_pe(pe, 0, 17)
            if stages >= 5:
                tr_pe(pe, 4, 18)
                la_pe(pe, 19)
            if stages >= 6:
                tr_pe(pe, 5, 20)
                mr_pe(pe, 1, 21)
                me_pe(pe, 1, 22)

        @block.scalar
        def _(act):
            setup_act(act)
            tr_act(act, 0, 2)
            if stages >= 1:
                ffn(act, "act", 0, 2)
            if stages >= 2:
                tr_act(act, 1, 7)
                ap_act(act, 8)
                aa_act(act, 9)
            if stages >= 3:
                tr_act(act, 2, 10)
                ffn(act, "act", 1, 10)
            if stages >= 4:
                tr_act(act, 3, 15)
                mr_act(act, 0, 16)
                me_act(act, 0, 17)
            if stages >= 5:
                tr_act(act, 4, 18)
                la_act(act, 19)
            if stages >= 6:
                tr_act(act, 5, 20)
                mr_act(act, 1, 21)
                me_act(act, 1, 22)

        @block.vector
        def _(dve):
            setup_dve(dve)
            tr_dve(dve, 0, 0.0, 2)
            if stages >= 1:
                ffn(dve, "dve", 0, 2)
            if stages >= 2:
                tr_dve(dve, 1, COEF[1], 7)
                ap_dve(dve, 8)
                aa_dve(dve, 9)
            if stages >= 3:
                tr_dve(dve, 2, COEF[2], 10)
                ffn(dve, "dve", 1, 10)
            if stages >= 4:
                tr_dve(dve, 3, COEF[3], 15)
                mr_dve(dve, 0, COEF[4], 16)
                me_dve(dve, 0, 17)
            if stages >= 5:
                tr_dve(dve, 4, 0.0, 18, added=True)
                la_dve(dve, 19)
            if stages >= 6:
                tr_dve(dve, 5, COEF[5], 20)
                mr_dve(dve, 1, COEF[6], 21)
                me_dve(dve, 1, 22)
            fin_dve(dve, COEF[stages], {4: 0, 6: 1}.get(stages))

        @block.gpsimd
        def _(pool):
            setup_pool(pool)
            tr_pool(pool, 0, 2)
            if stages >= 1:
                ffn(pool, "pool", 0, 2)
            if stages >= 2:
                tr_pool(pool, 1, 7)
                vm_zeros(pool)
                nothing(pool, "pool", 8)
                aa_pool(pool, 9)
            if stages >= 3:
                tr_pool(pool, 2, 10, kT_zeros)
                ffn(pool, "pool", 1, 10)
            if stages >= 4:
                tr_pool(pool, 3, 15)
                mr_pool(pool, 0, 16)
                me_pool(pool, 0, 17)
            if stages >= 5:
                tr_pool(pool, 4, 18, vA_ones, twice=True)
                nothing(pool, "pool", 19)
            if stages >= 6:
                tr_pool(pool, 5, 20)
                mr_pool(pool, 1, 21)
                me_pool(pool, 1, 22)


_INS = ["L0_attn_x", "L0_attn_qkv_w", "L0_attn_qkv_b", "L0_attn_out_w", "L0_attn_out_b", "L0_attn_decay_alpha",
        "L0_ffn_wqkv", "L0_ffn_q_scale", "L0_ffn_k_scale", "L0_ffn_wo", "L0_ffn_ln_g", "L0_ffn_ln_b", "L0_ffn_w1",
        "L0_ffn_b1", "L0_ffn_w2", "L0_ffn_b2", "L1_attn_w_qkv", "L1_attn_b_qkv", "L1_attn_w_gate", "L1_attn_b_gate",
        "L1_attn_w_proj", "L1_attn_b_proj", "L1_attn_ln_g", "L1_attn_ln_b", "L1_ffn_Ws1", "L1_ffn_bs1", "L1_ffn_Ws2",
        "L1_ffn_bs2", "L1_ffn_We1", "L1_ffn_be1", "L1_ffn_We2", "L1_ffn_be2", "L1_ffn_Wr", "L1_ffn_br"]


def kernel(**inputs):
    import concourse.bacc as bacc
    from concourse.bass_utils import run_bass_kernel_spmd

    nc = bacc.Bacc("TRN2", target_bir_lowering=False, num_devices=1)
    arrays, aps = {}, {}
    for name in _INS:
        arrays[f"in_{name}"] = np.ascontiguousarray(inputs[name])
    for name, value in constants().items():
        arrays[f"in_{name}"] = np.ascontiguousarray(value.reshape(value.shape))
    for name, value in arrays.items():
        aps[name[3:]] = nc.dram_tensor(name, value.shape, mybir.dt.from_np(value.dtype), kind="ExternalInput").ap()
    out = nc.dram_tensor("out_0", (NBATCH, SEQ, D), F32, kind="ExternalOutput").ap()
    build(nc, aps, out)
    r = run_bass_kernel_spmd(nc, [arrays], core_ids=[0])
    return r.results[0]["out_0"]
```

```python
from collections import namedtuple
from contextlib import ExitStack

import concourse.bass as bass
import numpy as np
from concourse import mybir

F32 = mybir.dt.float32
U32 = mybir.dt.uint32
F16 = mybir.dt.float16
F32R = mybir.dt.float32r
ALU = mybir.AluOpType
ACT = mybir.ActivationFunctionType
AX_X = mybir.AxisListType.X

P = 128
D = 128
NBATCH, SEQ = 8, 256
NT = NBATCH * SEQ // P
CH = 512
NCH = NT * P // CH
CT = CH // P
DEPTH, LH, LD, WIN = 2, 8, 64, 64
INNER = LH * LD
HID = int(D * 4 * 2 / 3)
HCH = [(0, 128), (128, 128), (256, HID - 256)]
QK_SCALE = 8.0
AH, AD = 16, 8
E, HS, HR, TAU = 12, 2 * D, 3 * D, 1.5
NEG = -1e25
LN_EPS, DEN_EPS = 1e-5, 1e-6
ARENA = 25002
NXT = (2 * NT * P) // P + E
NXG = NXT // 4

V_BE1, V_BS1, V_B1, V_LG, V_LB, V_QKVB, V_LQKVB, V_LGATE, V_LNG, V_LNB, V_N = (
    0, 72, 76, 88, 90, 92, 95, 98, 99, 100, 101)

SEMS = """
aq_hi a_qh inv_a inv_b u_stored inv_ps st_y2 st_y3 ld_x consts wt_ready ld_first ld_vec ld_rows ld_late ld_w1
vec_ps wt_ps ph_pe ph_act ph_dve ph_pool x_new stats_raw stats_ready rs_var rs_ready ln_done ln_ps hT_ready
q_ps k_ps v_ps sqq_done sqk_done rq_ab rk_ab qr_ready kadd_ready ssq_raw ssk_raw ss_ready rn_ready rn_self
kr_ready qT_ps qT_ready kT_ps kT_ready v_ready sim_ready mx_ready smax_ready exp_done rden_ready probs_ready
pT_ps pT_ready pv_done o_ready y_ps x1_done h_ps m_stats m_raw m_var m_rs hn_ready hnT_ps hT2_ready up_ps
gelu_done act_ready dn_ps x1b_ready x2_ready xT_ps xT_done x2_copied aq_ps av_ps aq_ready av_ready a_qm a_sim
a_mx a_max a_exp a_rd a_prob a_Tps a_Tready a_pv a_o a_yps a_out vm_ready alpha_ready r_lg r_self r_m12 r_e
r_both r_cum r_pos r_te r_wst r_wps r_wT s_up s_gelu s_act s_dn s_tmp ld_ew ld_x0 ld_x1 st_y0 st_y1 x_ps x_T
x_up_g x_up_a x_gb x_ab x_gl x_act x_Tps x_actT x_dn x_y gat0 gat1 x_sum n_xn n_proj n_min n_exp n_feat n_gexp
n_g n_gd n_v n_att n_am n_num n_den n_rec n_o n_oT_ps n_oT n_yps n_out out_done fin_x rs_self passed
""".split()

Semaphores = namedtuple("Semaphores", SEMS)


class Step:

    def __init__(self, q, Q=None):
        self.Q, self.inner = Q, Q is None
        self.opens = q % 2 == 0 and self.has(4)

    def has(self, d):
        return self.inner or 0 <= self.Q + d < NT

    def second(self, d):
        return self.inner or self.Q + d >= 1

    def after(self, n, u):
        return self.inner or 4 * self.Q + u >= n


def rotary_tables():
    f = np.float32
    half = np.arange(0, LD, 2, dtype=f)
    inv = f(1.0) / np.power(f(10000.0), half / f(LD)).astype(f)
    t = np.arange(SEQ, dtype=f)
    fr = (t[:, None] * inv[None, :]).astype(f)
    fr = np.concatenate([fr, fr], -1)
    base = ((half + f(0.4 * LD)) / f(1.4 * LD)).astype(f)
    power = ((t - SEQ // 2) / f(WIN // 2)).astype(f)
    sc = np.power(base[None, :].astype(f), power[:, None]).astype(f)
    sc = np.concatenate([sc, sc], -1)
    sign = np.concatenate([-np.ones(LD // 2, f), np.ones(LD // 2, f)])
    cos, sin = np.cos(fr).astype(f), np.sin(fr).astype(f) * sign
    tabs = np.stack([cos * sc, sin * sc, cos / sc, sin / sc]).astype(f)
    return np.ascontiguousarray(tabs.reshape(4, 2, P, LD).transpose(2, 0, 1, 3))


def constants():
    i, j = np.arange(P)[:, None], np.arange(P)[None, :]
    f = np.float32
    j1 = np.arange(64, SEQ)[None, :]
    band0 = np.where((j <= i) & (i - j <= WIN), 0, NEG).astype(f)
    band1 = np.where((j1 <= i + P) & (i + P - j1 <= WIN), 0, NEG).astype(f)
    jj = np.arange(SEQ)[None, :]
    dist = np.stack([np.abs(jj - i), np.abs(jj - i - P)], 1).astype(f)
    tri = (i <= j).astype(f)
    return {
        "ident": np.eye(P, dtype=f),
        "shift": np.concatenate([(j == i + 1), (i == P - 1) & (j == 0)], 1).astype(f),
        "rot": rotary_tables(),
        "band": np.concatenate([band0, band0, band1, band1], 1),
        "dist": dist,
        "headmask": (i // AD == np.arange(AH)[None, :]).astype(f),
        "causal": np.concatenate([tri, np.ones((P, P), f), tri], 1),
        "strict": (i < j).astype(f),
        "code": (np.array([1, -1])[None, :, None] * (1 + P * np.arange(NT)[None, None, :] + i[:, :, None])).astype(f),
        "slot": (2 * NT * P + P * np.arange(NXT)[None, :] + i).astype(f),
        "iota": np.broadcast_to(np.concatenate([np.arange(E), np.arange(NXT), P * np.arange(NT),
                                                np.arange(P)]).astype(f)[None, :],
                                (P, E + NXT + NT + P)).copy(),
    }


def build(nc, a, out, stages=6):
    with ExitStack() as ctx:
        def sb(name, shape, dt=F32):
            return ctx.enter_context(nc.sbuf_tensor(name, shape, dt))

        s = Semaphores(*[ctx.enter_context(nc.semaphore(n)) for n in SEMS])
        B = [ctx.enter_context(nc.psum_tensor(f"bank{n}", [P, 512], F32)) for n in range(8)]

        X = sb("X", [P, NT, D])
        U = sb("U", [P, NT, D])
        uT = sb("uT", [P, NT * P])
        ident = sb("ident_sb", [P, P])
        shift = sb("shift_sb", [P, 2, P])
        rot = sb("rot_sb", [P, 4, 2, LD])
        band = sb("band_sb", [P, 640])
        band_of = [band[:, 0:128], band[:, 256:448]]
        dist = sb("dist_sb", [P, 2, SEQ])
        headmask = sb("headmask_sb", [P, AH])
        causal = sb("causal_sb", [P, 384])
        iota = sb("iota_sb", [P, E + NXT + NT + P])
        vec_rows = sb("vec_rows", [P, P])
        vec = sb("vec", [P, V_N])
        mhalf = sb("mhalf", [P, NT])
        ebase = sb("ebase", [P, NT])
        qs_row = sb("qs_row", [P, DEPTH, 2, LD])
        ks_row = sb("ks_row", [P, DEPTH, 2, LD])
        b2_row = sb("b2_row", [P, DEPTH, D])
        bs2_row = sb("bs2_row", [P, D])
        ob_row = sb("ob_row", [P, D])
        bv_row = sb("bv_row", [P, D])
        lbv_row = sb("lbv_row", [P, D])
        lbp_row = sb("lbp_row", [P, D])
        alpha = sb("alpha", [P, AH])
        alpha_w = sb("alpha_w", [P, 3, AH])
        aw_rows = sb("aw_rows", [P, 4, D])
        awT = sb("awT", [P, 4, D])
        nqkv = sb("nqkv", [P, 3 * D])
        ngate = sb("ngate", [P, D])
        nproj = sb("nproj", [P, D])
        ws1 = sb("ws1", [P, 2 * HS])
        ws2 = sb("ws2", [P, 2, D])
        wr = sb("wr", [P, E])
        be2 = sb("be2", [E, D])
        wts = sb("wts", [P, NT, E])
        arena_at = nc.sbuf_base
        arena = sb("arena", [P, ARENA])

        def cut(start, *shape):
            n = int(np.prod(shape))
            assert start + n <= ARENA
            v = arena[:, start:start + n]
            names = "abcd"[:len(shape)]
            if len(shape) > 1:
                sizes = dict(zip(names[1:], shape[1:]))
                v = v.rearrange(f"p ({' '.join(names)}) -> p {' '.join(names)}", **sizes)
            return v

        wqkv = cut(18432, DEPTH, 3 * INNER)
        wo = cut(21504, DEPTH, 4, D)
        w1 = cut(22528, 2 * HID)
        w2 = cut(23210, DEPTH, 3, D)
        rtab = cut(23978, DEPTH, 4, 2, LD)
        st6 = sb("st6", [P, NT, 6])
        mv = sb("mv", [P, NT, 2])
        rs = sb("rs", [P, 5, NT])
        stg = sb("stg", [P, CT, D])
        stg_flat = stg[:, :, :].rearrange("p t d -> p (t d)")
        hT = [sb(f"hT{n}", [P, SEQ]) for n in range(2)]
        kT = [cut(n * 2048, 4, 2, SEQ) for n in range(2)]
        qT = [cut(4096 + n * 1024, 4, SEQ) for n in range(2)]
        vv = [cut(6144 + n * 1024, 2, INNER) for n in range(2)]
        rab = cut(8192, 4, INNER)
        sq = cut(10240, 2 * INNER)
        qr = cut(11264, INNER)
        kadd = cut(11776, INNER)
        kr = cut(12288, INNER)
        ss = sb("ss", [P, 2, 16])
        rn = sb("rn", [P, 4, 3, 8])
        rnp = sb("rnp", [P, 16])
        sm = [sb(f"sm{n}", [P, 2, SEQ]) for n in range(2)]
        mx = sb("mx", [P, 2, 2])
        nb = sb("nb", [P, 2, 2])
        den = sb("den", [P, 2, 2])
        rden = sb("rden", [P, 2, 2])
        pA = [sb(f"pA{n}", [P, 2, SEQ]) for n in range(2)]
        pB = [sb(f"pB{n}", [P, 2, SEQ]) for n in range(2)]
        pT = [sb(f"pT{n}", [P, 512]) for n in range(2)]
        oT = sb("oT", [P, 4, P])
        hn = sb("hn", [P, SEQ])
        hT2 = sb("hT2", [P, SEQ])
        gl_at = nc.sbuf_base
        gl = sb("gl", [P, 3, CH])
        act_b = sb("act_b", [P, 3, CH])
        x1b = sb("x1b", [P, SEQ])
        xs = sb("xs", [P, SEQ])
        mrs = sb("mrs", [P, 2, 2])
        dbias = cut(0, AH, 2, SEQ)
        VM_AT = 8192
        vm = cut(VM_AT, 2, AH, P)
        qTa = cut(12288, NT * P)
        va = cut(16384, NT, D)
        qm_hi = [sb(f"qm{n}", [P, SEQ], F32R) for n in range(2)]
        qm_lo = [sb(f"qm_lo{n}", [P, SEQ], F32R) for n in range(2)]
        kTa_hi = nc.alloc_sbuf_tensor_at("kTa_hi", [P, NT * P], F32R, offset=arena_at + 4 * 14336)
        kTa_lo = nc.alloc_sbuf_tensor_at("kTa_lo", [P, NT * P], F32R, offset=gl_at)
        oTa = sb("oTa", [P, SEQ])
        def flat(t):
            return t[:, :, :].rearrange("p a b -> p (a b)")

        def halves(t):
            return [t[:, n * NT * E:(n + 1) * NT * E].rearrange("p (t e) -> p t e", e=E) for n in range(2)]
        oh = halves(flat(pA[0]))
        both, lg = halves(flat(pA[1]))
        tot, pre0 = halves(flat(pB[0]))
        pre1, place = halves(flat(pB[1]))
        prod, wtmp = halves(pT[0])
        need = pT[1][:, 0:E * NT].rearrange("p (e t) -> p e t", e=E)
        top = sb("top", [P, NT, 8])
        idx = sb("idx", [P, NT, 8], U32)
        idf = sb("idf", [P, NT, 2])
        rw = sb("rw", [P, NT, 4])
        wc = sb("wc", [P, 2, NT])
        wst = sb("wst", [P, CT, E])
        wT = sb("wT", [E, CH])
        ntile = sb("ntile", [P, E])
        etile = sb("etile", [P, 2, E])
        ecmp = sb("ecmp", [P, NXT, E])
        tef = sb("tef", [P, 2, NXT])
        te = sb("te", [P, NXT], U32)
        posf = sb("posf", [P, 2, NT])
        pos = sb("pos", [P, 2, 2, NT], U32)
        posh = sb("posh", [P, 2, 2, NT])
        code = sb("code_sb", [P, 2, NT])
        slot = sb("slot_sb", [P, NXT])
        inv = sb("inv", [P, 5, NXT])
        inv_u = sb("inv_u", [P, 2, NXT], U32)
        RING = 8
        ringA = arena[:, 23940:24452].bitcast(F16).rearrange("p (r c) -> p r c", r=RING)
        ringB = arena[:, 24452:24452 + RING * NXT // 2].bitcast(F16).rearrange("p (r c) -> p r c", r=RING)
        strict = sb("strict_sb", [P, P])
        ones = sb("ones", [P, P])
        br_row = sb("br_row", [P, E])
        xg = sm[0][:, :, :].rearrange("p a (b d) -> p (a b) d", d=P)
        yb = stg
        xT = [pT[0][:, n * P:(n + 1) * P] for n in range(2)]
        gl_flat, act_flat = flat(gl), flat(act_b)
        xgate = [gl_flat[:, n * HR:(n + 1) * HR] for n in range(2)]
        xgelu = [gl_flat[:, (2 + n) * HR:(3 + n) * HR] for n in range(2)]
        xa = [act_flat[:, n * HR:(n + 1) * HR] for n in range(2)]
        xact = [act_flat[:, (2 + n) * HR:(3 + n) * HR] for n in range(2)]
        xactT = [flat(pA[n])[:, 0:HR] for n in range(2)]
        we1 = cut(0, E * 2 * HR)
        we2 = cut(E * 2 * HR, E * HR)
        be1_row = cut(E * 3 * HR, E * 2 * HR)
        xn = sb("xn", [P, CH])
        qf = [flat(pA[0]), gl_flat[:, 0:CH]]
        kf = [flat(pA[1]), gl_flat[:, CH:2 * CH]]
        z0, z1 = flat(pB[0]), flat(pB[1])
        z2, noT = pT[0][:, :], pT[1][:, :]
        osb = sm[0][:, :, :].rearrange("p a (b d) -> p (a b) d", d=P)
        vA = [cut(E * 5 * HR, CT, D + 1), act_flat[:, 0:CT * (D + 1)].rearrange("p (t d) -> p t d", d=D + 1)]
        am = [flat(sm[1])[:, 0:384], cut(E * 5 * HR + 516, 384)]
        ndr = sb("ndr", [P, 2, CT])

        u_rows = nc.dram_tensor("u_rows", [NT * P, D], F32, kind="Internal").ap()
        y_rows = nc.dram_tensor("y_rows", [2 * NT * P + NXT * P, D], F32, kind="Internal").ap()

        block = ctx.enter_context(nc.Block())
        engines = ("pe", "act", "dve", "pool")
        done = {"pe": s.ph_pe, "act": s.ph_act, "dve": s.ph_dve, "pool": s.ph_pool}

        def phase_end(eng, me, k):
            eng.drain().then_inc(done[me], 1)
            for other in engines:
                if other != me:
                    eng.wait_ge(done[other], k)
            eng.sem_inc(s.passed, 1)

        def wait_apart(eng, sem, count):
            eng.wait_ge(sem, count)
            eng.sem_inc(s.passed, 1)

        def bc(ap, shape):
            return ap.broadcast_to(shape)

        def heads(ap):
            return ap.rearrange("p (h d) -> p h d", h=LH)

        def flipped(ap):
            return ap.rearrange("p (h a d) -> p h a d", h=LH, a=2)[:, :, ::-1, :]

        N_FIRST, N_VEC, N_ROWS, N_LATE = 8, 21, 6, 24

        def setup_sync(sp):
            def row(ap, n):
                return ap.rearrange("(o n) -> o n", o=1).broadcast_to([P, n])
            sp.dma_start(X[:, :, :], a["L0_attn_x"].rearrange("b (t p) d -> p (b t) d", p=P)).then_inc(s.ld_x, 16)
            sp.dma_start(ident[:, :], a["ident"]).then_inc(s.ld_x, 16)
            first = [(rot[:, :, :, :], a["rot"]), (band[:, :], a["band"]),
                     (wqkv[:, :, :], a["L0_ffn_wqkv"].rearrange("l k n -> k l n")),
                     (wo[:, :, :, :], a["L0_ffn_wo"].rearrange("l (c k) n -> k l c n", k=P)),
                     (shift[:, :, :], a["shift"].rearrange("p (a b) -> p a b", a=2)),
                     (w2[:, 0, 0:2, :], a["L0_ffn_w2"][0, 0:256, :].rearrange("(c k) n -> k c n", k=P)),
                     (w2[:, 1, 0:2, :], a["L0_ffn_w2"][1, 0:256, :].rearrange("(c k) n -> k c n", k=P)),
                     (w2[0:HCH[2][1], :, 2, :], a["L0_ffn_w2"][:, 256:HID, :].rearrange("l k n -> k l n"))]
            assert len(first) == N_FIRST
            for dst, src in first:
                sp.dma_start(dst, src).then_inc(s.ld_first, 16)
            sp.wait_ge(s.consts, 1)
            b1 = a["L0_ffn_b1"]
            vec_loads = [(vec_rows[V_BE1:V_BE1 + 72, :], a["L1_ffn_be1"].rearrange("e (c k) -> (e c) k", k=P)),
                         (vec_rows[V_BS1:V_BS1 + 4, :], a["L1_ffn_bs1"].rearrange("(c k) -> c k", k=P)),
                         (vec_rows[V_LG:V_LG + 2, :], a["L0_ffn_ln_g"]), (vec_rows[V_LB:V_LB + 2, :], a["L0_ffn_ln_b"]),
                         (vec_rows[V_QKVB:V_QKVB + 3, :], a["L0_attn_qkv_b"].rearrange("(c k) -> c k", k=P)),
                         (vec_rows[V_LQKVB:V_LQKVB + 3, :], a["L1_attn_b_qkv"].rearrange("(c k) -> c k", k=P)),
                         (vec_rows[V_LGATE:V_LGATE + 1, :], a["L1_attn_b_gate"].rearrange("(c k) -> c k", k=P)),
                         (vec_rows[V_LNG:V_LNG + 1, :], a["L1_attn_ln_g"].rearrange("(c k) -> c k", k=P)),
                         (vec_rows[V_LNB:V_LNB + 1, :], a["L1_attn_ln_b"].rearrange("(c k) -> c k", k=P))]
            for l in range(DEPTH):
                for g in range(2):
                    for c, (h0, hn_) in enumerate(HCH):
                        r = V_B1 + l * 6 + g * 3 + c
                        vec_loads.append((vec_rows[r:r + 1, 0:hn_], b1[l:l + 1, g * HID + h0:g * HID + h0 + hn_]))
            assert len(vec_loads) == N_VEC
            for dst, src in vec_loads:
                sp.dma_start(dst, src).then_inc(s.ld_vec, 16)
            qs, ks = a["L0_ffn_q_scale"], a["L0_ffn_k_scale"]
            rows = []
            for t, src in ((qs_row, qs), (ks_row, ks)):
                v = src.rearrange("(o l) d -> o l d", o=1)
                rows.append((t[:, :, 0, :], v.broadcast_to([P, DEPTH, LD])))
                for h in range(2):
                    rows.append((t[:, :, 1, 32 * h:32 * h + 32],
                                 v[:, :, 32 - 32 * h:64 - 32 * h].broadcast_to([P, DEPTH, 32])))
            assert len(rows) == N_ROWS
            for dst, src in rows:
                sp.dma_start(dst, src).then_inc(s.ld_rows, 16)
            late = [(b2_row[:, :, :], a["L0_ffn_b2"].rearrange("(o l) d -> o l d", o=1).broadcast_to([P, DEPTH, D])),
                     (bs2_row[:, :], row(a["L1_ffn_bs2"], D)), (ob_row[:, :], row(a["L0_attn_out_b"], D)),
                     (bv_row[:, :], row(a["L0_attn_qkv_b"][2 * D:3 * D], D)),
                     (lbv_row[:, :], row(a["L1_attn_b_qkv"][2 * D:3 * D], D)),
                     (lbp_row[:, :], row(a["L1_attn_b_proj"], D)),
                     (alpha[:, :], row(a["L0_attn_decay_alpha"], AH))]
            late += [(aw_rows[:, 0:3, :], a["L0_attn_qkv_w"].rearrange("(c p) k -> p c k", p=P)),
                    (aw_rows[:, 3, :], a["L0_attn_out_w"]), (dist[:, :, :], a["dist"]),
                    (headmask[:, :], a["headmask"]), (causal[:, :], a["causal"]), (iota[:, :], a["iota"]),
                    (nqkv[:, :], a["L1_attn_w_qkv"]), (ngate[:, :], a["L1_attn_w_gate"]),
                    (nproj[:, :], a["L1_attn_w_proj"]), (ws1[:, :], a["L1_ffn_Ws1"]),
                    (ws2[:, :, :], a["L1_ffn_Ws2"].rearrange("(c k) n -> k c n", k=P)),
                    (wr[:, :], a["L1_ffn_Wr"]), (br_row[:, :], row(a["L1_ffn_br"], E)), (strict[:, :], a["strict"]),
                    (code[:, :, :], a["code"]), (slot[:, :], a["slot"]),
                    (be2[:, :], a["L1_ffn_be2"])]
            assert len(late) == N_LATE
            for dst, src in late:
                sp.dma_start(dst, src).then_inc(s.ld_late, 16)

        def setup_pool(pool):
            pool.memset(vec_rows[:, :], 0.0).then_inc(s.consts, 1)
            pool.memset(mhalf[:, :], -0.5).then_inc(s.consts, 1)

        def setup2_pool(pool, ph):
            zeros = [hT[n][:, :] for n in range(2)]
            for n in range(2):
                zeros += [kT[n][:, :, :, :], pB[n][:, :, :]]
            for z in zeros:
                pool.memset(z, 0.0)
            pool.memset(ones[:, :], 1.0)
            pool.memset(ebase[:, :], float(np.e))
            phase_end(pool, "pool", ph)

        def setup2_pe(pe, ph):
            pe.wait_ge(s.ld_first, 16 * N_FIRST)
            pe.wait_ge(s.ld_vec, 16 * N_VEC)
            pe.transpose(B[0][:, 0:P], vec_rows[:, :], ident[:, :]).then_inc(s.vec_ps, 1)
            phase_end(pe, "pe", ph)

        def setup2_dve(dve, ph):
            dve.wait_ge(s.ld_first, 16 * N_FIRST)
            dve.wait_ge(s.ld_rows, 16 * N_ROWS)
            for l in range(DEPTH):
                for kind in range(4):
                    row_ = (qs_row, ks_row)[kind // 2][:, l, kind % 2, :]
                    dve.tensor_tensor(rtab[:, l, kind, :, :], rot[:, kind, :, :],
                                      bc(row_.unsqueeze(1), [P, 2, LD]), ALU.mult)
            dve.wait_ge(s.vec_ps, 1)
            dve.tensor_copy(vec[:, :], B[0][:, 0:V_N]).then_inc(s.wt_ready, 1)
            dve.wait_ge(s.wt_ready, 1)
            dve.tensor_scalar(vec[:, V_QKVB:V_QKVB + 1], vec[:, V_QKVB:V_QKVB + 1], AD ** -0.5, None, ALU.mult)
            phase_end(dve, "dve", ph)

        HALF = NT // 2

        def tr_dve(dve, n, coef, ph, added=False):
            adds = n and not added
            first_x = (n - 1 - n // 5) * NCH

            def x_chunk(c):
                ts = slice(c * CT, (c + 1) * CT)
                dve.scalar_tensor_tensor(X[:, ts, :], U[:, ts, :], coef, X[:, ts, :], ALU.mult, ALU.add)\
                    .then_inc(s.x_new, 1)

            if not n:
                dve.wait_ge(s.ld_x, 32)
            if n == 1:
                dve.wait_ge(s.ld_late, 16 * N_LATE)
                dve.scalar_tensor_tensor(alpha_w[:, 0, :], alpha[:, :], -1.0, alpha[:, :], ALU.mult, ALU.min)\
                    .then_inc(s.alpha_ready, 1)
            if adds:
                x_chunk(0)
            for c in range(NCH):
                if added:
                    add_experts(dve, 0, c)
                    dve.wait_ge(s.x_sum, 2 * (c + 1) * CT)
                if adds:
                    if c + 1 < NCH:
                        x_chunk(c + 1)
                    dve.wait_ge(s.x_new, first_x + c + 1)
                for t in range(c * CT, (c + 1) * CT):
                    m = dve.bn_stats(st6[:, t, :], X[:, t, :])
                m.then_inc(s.stats_raw, 1)
                if c % 2:
                    dve.wait_ge(s.stats_raw, n * NCH + c + 1)
                    for t in range(c * CT - CT, (c + 1) * CT):
                        m = dve.bn_aggr(mv[:, t, :], st6[:, t, :])
                    m.then_inc(s.stats_ready, 1)
            for c in range(NCH):
                if c % 2 == 0:
                    dve.wait_ge(s.rs_ready, n * 2 + c // 2 + 1)
                    dve.wait_ge(s.stats_ready, n * 2 + c // 2 + 1)
                for t in range(c * CT, (c + 1) * CT):
                    m = dve.tensor_scalar(U[:, t, :], X[:, t, :], mv[:, t, 0:1], rs[:, 1, t:t + 1],
                                          ALU.subtract, ALU.mult)
                m.then_inc(s.ln_done, 1)
            if n == 1:
                dve.wait_ge(s.alpha_ready, 3)
                dve.scalar_tensor_tensor(alpha[:, :], alpha[:, :], 0.0, alpha_w[:, 2, :], ALU.max, ALU.add)\
                    .then_inc(s.alpha_ready, 1)
            phase_end(dve, "dve", ph)

        def tr_pe(pe, n, ph):
            if not n:
                pe.wait_ge(s.ld_x, 32)
            for c in range(NCH):
                pe.wait_ge(s.ln_done, n * NCH + c + 1)
                for j in range(CT):
                    m = pe.transpose(B[c][:, j * P:(j + 1) * P], U[:, c * CT + j, :], ident[:, :])
                m.then_inc(s.ln_ps, 1)
            phase_end(pe, "pe", ph)

        def tr_act(act, n, ph):
            if n == 1:
                act.wait_ge(s.alpha_ready, 1)
                act.activation(alpha_w[:, 1, :], alpha_w[:, 0, :], ACT.Exp).then_inc(s.alpha_ready, 1)
                act.wait_ge(s.alpha_ready, 2)
                act.activation(alpha_w[:, 2, :], alpha_w[:, 1, :], ACT.Ln, bias=1.0).then_inc(s.alpha_ready, 1)
            act.preload_act_table(ACT.Exp)
            for c in range(NCH):
                act.wait_ge(s.ln_ps, n * NCH + c + 1)
                act.activation(uT[:, c * CH:(c + 1) * CH], B[c][:, :], ACT.Copy)
            phase_end(act, "act", ph)

        def vm_zeros(pool):
            pool.memset(vm[:, :, :, :], 0.0).then_inc(s.vm_ready, 1)

        def kT_zeros(pool):
            for n in range(2):
                pool.memset(kT[n][:, :, :, :], 0.0)

        def vA_ones(pool):
            for n in range(2):
                pool.memset(vA[n][:, :, D:D + 1], 1.0)

        def tr_pool(pool, n, ph, extra=None, twice=False):
            if extra:
                extra(pool)
            if not n:
                pool.wait_ge(s.consts, 2)
            for h in range(2):
                def part(k):
                    return rs[:, k, h * HALF:(h + 1) * HALF]

                def then_own(m, k):
                    m.then_inc(s.rs_self, 1)
                    pool.wait_ge(s.rs_self, 5 * h + k)

                power = mhalf[:, 0:HALF]
                pool.wait_ge(s.stats_ready, 2 * n + h + 1)
                var = mv[:, h * HALF:(h + 1) * HALF, 1]
                pool.tensor_scalar(part(0), var, LN_EPS, 0.0, ALU.add, ALU.add).then_inc(s.rs_var, 1)
                pool.wait_ge(s.rs_var, 2 * n + h + 1)
                if not twice:
                    pool.tensor_tensor(part(1), part(0), power, ALU.pow).then_inc(s.rs_ready, 1)
                else:
                    then_own(pool.tensor_tensor(part(2), part(0), power, ALU.pow), 1)
                    then_own(pool.tensor_tensor(part(3), part(2), part(2), ALU.mult), 2)
                    then_own(pool.tensor_tensor(part(4), part(3), var, ALU.mult), 3)
                    then_own(pool.tensor_scalar(part(3), part(4), LN_EPS, 0.0, ALU.add, ALU.add), 4)
                    then_own(pool.tensor_tensor(part(4), part(3), power, ALU.pow), 5)
                    pool.tensor_tensor(part(1), part(2), part(4), ALU.mult).then_inc(s.rs_ready, 1)
            phase_end(pool, "pool", ph)

        BQ, BK, BV, BT, BS, BP, BO = B[0], B[1], B[2], B[3], (B[4], B[5]), B[6], B[7]

        def steps(eng, step):
            for q in range(4):
                step(-1, q, Step(q, q - 4))
            for q in range(4):
                step(0, q, Step(q, q))
            with eng.Fori(1, NT // 4 - 1) as i:
                for q in range(4):
                    step(i, q, Step(q))
            for q in range(4):
                step(NT // 4 - 1, q, Step(q, NT - 4 + q))
            for q in (0, 1):
                step(NT // 4, q, Step(q, NT + q))

        def geometry(q):
            t = q % 2
            return (q // 2) % 2, t, (P if t == 0 else 192), (0 if t == 0 else 64)

        def probs(q, par):
            return (pA if q % 2 == 0 else pB)[par]

        def lo_pe(pe, l, pb, ph):
            tb, qb, hb = pb * NT, pb * NT * 4, pb * NBATCH

            def sim(i, q, u, banks_used):
                c, t, nk, k0 = geometry(q % 4)
                Q = 4 * i + q
                if u == 0:
                    pe.wait_ge(s.kT_ready, tb + Q + 1)
                if banks_used:
                    pe.wait_ge(s.smax_ready, qb + 4 * Q + u - 1)
                pe.matmul(BS[u % 2][:, 0:2 * nk], qT[c][:, u, t * P:(t + 1) * P], kT[c][:, u, :, k0:k0 + nk],
                          start=True, stop=True).then_inc(s.sim_ready, 1)

            def turn(i, q, u, bank_used):
                c, t, nk, k0 = geometry(q)
                n = qb + 4 * (4 * i + q) + u
                pe.wait_ge(s.probs_ready, n + 1)
                if bank_used:
                    pe.wait_ge(s.pT_ready, n)
                pr = probs(q, u % 2)
                for j in range(1 + t):
                    for x in range(2):
                        m = pe.transpose(BP[:, (2 * j + x) * P:(2 * j + x + 1) * P], pr[:, x, j * P:(j + 1) * P],
                                         ident[:, :])
                m.then_inc(s.pT_ps, 1)

            def pv(i, q, u, bank_used):
                c, t, nk, k0 = geometry(q)
                n = qb + 4 * (4 * i + q) + u
                pe.wait_ge(s.pT_ready, n + 1)
                if u == 0 and bank_used:
                    pe.wait_ge(s.o_ready, tb + 4 * i + q)
                if u == 0:
                    pe.wait_ge(s.v_ready, tb + 4 * i + q + 1)
                for x in range(2):
                    h = 2 * u + x
                    for j in range(1 + t):
                        m = pe.matmul(BO[64 * x:64 * x + 64, u * P:(u + 1) * P], vv[c][:, j, h * LD:(h + 1) * LD],
                                      pT[u % 2][:, (2 * j + x) * P:(2 * j + x + 1) * P], start=(j == 0), stop=(j == t))
                m.then_inc(s.pv_done, 1)

            def hT_of(q):
                return hT[(q // 2) % 2][:, (q % 2) * P:(q % 2 + 1) * P]

            def step(i, q, f):
                Q = 4 * i + q
                for u in range(4):
                    if u < 3:
                        if f.has(0):
                            sim(i, q, u + 1, f.after(2, u + 1))
                    elif f.has(1):
                        sim(i, q + 1, 0, f.second(1))
                    if u > 0:
                        if f.has(0):
                            turn(i, q, u - 1, f.after(1, u - 1))
                    elif f.has(-1):
                        turn(i if q else i - 1, (q - 1) % 4, 3, True)
                    if u == 0 and f.has(1):
                        pe.wait_ge(s.qr_ready, tb + Q + 2)
                        if f.second(1):
                            pe.wait_ge(s.kT_ready, tb + Q + 1)
                        for w in range(4):
                            m = pe.transpose(BT[:, w * P:(w + 1) * P], qr[:, w * P:(w + 1) * P], ident[:, :])
                        m.then_inc(s.qT_ps, 1)
                    if u == 0 and f.has(-2):
                        pe.wait_ge(s.o_ready, tb + Q - 1)
                        if f.has(1):
                            pe.wait_ge(s.v_ready, tb + Q + 2)
                        else:
                            pe.wait_ge(s.x1_done, tb + Q - 2)
                        for w in range(4):
                            m = pe.matmul(BV[:, 0:D], oT[:, w, :], wo_l(l, w), start=(w == 0), stop=(w == 3))
                        m.then_inc(s.y_ps, 1)
                    if u == 1 and f.has(1):
                        pe.wait_ge(s.kr_ready, tb + Q + 2)
                        pe.wait_ge(s.qT_ready, tb + Q + 2)
                        for w in range(4):
                            m = pe.transpose(BT[:, w * P:(w + 1) * P], kr[:, w * P:(w + 1) * P], ident[:, :])
                        m.then_inc(s.kT_ps, 1)
                    if u == 2 and f.has(3):
                        pe.wait_ge(s.hT_ready, hb + 2 * i + (q + 3) // 2 + 1)
                        if f.second(3):
                            pe.wait_ge(s.rq_ab, tb + Q + 3)
                        pe.matmul(BQ[:, :], hT_of(q + 3), wqkv_l(l, 0), start=True, stop=True).then_inc(s.q_ps, 1)
                    if u == 3 and f.has(3):
                        if f.second(3):
                            pe.wait_ge(s.rk_ab, tb + Q + 3)
                        pe.matmul(BK[:, :], hT_of(q + 3), wqkv_l(l, 1), start=True, stop=True).then_inc(s.k_ps, 1)
                    if u == 3 and f.has(2):
                        if f.has(-2):
                            pe.wait_ge(s.x1_done, tb + Q - 1)
                        elif f.second(2):
                            pe.wait_ge(s.v_ready, tb + Q + 2)
                        pe.matmul(BV[:, :], hT_of(q + 2), wqkv_l(l, 2), start=True, stop=True).then_inc(s.v_ps, 1)
                    if u >= 2:
                        if f.has(0):
                            pv(i, q, u - 2, f.has(-1))
                    elif f.has(-1):
                        pv(i if q else i - 1, (q - 1) % 4, u + 2, True)

            steps(pe, step)
            phase_end(pe, "pe", ph)

        def wqkv_l(l, k):
            return wqkv[:, bass.ds(l, 1), k * INNER:(k + 1) * INNER].rearrange("p o n -> p (o n)")

        def wo_l(l, w):
            return wo[:, bass.ds(l, 1), w, :].rearrange("p o n -> p (o n)")

        def lo_dve(dve, l, pb, ph):
            tb, qb = pb * NT, pb * NT * 4
            hb = pb * NBATCH

            def table(kind, t):
                v = rtab[:, bass.ds(l, 1), kind, t, :]
                return v

            def step(i, q, f):
                c, t, nk, k0 = geometry(q)
                Q = 4 * i + q
                r = Q + 2
                tr_ = (q + 2) % 2
                for u in range(4):
                    par = u % 2
                    n = qb + 4 * Q + u
                    if f.has(0):
                        wait_apart(dve, s.sim_ready, n + 1)
                        for x in range(2):
                            m = dve.tensor_tensor_reduce(sm[par][:, x, 0:nk], BS[par][:, x * nk:(x + 1) * nk], band_of[t],
                                                         1.0, -3e38, ALU.add, ALU.max, mx[:, par, x:x + 1])
                        m.then_inc(s.mx_ready, 1)
                    if f.has(0 if u else -1):
                        dve.wait_ge(s.exp_done, n)
                        dve.reciprocal(rden[:, 1 - par, :], den[:, 1 - par, :]).then_inc(s.rden_ready, 1)
                    if f.has(0):
                        dve.wait_ge(s.mx_ready, n + 1)
                        dve.tensor_tensor(nb[:, par, :], mx[:, par, :], rn[:, q, 2, 2 * u:2 * u + 2], ALU.mult)\
                            .then_inc(s.smax_ready, 1)
                    back = (q, u - 1) if u else ((q - 1) % 4, 3)
                    if f.has(0 if u else -1):
                        bp, nkb, k0b = 1 - par, geometry(back[0])[2], geometry(back[0])[3]
                        dve.wait_ge(s.rden_ready, n)
                        pr = probs(back[0], bp)
                        for x in range(2):
                            v = pr[:, x, k0b:k0b + nkb]
                            m = dve.tensor_scalar(v, v, rden[:, bp, x:x + 1], None, ALU.mult)
                        m.then_inc(s.probs_ready, 1)
                    if u == 3 and f.has(3):
                        dve.wait_ge(s.sqq_done, tb + Q + 4)
                        if f.second(3):
                            dve.wait_ge(s.ss_ready, tb + Q + 3)
                        dve.tensor_reduce(ss[:, 0, 0:8], heads(sq[:, 0:INNER]), AX_X, ALU.add).then_inc(s.ssq_raw, 1)
                    if u == 1 and f.has(2):
                        dve.wait_ge(s.sqk_done, tb + r + 1)
                        dve.tensor_reduce(ss[:, 0, 8:16], heads(sq[:, INNER:]), AX_X, ALU.add).then_inc(s.ssk_raw, 1)
                        dve.wait_ge(s.ssq_raw, tb + r + 1)
                        dve.wait_ge(s.ssk_raw, tb + r + 1)
                        if f.second(2):
                            dve.wait_ge(s.rn_ready, tb + r)
                        dve.tensor_scalar(ss[:, 1, :], ss[:, 0, :], 1e-24, None, ALU.max).then_inc(s.ss_ready, 1)
                    if f.has(2) and u < 3:
                        for kind in ((0, 1), (2,), (3,))[u]:
                            bank = BQ if kind < 2 else BK
                            if kind == 0 and f.second(2):
                                dve.wait_ge(s.qr_ready, tb + r)
                            if kind == 2 and f.second(2):
                                dve.wait_ge(s.kadd_ready, tb + r)
                            if kind % 2 == 0:
                                m = dve.tensor_tensor(heads(rab[:, kind, :]), heads(bank[:, :]),
                                                      bc(table(kind, tr_), [P, LH, LD]), ALU.mult)
                            else:
                                tb_ = table(kind, tr_).rearrange("p o (a d) -> p o a d", a=2)
                                m = dve.tensor_tensor(rab[:, kind, :].rearrange("p (h a d) -> p h a d", h=LH, a=2),
                                                      flipped(bank[:, :]), bc(tb_, [P, LH, 2, LD // 2]), ALU.mult)
                                m.then_inc(s.rq_ab if kind == 1 else s.rk_ab, 1)
                    if u == 1 and f.has(-2):
                        dve.wait_ge(s.y_ps, tb + Q - 1)
                        ut = U[:, bass.ds(Q - 2, 1), :].rearrange("p o d -> p (o d)")
                        dve.tensor_tensor(ut, BV[:, 0:D], ut, ALU.add).then_inc(s.x1_done, 1)
                    if u == 3 and f.opens:
                        h = hT[((q + 4) // 2) % 2]
                        b = 2 * i + (q + 4) // 2
                        src = uT[:, bass.ts(b, SEQ)]
                        if f.inner or Q >= 0:
                            dve.wait_ge(s.v_ps, tb + Q + 1)
                        dve.tensor_copy(h[0:64, :], src[0:64, :])
                        dve.tensor_copy(h[64:128, 1:SEQ], src[64:128, 0:SEQ - 1]).then_inc(s.hT_ready, 1)

            steps(dve, step)
            phase_end(dve, "dve", ph)

        def lo_act(act, l, pb, ph):
            tb, qb = pb * NT, pb * NT * 4
            act.preload_act_table(ACT.Exp)

            def pt_evac(q, u, n):
                act.wait_ge(s.pT_ps, n)
                cols = 256 * (1 + q % 2)
                act.activation(pT[u % 2][:, 0:cols], BP[:, 0:cols], ACT.Copy).then_inc(s.pT_ready, 1)

            def step(i, q, f):
                c, t, nk, k0 = geometry(q)
                Q = 4 * i + q
                for u in range(4):
                    par = u % 2
                    n = qb + 4 * Q + u
                    if u == 2 and f.has(-1):
                        act.wait_ge(s.pv_done, qb + 4 * Q)
                        if f.has(-2):
                            act.wait_ge(s.y_ps, tb + Q - 1)
                        act.activation(oT[:, :, :].rearrange("p w t -> p (w t)"), BO[:, :], ACT.Copy)\
                            .then_inc(s.o_ready, 1)
                    if f.has(0):
                        act.wait_ge(s.smax_ready, n + 1)
                        pr = probs(q, par)
                        for x in range(2):
                            m = act.activation(pr[:, x, k0:k0 + nk], sm[par][:, x, 0:nk], ACT.Exp,
                                               bias=nb[:, par, x:x + 1], scale=rn[:, q, 1, 2 * u + x:2 * u + x + 1],
                                               accum_out=den[:, par, x:x + 1])
                        m.then_inc(s.exp_done, 1)
                    bq, bu = (q, u - 1) if u else ((q - 1) % 4, 3)
                    if f.has(0 if u else -1):
                        if f.after(3, u):
                            act.wait_ge(s.pv_done, n - 2)
                        pt_evac(bq, bu, n)
                    c1, t1, _, _ = geometry((q + 1) % 4)
                    if u == 0 and f.has(1):
                        act.wait_ge(s.qT_ps, tb + Q + 2)
                        act.activation(qT[c1][:, :, t1 * P:(t1 + 1) * P], BT[:, :].rearrange("p (w t) -> p w t", w=4),
                                       ACT.Copy).then_inc(s.qT_ready, 1)
                    if u == 1 and f.has(1):
                        act.wait_ge(s.kT_ps, tb + Q + 2)
                        for x in range(2):
                            m = act.activation(kT[c1][64 * x:64 * x + 64, :, x, t1 * P:(t1 + 1) * P],
                                               BT[64 * x:64 * x + 64, :].rearrange("p (w t) -> p w t", w=4), ACT.Copy)
                        m.then_inc(s.kT_ready, 1)
                    if u == 3 and f.has(2):
                        cr, trr, _, _ = geometry((q + 2) % 4)
                        act.wait_ge(s.v_ps, tb + Q + 3)
                        act.activation(vv[cr][:, trr, :], BV[:, :], ACT.Copy).then_inc(s.v_ready, 1)
                    if u == 2 and f.has(3):
                        act.wait_ge(s.q_ps, tb + Q + 4)
                        if f.second(3):
                            act.wait_ge(s.ssq_raw, tb + Q + 3)
                        act.activation(sq[:, 0:INNER], BQ[:, :], ACT.Square).then_inc(s.sqq_done, 1)
                    if u == 3 and f.has(3):
                        act.wait_ge(s.k_ps, tb + Q + 4)
                        if f.second(3):
                            act.wait_ge(s.ssk_raw, tb + Q + 3)
                        act.activation(sq[:, INNER:], BK[:, :], ACT.Square).then_inc(s.sqk_done, 1)

            steps(act, step)
            phase_end(act, "act", ph)

        def lo_pool(pool, l, pb, ph):
            tb, qb = pb * NT, pb * NT * 4

            def step(i, q, f):
                Q = 4 * i + q
                r = Q + 2
                rq = (q + 2) % 4
                if f.has(2):
                    wait_apart(pool, s.rq_ab, tb + r + 1)
                    if f.second(2):
                        wait_apart(pool, s.qT_ps, tb + r)
                    pool.tensor_tensor(qr[:, :], rab[:, 0, :], rab[:, 1, :], ALU.add).then_inc(s.qr_ready, 1)
                    wait_apart(pool, s.ss_ready, tb + r + 1)
                    pool.tensor_tensor(rnp[:, :], ss[:, 1, :], mhalf[:, :], ALU.pow).then_inc(s.rn_self, 1)
                    wait_apart(pool, s.rn_self, tb + r + 1)
                    pool.tensor_scalar(rn[:, rq, 1, :], rnp[:, 0:8], QK_SCALE, 1.0, ALU.mult, ALU.mult)
                    pool.tensor_scalar(rn[:, rq, 2, :], rnp[:, 0:8], -QK_SCALE, 1.0, ALU.mult, ALU.mult)
                    pool.tensor_scalar(rn[:, rq, 0, :], rnp[:, 8:16], 1.0, 1.0, ALU.mult, ALU.mult)\
                        .then_inc(s.rn_ready, 1)
                    wait_apart(pool, s.rk_ab, tb + r + 1)
                    if f.second(2):
                        wait_apart(pool, s.kr_ready, tb + r)
                    pool.tensor_tensor(kadd[:, :], rab[:, 2, :], rab[:, 3, :], ALU.add).then_inc(s.kadd_ready, 1)
                    wait_apart(pool, s.kadd_ready, tb + r + 1)
                    if f.second(2):
                        wait_apart(pool, s.kT_ps, tb + r)
                    pool.tensor_tensor(heads(kr[:, :]), heads(kadd[:, :]),
                                       bc(rn[:, rq, 0, :].unsqueeze(2), [P, LH, LD]), ALU.mult)\
                        .then_inc(s.kr_ready, 1)

            steps(pool, step)
            phase_end(pool, "pool", ph)

        MH, MT, MG, MY, MX = B[0], B[1], (B[2], B[3], B[4]), B[5], B[6]

        def over_batches(eng, head, body, tail):
            head(0)
            body(0, True, True)
            with eng.Fori(1, NBATCH - 1) as b:
                body(b, False, True)
            body(NBATCH - 1, False, False)
            tail(NBATCH)

        def ff_pe(pe, l, pb, ph):
            hb = pb * NBATCH

            def shifted(b):
                if isinstance(b, int) and b == 0:
                    pass
                else:
                    pe.wait_ge(s.hn_ready, hb + b)
                h3 = MH[:, 0:SEQ].rearrange("p (t d) -> p t d", t=2)
                ub = U[:, bass.ts(b, 2), :]
                pe.matmul(h3[:, :, 0:64], ident[:, :], ub[:, :, 0:64], start=True, stop=True)
                pe.matmul(h3[:, :, 64:128], shift[:, 0, :], ub[:, :, 64:128], start=True, stop=False,
                          skip_group_check=True)
                pe.matmul(h3[:, 1, 64:128], shift[:, 1, :], ub[:, 0, 64:128], start=False, stop=True,
                          skip_group_check=True).then_inc(s.h_ps, 1)

            def turned(b):
                pe.wait_ge(s.hn_ready, hb + b + 1)
                for t in range(2):
                    m = pe.transpose(MT[:, t * P:(t + 1) * P], hn[:, t * P:(t + 1) * P], ident[:, :])
                m.then_inc(s.hnT_ps, 1)

            def x_turned(b):
                pe.wait_ge(s.x2_ready, hb + b)
                if not (isinstance(b, int) and b == 1):
                    pe.wait_ge(s.xT_done, hb + b - 1)
                for t in range(2):
                    m = pe.transpose(MX[:, t * P:(t + 1) * P], xs[:, t * P:(t + 1) * P], ident[:, :])
                m.then_inc(s.xT_ps, 1)

            def head(b):
                shifted(b)
                turned(b)

            def body(b, is_first, more):
                if more:
                    shifted(b + 1)
                pe.wait_ge(s.hT2_ready, hb + b + 1)
                for c, (h0, n) in enumerate(HCH):
                    if c == 0 and not is_first:
                        pe.wait_ge(s.act_ready, 3 * (hb + b))
                    for g in range(2):
                        m = pe.matmul(MG[c][0:n, g * SEQ:(g + 1) * SEQ], w1[:, g * HID + h0:g * HID + h0 + n], hT2[:, :],
                                      start=True, stop=True)
                    m.then_inc(s.up_ps, 1)
                if more:
                    turned(b + 1)
                if not is_first:
                    x_turned(b)
                pe.wait_ge(s.act_ready, 3 * (hb + b) + 3)
                for t in range(2):
                    for c, (h0, n) in enumerate(HCH):
                        m = pe.matmul(MY[:, t * P:(t + 1) * P], act_b[0:n, c, t * P:(t + 1) * P],
                                      w2[0:n, bass.ds(l, 1), c, :].rearrange("p o d -> p (o d)"),
                                      start=(c == 0), stop=(c == 2))
                m.then_inc(s.dn_ps, 1)

            pe.wait_ge(s.ld_w1, 16 * (pb + 1))
            over_batches(pe, head, body, x_turned)
            phase_end(pe, "pe", ph)

        def ff_dve(dve, l, pb, ph):
            hb = pb * NBATCH

            def stats(b):
                dve.wait_ge(s.h_ps, hb + b + 1)
                for t in range(2):
                    dve.bn_stats(st6[:, t, :], MH[:, t * P:(t + 1) * P]).then_inc(s.m_raw, 1)
                wait_apart(dve, s.m_raw, 2 * (hb + b) + 2)
                for t in range(2):
                    m = dve.bn_aggr(mv[:, t, :], st6[:, t, :])
                m.then_inc(s.m_stats, 1)

            def normed(b, is_first=False):
                dve.wait_ge(s.m_rs, hb + b + 1)
                if not is_first:
                    dve.wait_ge(s.hnT_ps, hb + b)
                for t in range(2):
                    m = dve.tensor_scalar(hn[:, t * P:(t + 1) * P], MH[:, t * P:(t + 1) * P], mv[:, t, 0:1],
                                          mrs[:, 1, t:t + 1], ALU.subtract, ALU.mult)
                m.then_inc(s.hn_ready, 1)

            def head(b):
                stats(b)
                normed(b, True)

            def body(b, is_first, more):
                if more:
                    stats(b + 1)
                for c, (h0, n) in enumerate(HCH):
                    dve.wait_ge(s.gelu_done, 3 * (hb + b) + c + 1)
                    if c == 0 and not is_first:
                        dve.wait_ge(s.dn_ps, hb + b)
                    row_a = V_B1 + c
                    ba = vec[0:n, bass.ds(l * 6 + row_a, 1)]
                    dve.scalar_tensor_tensor(act_b[0:n, c, 0:SEQ], MG[c][0:n, 0:SEQ], ba, gl[0:n, c, 0:SEQ],
                                             ALU.add, ALU.mult).then_inc(s.act_ready, 1)
                    if c == 0 and more:
                        normed(b + 1)
                dve.wait_ge(s.dn_ps, hb + b + 1)
                dve.wait_ge(s.x1b_ready, hb + b + 1)
                if not is_first:
                    dve.wait_ge(s.xT_ps, hb + b)
                    dve.wait_ge(s.x2_copied, hb + b)
                dve.tensor_tensor(xs[:, :], MY[:, 0:SEQ], x1b[:, :], ALU.add).then_inc(s.x2_ready, 1)

            over_batches(dve, head, body, lambda b: None)
            phase_end(dve, "dve", ph)

        def ff_act(act, l, pb, ph):
            hb = pb * NBATCH
            act.preload_act_table(ACT.Gelu)

            def head(b):
                wait_apart(act, s.hnT_ps, hb + b + 1)
                act.activation(hT2[:, :], MT[:, 0:SEQ], ACT.Identity, bias=vec[:, bass.ds(l + V_LB, 1)],
                               scale=vec[:, bass.ds(l + V_LG, 1)]).then_inc(s.hT2_ready, 1)

            def x_out(b):
                wait_apart(act, s.xT_ps, hb + b)
                act.activation(uT[:, bass.ts(b - 1, SEQ)], MX[:, 0:SEQ], ACT.Copy).then_inc(s.xT_done, 1)

            def body(b, is_first, more):
                for c, (h0, n) in enumerate(HCH):
                    wait_apart(act, s.up_ps, 3 * (hb + b) + c + 1)
                    act.activation(gl[0:n, c, 0:SEQ], MG[c][0:n, SEQ:2 * SEQ], ACT.Gelu,
                                   bias=vec[0:n, bass.ds(l * 6 + V_B1 + 3 + c, 1)]).then_inc(s.gelu_done, 1)
                if more:
                    head(b + 1)
                if not is_first:
                    x_out(b)

            over_batches(act, head, body, x_out)
            phase_end(act, "act", ph)

        def ff_pool(pool, l, pb, ph):
            hb = pb * NBATCH
            pool.wait_ge(s.ld_late, 16 * N_LATE)

            def head(b):
                wait_apart(pool, s.m_stats, hb + b + 1)
                pool.tensor_scalar(mrs[:, 0, :], mv[:, 0:2, 1], LN_EPS, 0.0, ALU.add, ALU.add).then_inc(s.m_var, 1)
                wait_apart(pool, s.m_var, hb + b + 1)
                pool.tensor_tensor(mrs[:, 1, :], mrs[:, 0, :], mhalf[:, 0:2], ALU.pow).then_inc(s.m_rs, 1)

            def body(b, is_first, more):
                if more:
                    head(b + 1)
                if not is_first:
                    wait_apart(pool, s.x2_ready, hb + b)
                pool.tensor_tensor(x1b[:, :].rearrange("p (t d) -> p t d", t=2), U[:, bass.ts(b, 2), :],
                                   bc(b2_row[:, bass.ds(l, 1), :], [P, 2, D]), ALU.add).then_inc(s.x1b_ready, 1)
                wait_apart(pool, s.x2_ready, hb + b + 1)
                wait_apart(pool, s.h_ps, hb + b + 1)
                pool.tensor_copy(U[:, bass.ts(b, 2), :], xs[:, :].rearrange("p (t d) -> p t d", t=2))\
                    .then_inc(s.x2_copied, 1)

            over_batches(pool, head, body, lambda b: None)
            phase_end(pool, "pool", ph)

        def ffn_sync(sp, site, ph0):
            with sp.Fori(0, DEPTH) as l:
                pb = l + site * DEPTH
                sp.wait_ge(s.ph_pe, ph0 + 2 * l)
                sp.dma_start(w1[:, :], a["L0_ffn_w1"][bass.ds(l, 1), :, :].rearrange("o k n -> (o k) n"))\
                    .then_inc(s.ld_w1, 16)

        def ffn(eng, name, site, ph0):
            parts = {"pe": (lo_pe, ff_pe), "act": (lo_act, ff_act), "dve": (lo_dve, ff_dve),
                     "pool": (lo_pool, ff_pool)}[name]
            with eng.Fori(0, DEPTH) as l:
                pb = l + site * DEPTH
                parts[0](eng, l, pb, ph0 + 1 + 2 * l)
                parts[1](eng, l, pb, ph0 + 2 + 2 * l)

        def ap_pe(pe, ph):
            pe.wait_ge(s.ld_late, 16 * N_LATE)
            for c in range(4):
                t = pe.transpose(B[3][:, c * P:(c + 1) * P], aw_rows[:, c, :], ident[:, :])
            t.then_inc(s.wt_ps, 1)
            pe.wait_ge(s.wt_ready, 2)
            for c in range(NCH):
                bq, bk, bv = B[4 * (c % 2):4 * (c % 2) + 3]
                if c > 1:
                    pe.wait_ge(s.aq_ready, c - 1)
                    pe.wait_ge(s.av_ready, c - 1)
                for k, bank in enumerate((bq, bk)):
                    m = pe.matmul(bank[:, :], awT[:, k, :], uT[:, c * CH:(c + 1) * CH], start=True, stop=True)
                m.then_inc(s.aq_ps, 1)
                for j in range(CT):
                    t = c * CT + j
                    m = pe.matmul(bv[:, j * P:(j + 1) * P], uT[:, t * P:(t + 1) * P], awT[:, 2, :],
                                  start=True, stop=True)
                m.then_inc(s.av_ps, 1)
            phase_end(pe, "pe", ph)

        def ap_act(act, ph):
            act.preload_act_table(ACT.Exp)
            for c in range(NCH):
                cs = slice(c * CH, (c + 1) * CH)
                act.wait_ge(s.aq_ps, c + 1)
                act.activation(qTa[:, cs], B[4 * (c % 2)][:, :], ACT.Identity, bias=vec[:, V_QKVB:V_QKVB + 1],
                               scale=AD ** -0.5)
                act.activation(kTa_hi[:, cs], B[4 * (c % 2) + 1][:, :], ACT.Identity,
                               bias=vec[:, V_QKVB + 1:V_QKVB + 2]).then_inc(s.aq_hi, 1)
            phase_end(act, "act", ph)

        def ap_dve(dve, ph):
            dve.wait_ge(s.ld_late, 16 * N_LATE)
            dve.wait_ge(s.wt_ps, 1)
            dve.tensor_copy(awT[:, :, :].rearrange("p c d -> p (c d)"), B[3][:, :]).then_inc(s.wt_ready, 1)
            dve.wait_ge(s.alpha_ready, 4)
            for c in range(NCH):
                for h in range(4 * c, 4 * c + 4):
                    dve.tensor_scalar(dbias[:, h, :, :], dist[:, :, :], alpha[:, h:h + 1], -1.0, ALU.mult, ALU.mult)
                cs = slice(c * CH, (c + 1) * CH)
                dve.wait_ge(s.aq_hi, c + 1)
                dve.scalar_tensor_tensor(kTa_lo[:, cs], B[4 * (c % 2) + 1][:, :], vec[:, V_QKVB + 1:V_QKVB + 2],
                                         kTa_hi[:, cs].bitcast(F32), ALU.add, ALU.subtract).then_inc(s.aq_ready, 1)
                dve.wait_ge(s.av_ps, c + 1)
                dve.tensor_tensor(va[:, c * CT:(c + 1) * CT, :], B[4 * (c % 2) + 2][:, :].rearrange("p (t d) -> p t d", t=CT),
                                  bc(bv_row[:, :].unsqueeze(1), [P, CT, D]), ALU.add).then_inc(s.av_ready, 1)
            phase_end(dve, "dve", ph)

        AS, AP_, AO, AY = (B[4], B[5]), (B[6], B[3]), B[7], B[2]

        def over_sequences(eng, body, tail):
            body(0, True, False)
            with eng.Fori(1, NBATCH - 1) as b:
                body(b, False, False)
            body(NBATCH - 1, False, True)
            tail(NBATCH)

        def aa_pe(pe, ph):
            def sim(b, h):
                n = b * AH + h
                pe.wait_ge(s.a_qm, n + 1)
                if not (isinstance(n, int) and n < 2):
                    pe.wait_ge(s.a_max, n - 1)
                ks = bass.ts(b, SEQ)
                for t in range(2):
                    parts = ((qm_hi, kTa_hi), (qm_hi, kTa_lo), (qm_lo, kTa_hi))
                    for x, (q_, k_) in enumerate(parts):
                        m = pe.matmul(AS[h % 2][:, t * SEQ:(t + 1) * SEQ], q_[h % 2][:, t * P:(t + 1) * P], k_[:, ks],
                                      start=(x == 0), stop=(x == 2))
                m.then_inc(s.a_sim, 1)

            def turn(b, h):
                n = b * AH + h
                pe.wait_ge(s.a_rd, 2 * n + 2)
                pe.wait_ge(s.a_prob, n + 1)
                if not (isinstance(n, int) and n < 2):
                    pe.wait_ge(s.a_Tready, n - 1)
                for j in range(2):
                    for t in range(2):
                        m = pe.transpose(AP_[h % 2][:, (2 * j + t) * P:(2 * j + t + 1) * P],
                                         pA[h % 2][:, t, j * P:(j + 1) * P], ident[:, :])
                m.then_inc(s.a_Tps, 1)

            def pv(b, h):
                n = b * AH + h
                pe.wait_ge(s.a_Tready, n + 1)
                if h == 0:
                    pe.wait_ge(s.vm_ready, b + 2)
                    if not (isinstance(b, int) and b == 0):
                        pe.wait_ge(s.a_o, b)
                for j in range(2):
                    m = pe.matmul(AO[:, 0:SEQ], vm[:, j, h, :], pT[h % 2][:, j * SEQ:(j + 1) * SEQ],
                                  start=(h == 0 and j == 0), stop=(h == AH - 1 and j == 1))
                m.then_inc(s.a_pv, 1)

            def out_proj(b):
                pe.wait_ge(s.a_o, b)
                if not (isinstance(b, int) and b == 1):
                    pe.wait_ge(s.a_out, b - 1)
                for t in range(2):
                    m = pe.matmul(AY[:, t * P:(t + 1) * P], oTa[:, t * P:(t + 1) * P], awT[:, 3, :],
                                  start=True, stop=True)
                m.then_inc(s.a_yps, 1)

            def body(b, is_first, is_last):
                for h in range(AH):
                    if h + 1 < AH:
                        sim(b, h + 1)
                    elif not is_last:
                        sim(b + 1, 0)
                    if h >= 1:
                        turn(b, h - 1)
                    elif not is_first:
                        turn(b - 1, AH - 1)
                    if h >= 2:
                        pv(b, h - 2)
                    elif not is_first:
                        pv(b - 1, AH - 2 + h)
                    if h == 3 and not is_first:
                        out_proj(b)

            def tail(b):
                turn(b - 1, AH - 1)
                pv(b - 1, AH - 2)
                pv(b - 1, AH - 1)
                out_proj(b)

            sim(0, 0)
            over_sequences(pe, body, tail)
            phase_end(pe, "pe", ph)

        def aa_dve(dve, ph):
            def masked(b, h):
                dve.wait_ge(s.a_qh, b * AH + h + 1)
                dve.scalar_tensor_tensor(qm_lo[h % 2][:, :], qTa[:, bass.ts(b, SEQ)], headmask[:, h:h + 1],
                                         qm_hi[h % 2][:, :].bitcast(F32), ALU.mult, ALU.subtract).then_inc(s.a_qm, 1)

            def inverted(n, par):
                dve.wait_ge(s.a_exp, n)
                dve.reciprocal(rden[:, par, :], den[:, par, :]).then_inc(s.a_rd, 1)

            def scaled(n, par):
                dve.wait_ge(s.a_rd, 2 * n - 1)
                dve.tensor_scalar(pA[par][:, 0, :], pA[par][:, 0, :], rden[:, par, 0:1], None, ALU.mult)\
                    .then_inc(s.a_rd, 1)

            def result(b):
                dve.wait_ge(s.a_yps, b)
                dve.tensor_tensor(U[:, bass.ts(b - 1, 2), :], AY[:, 0:SEQ].rearrange("p (t d) -> p t d", t=2),
                                  bc(ob_row[:, :].unsqueeze(1), [P, 2, D]), ALU.add).then_inc(s.a_out, 1)

            def body(b, is_first, is_last):
                for h in range(AH):
                    n = b * AH + h
                    par = h % 2
                    wait_apart(dve, s.a_sim, n + 1)
                    for t in range(2):
                        m = dve.tensor_tensor_reduce(sm[par][:, t, :], AS[par][:, t * SEQ:(t + 1) * SEQ],
                                                     dbias[:, h, t, :], 1.0, -3e38, ALU.add, ALU.max,
                                                     mx[:, par, t:t + 1])
                    m.then_inc(s.a_mx, 1)
                    if not (is_first and h == 0):
                        inverted(n, 1 - par)
                    dve.wait_ge(s.a_mx, n + 1)
                    dve.tensor_scalar(nb[:, par, :], mx[:, par, :], -1.0, None, ALU.mult).then_inc(s.a_max, 1)
                    if not (is_first and h == 0):
                        scaled(n, 1 - par)
                    if h + 2 < AH:
                        masked(b, h + 2)
                    elif not is_last:
                        masked(b + 1, h + 2 - AH)
                    if h == 5 and not is_first:
                        result(b)

            def tail(b):
                inverted(AH * b, 1)
                scaled(AH * b, 1)
                result(b)

            masked(0, 0)
            masked(0, 1)
            over_sequences(dve, body, tail)
            phase_end(dve, "dve", ph)

        def aa_act(act, ph):
            act.preload_act_table(ACT.Exp)

            def evac(n, par, back_ok):
                act.wait_ge(s.a_Tps, n)
                if back_ok:
                    act.wait_ge(s.a_pv, n - 2)
                act.activation(pT[par][:, :], AP_[par][:, :], ACT.Copy).then_inc(s.a_Tready, 1)

            def masked(b, h):
                act.activation(qm_hi[h % 2][:, :], qTa[:, bass.ts(b, SEQ)], ACT.Copy, scale=headmask[:, h:h + 1])\
                    .then_inc(s.a_qh, 1)

            def outs(b):
                act.wait_ge(s.a_pv, AH * b)
                if not (isinstance(b, int) and b == 1):
                    act.wait_ge(s.a_yps, b - 1)
                act.activation(oTa[:, :], AO[:, 0:SEQ], ACT.Copy).then_inc(s.a_o, 1)

            def body(b, is_first, is_last):
                for h in range(AH):
                    n = b * AH + h
                    par = h % 2
                    wait_apart(act, s.a_sim, n + 1)
                    if h + 2 < AH:
                        masked(b, h + 2)
                    elif not is_last:
                        masked(b + 1, h + 2 - AH)
                    act.wait_ge(s.a_max, n + 1)
                    for t in range(2):
                        m = act.activation(pA[par][:, t, :], sm[par][:, t, :], ACT.Exp, bias=nb[:, par, t:t + 1],
                                           accum_out=den[:, par, t:t + 1])
                    m.then_inc(s.a_exp, 1)
                    if not (is_first and h == 0):
                        evac(n, 1 - par, not (is_first and h < 3))
                    if h == 1 and not is_first:
                        outs(b)

            def tail(b):
                evac(AH * b, 1, True)
                outs(b)

            masked(0, 0)
            masked(0, 1)
            over_sequences(act, body, tail)
            phase_end(act, "act", ph)

        def aa_pool(pool, ph):
            pool.wait_ge(s.vm_ready, 1)

            def spread(b):
                for t in range(2):
                    blocks = bass.AP(tensor=arena, offset=VM_AT + t * AH * P, ap=[[ARENA, P], [P + AD, AH], [1, AD]])
                    m = pool.tensor_copy(blocks, va[:, bass.ds(b * 2 + t, 1), :]
                                         .rearrange("p o (h d) -> p (o h) d", h=AH))
                m.then_inc(s.vm_ready, 1)

            def scaled(b, h):
                wait_apart(pool, s.a_rd, 2 * (b * AH + h) + 1)
                v = pA[h % 2][:, 1, :]
                pool.tensor_scalar(v, v, rden[:, h % 2, 1:2], 1.0, ALU.mult, ALU.mult).then_inc(s.a_prob, 1)

            spread(0)
            for h in range(AH):
                scaled(0, h)
            with pool.Fori(1, NBATCH) as b:
                scaled(b, 0)
                scaled(b, 1)
                wait_apart(pool, s.a_pv, AH * b)
                spread(b)
                for h in range(2, AH):
                    scaled(b, h)
            phase_end(pool, "pool", ph)

        EVERY = 2 * NT // NCH

        def pool_has(m):
            return m % 5 in (0, 2)

        def pool_done(m):
            return sum(pool_has(x) for x in range(m))

        def mr_pe(pe, k0, ph):
            for t in range(NT):
                m = pe.matmul(B[0][:, t * E:(t + 1) * E], uT[:, t * P:(t + 1) * P], wr[:, :], start=True, stop=True)
            m.then_inc(s.r_lg, 1)

            def up(c, g, wait):
                if wait:
                    pe.wait_ge(s.s_act, 2 * (k0 * NCH + c) + g - 1)
                for half in range(2):
                    m = pe.matmul(B[1 + 2 * g + half][:, :], ws1[:, (2 * half + g) * P:(2 * half + g + 1) * P],
                                  uT[:, bass.ts(c, CH)], start=True, stop=True)
                m.then_inc(s.s_up, 1)

            def down(c):
                k = c + k0 * NCH
                pe.wait_ge(s.r_wst, k + 1)
                for j in range(CT):
                    m = pe.transpose(B[6][0:E, j * P:(j + 1) * P], wst[:, j, :], ident[:, :])
                m.then_inc(s.r_wps, 1)
                pe.wait_ge(s.s_act, 2 * k + 2)
                pe.wait_ge(s.s_tmp, 2 * k + 1)
                for j in range(CT):
                    js = slice(j * P, (j + 1) * P)
                    pe.matmul(B[5][:, js], act_b[:, 0, js], ws2[:, 0, :], start=True, stop=False)
                    pe.matmul(B[5][:, js], act_b[:, 1, js], ws2[:, 1, :], start=False, stop=False)
                    if j == 0:
                        pe.wait_ge(s.r_wT, k + 1)
                    m = pe.matmul(B[5][:, js], wT[:, js], be2[:, :], start=False, stop=True)
                m.then_inc(s.s_dn, 1)

            for g in range(2):
                up(0, g, False)
            pe.wait_ge(s.r_both, k0 + 1)
            flat_both = both.rearrange("p t e -> p (t e)")
            pe.matmul(B[7][:, 0:NT * E], strict[:, :], flat_both, start=True, stop=True)
            pe.matmul(B[7][:, 256:256 + NT * E], ones[:, :], flat_both, start=True, stop=True).then_inc(s.r_cum, 1)
            for m in range(2 * NT):
                if pool_has(m):
                    pe.wait_ge(s.inv_a, k0 * pool_done(2 * NT) + pool_done(m + 1))
                pe.wait_ge(s.inv_b, k0 * 2 * NT + m + 1)
                pe.matmul(B[0][:, 256:256 + NXT], ringA[:, m % RING, :], ringB[:, m % RING, :],
                          start=(m == 0), stop=(m == 2 * NT - 1)).then_inc(s.inv_ps, 1)
                if m % EVERY == EVERY - 1:
                    c = m // EVERY
                    if c + 1 < NCH:
                        for g in range(2):
                            up(c + 1, g, True)
                        down(c)
            down(NCH - 1)
            phase_end(pe, "pe", ph)

        def mr_act(act, k0, ph):
            act.preload_act_table(ACT.Gelu)
            with act.Fori(0, NCH) as c:
                k = c + k0 * NCH
                for g in range(2):
                    wait_apart(act, s.s_up, 2 * k + g + 1)
                    act.activation(gl[:, g, :], B[2 + 2 * g][:, :], ACT.Gelu, bias=vec[:, V_BS1 + 2 + g:V_BS1 + 3 + g])\
                        .then_inc(s.s_gelu, 1)
                wait_apart(act, s.r_wps, k + 1)
                act.activation(wT[:, :], B[6][0:E, :], ACT.Copy).then_inc(s.r_wT, 1)
            phase_end(act, "act", ph)

        R_PLACES = 33
        R_STEPS = 47

        def mr_dve(dve, k0, coef, ph):
            taken = [k0 * R_STEPS]

            def done_(m):
                m.then_inc(s.r_self, 1)
                taken[0] += 1

            def own():
                dve.wait_ge(s.r_self, taken[0])

            def tiles_bc(v):
                return bc(v.unsqueeze(1), [P, NT, E])

            def experts_bc(v):
                return bc(v.unsqueeze(2), [P, NT, E])

            def prefix(bufs, n, view):
                src, others = bufs[0], [bufs[1], bufs[2]]
                step, m = 1, 0
                while step < n:
                    dst = others[m % 2]
                    own()
                    dve.tensor_tensor(view(dst, step, n), view(src, step, n), view(src, 0, n - step), ALU.add)
                    done_(dve.tensor_copy(view(dst, 0, step), view(src, 0, step)))
                    src, step, m = dst, 2 * step, m + 1
                return src

            dve.wait_ge(s.r_lg, k0 + 1)
            done_(dve.tensor_tensor(lg, B[0][:, 0:NT * E].rearrange("p (t e) -> p t e", e=E), tiles_bc(br_row[:, :]),
                                    ALU.add))
            own()
            done_(dve.tensor_scalar(lg, lg, 1.0 / TAU, None, ALU.mult))
            own()
            for t in range(NT):
                m = dve.max(top[:, t, :], lg[:, t, :])
            done_(m)
            own()
            dve.tensor_tensor(rw[:, :, 0], top[:, :, 1], top[:, :, 0], ALU.subtract).then_inc(s.r_m12, 1)
            for t in range(NT):
                m = dve.max_index(idx[:, t, :], top[:, t, :], lg[:, t, :])
            done_(m)
            own()
            done_(dve.tensor_copy(idf[:, :, :], idx[:, :, 0:2]))
            own()
            for n in range(2):
                m = dve.tensor_tensor(oh[n], tiles_bc(iota[:, 0:E]), experts_bc(idf[:, :, n]), ALU.is_equal)
            done_(m)
            own()
            dve.tensor_tensor(both, oh[0], oh[1], ALU.add).then_inc(s.r_both, 1)
            dve.wait_ge(s.r_e, k0 + 1)
            done_(dve.tensor_scalar(rw[:, :, 0], rw[:, :, 1], 1.0, None, ALU.add))
            own()
            done_(dve.reciprocal(rw[:, :, 2], rw[:, :, 0]))
            own()
            done_(dve.tensor_tensor(rw[:, :, 3], rw[:, :, 1], rw[:, :, 2], ALU.mult))
            own()
            dve.wait_ge(s.r_cum, k0 + 1)
            done_(dve.tensor_copy(tot, B[7][:, 256:256 + NT * E].rearrange("p (t e) -> p t e", e=E)))
            incl = prefix([tot, pre0, pre1], NT, lambda v, a_, b_: v[:, a_:b_, :])
            own()
            done_(dve.tensor_tensor(need, bc(incl[:, NT - 1, :].unsqueeze(2), [P, E, NT]),
                                    bc(iota[:, E + NXT:E + NXT + NT].unsqueeze(1), [P, E, NT]), ALU.is_gt))
            own()
            done_(dve.tensor_reduce(ntile[:, :], need, AX_X, ALU.add))
            ends = prefix([ntile[:, :], etile[:, 0, :], etile[:, 1, :]], E, lambda v, a_, b_: v[:, a_:b_])
            own()
            done_(dve.tensor_tensor(ecmp[:, :, :], bc(ends.unsqueeze(1), [P, NXT, E]),
                                    bc(iota[:, E:E + NXT].unsqueeze(2), [P, NXT, E]), ALU.is_le))
            done_(dve.tensor_tensor(place, incl, tot, ALU.subtract))
            own()
            done_(dve.tensor_tensor(place, place, B[7][:, 0:NT * E].rearrange("p (t e) -> p t e", e=E), ALU.add))
            done_(dve.tensor_tensor(ntile[:, :], ends, ntile[:, :], ALU.subtract))
            own()
            done_(dve.scalar_tensor_tensor(place, tiles_bc(ntile[:, :]), float(P), place, ALU.mult, ALU.add))
            for n in range(2):
                own()
                done_(dve.tensor_tensor(prod, oh[n], place, ALU.mult))
                own()
                done_(dve.tensor_reduce(posf[:, n, :], prod, AX_X, ALU.add))
            own()
            done_(dve.tensor_copy(pos[:, 0, :, :], posf[:, :, :]))
            own()
            done_(dve.tensor_scalar(pos[:, 1, :, :], pos[:, 0, :, :], 7, None, ALU.logical_shift_right))
            own()
            done_(dve.tensor_copy(posh[:, 0, :, :], pos[:, 1, :, :]))
            own()
            done_(dve.scalar_tensor_tensor(posh[:, 1, :, :], posh[:, 0, :, :], float(-P), posf[:, :, :],
                                           ALU.mult, ALU.add))
            own()
            assert taken[0] == k0 * R_STEPS + R_PLACES, taken
            done_(dve.tensor_reduce(tef[:, 0, :], ecmp[:, :, :], AX_X, ALU.add))
            own()
            done_(dve.tensor_scalar(tef[:, 1, :], tef[:, 0, :], float(E - 1), None, ALU.min))
            own()
            dve.tensor_copy(te[:, :], tef[:, 1, :]).then_inc(s.r_te, 1)
            done_(dve.tensor_tensor(wtmp, oh[0], experts_bc(rw[:, :, 2]), ALU.mult))
            done_(dve.tensor_tensor(wts[:, :, :], oh[1], experts_bc(rw[:, :, 3]), ALU.mult))
            own()
            done_(dve.tensor_tensor(wts[:, :, :], wts[:, :, :], wtmp, ALU.add))
            for n in range(2):
                m = dve.tensor_scalar(wc[:, n, :], rw[:, :, 2 + n], coef, None, ALU.mult)
            done_(m)
            own()

            def acts(c):
                k = c + k0 * NCH
                for g in range(2):
                    dve.wait_ge(s.s_gelu, 2 * k + g + 1)
                    if not (isinstance(c, int) and c == 0 and k0 == 0) and g == 0:
                        dve.wait_ge(s.s_dn, k)
                    dve.scalar_tensor_tensor(act_b[:, g, :], B[1 + 2 * g][:, :], vec[:, V_BS1 + g:V_BS1 + g + 1],
                                             gl[:, g, :], ALU.add, ALU.mult).then_inc(s.s_act, 1)

            def weights(c):
                k = c + k0 * NCH
                if not (isinstance(c, int) and c == 0 and k0 == 0):
                    dve.wait_ge(s.r_wps, k)
                dve.tensor_copy(wst[:, :, :], wts[:, bass.ts(c, CT), :]).then_inc(s.r_wst, 1)

            def result(c):
                k = c + k0 * NCH
                dve.wait_ge(s.s_dn, k + 1)
                dve.wait_ge(s.s_tmp, 2 * k + 2)
                xc = X[:, bass.ts(c, CT), :]
                dve.tensor_tensor(stg[:, :, :], B[5][:, :].rearrange("p (t d) -> p t d", t=CT),
                                  bc(bs2_row[:, :].unsqueeze(1), [P, CT, D]), ALU.add).then_inc(s.s_tmp, 1)
                dve.wait_ge(s.s_tmp, 2 * k + 3)
                dve.scalar_tensor_tensor(xc, stg[:, :, :], coef, xc, ALU.mult, ALU.add).then_inc(s.s_tmp, 1)

            if not k0:
                dve.sem_inc(s.s_tmp, 2)
            for m in range(2 * NT):
                n, t = m // NT, m % NT
                if m >= RING:
                    dve.wait_ge(s.inv_ps, k0 * 2 * NT + m + 1 - RING)
                if not pool_has(m):
                    dve.tensor_scalar(ringA[:, m % RING, :], iota[:, E + NXT + NT:], posh[:, 1, n, t:t + 1], None,
                                      ALU.is_equal)
                dve.tensor_scalar(ringB[:, m % RING, :], iota[:, E:E + NXT], posh[:, 0, n, t:t + 1],
                                  code[:, n, t:t + 1], ALU.is_equal, ALU.mult).then_inc(s.inv_b, 1)
                if m % EVERY == EVERY - 1:
                    c = m // EVERY
                    weights(c)
                    acts(c)
                    if c:
                        result(c - 1)
            dve.wait_ge(s.inv_ps, (k0 + 1) * 2 * NT)
            done_(dve.tensor_copy(inv[:, 0, :], B[0][:, 256:256 + NXT]))
            own()
            done_(dve.scalar_tensor_tensor(inv[:, 1, :], inv[:, 0, :], -1.0, inv[:, 0, :], ALU.mult, ALU.max))
            done_(dve.tensor_scalar(inv[:, 2, :], inv[:, 0, :], 0.0, None, ALU.is_equal))
            done_(dve.tensor_scalar(inv[:, 4, :], inv[:, 0, :], 0.0, float(NT * P), ALU.is_lt, ALU.mult))
            own()
            done_(dve.tensor_scalar(inv[:, 3, :], inv[:, 1, :], -1.0, 0.0, ALU.add, ALU.max))
            done_(dve.tensor_tensor(inv[:, 2, :], inv[:, 2, :], slot[:, :], ALU.mult))
            own()
            done_(dve.tensor_tensor(inv[:, 4, :], inv[:, 4, :], inv[:, 3, :], ALU.add))
            own()
            done_(dve.tensor_tensor(inv[:, 4, :], inv[:, 4, :], inv[:, 2, :], ALU.add))
            own()
            dve.tensor_copy(inv_u[:, 0, :], inv[:, 3, :])
            dve.tensor_copy(inv_u[:, 1, :], inv[:, 4, :]).then_inc(s.r_pos, 1)
            assert taken[0] == (k0 + 1) * R_STEPS, taken
            result(NCH - 1)
            phase_end(dve, "dve", ph)

        def gather(pool, k0, n):
            pool.indirect_dma_start(xg[:, n % 4, :], None, u_rows[:, :],
                                    bass.IndirectOffsetOnAxis(ap=inv_u[:, 0, n:n + 1], axis=0))\
                .then_inc((s.ld_x0, s.ld_x1)[n % 2], 16)

        def mr_pool(pool, k0, ph):
            pool.wait_ge(s.r_m12, k0 + 1)
            pool.tensor_tensor(rw[:, :, 1], ebase[:, :], rw[:, :, 0], ALU.pow).then_inc(s.r_e, 1)
            pool.wait_ge(s.r_self, k0 * R_STEPS + R_PLACES)
            for m in filter(pool_has, range(2 * NT)):
                if m >= RING:
                    pool.wait_ge(s.inv_ps, k0 * 2 * NT + m + 1 - RING)
                pool.tensor_scalar(ringA[:, m % RING, :], iota[:, E + NXT + NT:], posh[:, 1, m // NT, m % NT:m % NT + 1],
                                   1.0, ALU.is_equal, ALU.mult).then_inc(s.inv_a, 1)
            pool.wait_ge(s.r_pos, k0 + 1)
            pool.wait_ge(s.u_stored, 16 * (k0 + 1))
            for n in range(2):
                gather(pool, k0, n)
            phase_end(pool, "pool", ph)

        XIN, XUP, XTA, XY = B[0], ((B[1], B[2]), (B[3], B[4])), B[5], B[6]

        def over_tiles(eng, step):
            for n in (-2, -1):
                step(-1, n + 4, lambda d, n=n: 0 <= n + d < NXT)
            for q in range(4):
                step(0, q, lambda d, n=q: 0 <= n + d < NXT)
            with eng.Fori(1, NXG - 1) as i:
                for q in range(4):
                    step(i, q, lambda d: True)
            for q in range(4):
                step(NXG - 1, q, lambda d, n=NXT - 4 + q: 0 <= n + d < NXT)
            step(NXG, 0, lambda d: NXT + d < NXT)

        def me_pe(pe, k0, ph):
            base = k0 * NXT

            def expert(n):
                return pe.value_load(te[0:1, bass.ds(n, 1)], min_val=0, max_val=E - 1)

            def step(i, q, has):
                n = 4 * i + q
                if has(1):
                    e = expert(n + 1)
                    pe.wait_ge(s.x_T, base + n + 2)
                    if has(-1) or k0:
                        pe.wait_ge(s.x_ab, base + n)
                    for half, sem in ((1, s.x_up_g), (0, s.x_up_a)):
                        pe.matmul(XUP[(q + 1) % 2][half][:, 0:HR], xT[(q + 1) % 2],
                                  we1[:, bass.ds(e * (2 * HR) + half * HR, HR)], start=True, stop=True).then_inc(sem, 1)
                if has(2):
                    q2 = (q + 2) % 4
                    i2 = i + (q + 2) // 4
                    pe.wait_ge((s.ld_x0, s.ld_x1)[q2 % 2], 16 * (NXT // 2 * k0 + 2 * i2 + q2 // 2 + 1))
                    pe.transpose(XIN[:, 0:P], xg[:, q2, :], ident[:, :]).then_inc(s.x_ps, 1)
                if has(-1):
                    e = expert(n - 1)
                    pe.wait_ge(s.x_actT, base + n)
                    if has(-2) or k0:
                        pe.wait_ge(s.x_y, base + n - 1)
                    for j in range(3):
                        m = pe.matmul(XY[:, 0:D], xactT[(q + 1) % 2][:, j * P:(j + 1) * P],
                                      we2[:, bass.ds(e * HR + j * D, D)], start=(j == 0), stop=(j == 2))
                    m.then_inc(s.x_dn, 1)
                if has(0):
                    pe.wait_ge(s.x_act, base + n + 1)
                    for j in range(3):
                        m = pe.transpose(XTA[:, j * P:(j + 1) * P], xact[q % 2][:, j * P:(j + 1) * P], ident[:, :])
                    m.then_inc(s.x_Tps, 1)

            pe.wait_ge(s.ld_ew, 16 * N_EW)
            pe.wait_ge(s.r_te, k0 + 1)
            over_tiles(pe, step)
            phase_end(pe, "pe", ph)

        def me_act(act, k0, ph):
            base = k0 * NXT

            def step(i, q, has):
                n = 4 * i + q
                if has(1):
                    act.wait_ge(s.x_gb, base + n + 2)
                    act.activation(xgelu[(q + 1) % 2], xgate[(q + 1) % 2], ACT.Gelu).then_inc(s.x_gl, 1)
                if has(2):
                    act.wait_ge(s.x_ps, base + n + 3)
                    if has(0):
                        act.wait_ge(s.x_up_a, base + n + 1)
                    act.activation(xT[q % 2], XIN[:, 0:P], ACT.Copy).then_inc(s.x_T, 1)
                if has(-1):
                    q1 = (q - 1) % 4
                    i1 = i if q else i - 1
                    act.wait_ge(s.x_dn, base + n)
                    if not (isinstance(i1, int) and i1 + k0 == 0):
                        act.wait_ge((s.st_y0, s.st_y1, s.st_y2, s.st_y3)[q1], 16 * (NXG * k0 + i1))
                    act.activation(yb[:, q1, :], XY[:, 0:D], ACT.Copy).then_inc(s.x_y, 1)
                if has(0):
                    act.wait_ge(s.x_Tps, base + n + 1)
                    if has(-2):
                        act.wait_ge(s.x_dn, base + n - 1)
                    act.activation(xactT[q % 2], XTA[:, 0:HR], ACT.Copy).then_inc(s.x_actT, 1)

            over_tiles(act, step)
            phase_end(act, "act", ph)

        def me_dve(dve, k0, ph):
            base = k0 * NXT

            def step(i, q, has):
                n = 4 * i + q
                par = (q + 1) % 2
                if has(1):
                    e = dve.value_load(te[0:1, bass.ds(n + 1, 1)], min_val=0, max_val=E - 1)
                    dve.wait_ge(s.x_up_g, base + n + 2)
                    dve.tensor_tensor(xgate[par], XUP[par][1][:, 0:HR], be1_row[:, bass.ds(e * (2 * HR) + HR, HR)],
                                      ALU.add).then_inc(s.x_gb, 1)
                    dve.wait_ge(s.x_up_a, base + n + 2)
                    dve.tensor_tensor(xa[par], XUP[par][0][:, 0:HR], be1_row[:, bass.ds(e * (2 * HR), HR)],
                                      ALU.add).then_inc(s.x_ab, 1)
                    dve.wait_ge(s.x_gl, base + n + 2)
                    dve.wait_ge(s.x_ab, base + n + 2)
                    if has(-1):
                        dve.wait_ge(s.x_Tps, base + n)
                    dve.tensor_tensor(xact[par], xa[par], xgelu[par], ALU.mult).then_inc(s.x_act, 1)

            over_tiles(dve, step)
            phase_end(dve, "dve", ph)

        def add_experts(dve, k0, c):
            dve.wait_ge((s.gat0, s.gat1)[c // 2], 16 * 2 * (k0 + 1))
            for t in range(c * CT, (c + 1) * CT):
                for n in range(2):
                    if n:
                        dve.wait_ge(s.x_sum, 2 * (k0 * NT + t) + 1)
                    src = (U[:, t, :], uT[:, t * P:(t + 1) * P])[n]
                    dve.scalar_tensor_tensor(X[:, t, :], src, wc[:, n, t:t + 1], X[:, t, :], ALU.mult, ALU.add)\
                        .then_inc(s.x_sum, 1)

        def me_pool(pool, k0, ph):
            base, lag = k0 * NXT, 6
            for n in range(2, NXT + lag):
                if n < NXT:
                    pool.wait_ge(s.x_ps, base + n - 1)
                    gather(pool, k0, n)
                m = n - lag
                if m >= 0:
                    pool.wait_ge(s.x_y, base + m + 1)
                    pool.indirect_dma_start(y_rows[:, :], bass.IndirectOffsetOnAxis(ap=inv_u[:, 1, m:m + 1], axis=0),
                                            yb[:, m % 4, :], None)\
                        .then_inc((s.st_y0, s.st_y1, s.st_y2, s.st_y3)[m % 4], 16)
            phase_end(pool, "pool", ph)

        N_EW = 9

        def me_sync(sp, k0):
            if not k0:
                for sem in (s.ph_pe, s.ph_act, s.ph_dve, s.ph_pool):
                    sp.wait_ge(sem, 14)
                for n in range(3):
                    e0, e1 = 4 * n, 4 * n + 4
                    sp.dma_start(we1[:, e0 * 768:e1 * 768].rearrange("k (e n) -> k e n", e=4),
                                 a["L1_ffn_We1"][e0:e1].rearrange("e k n -> k e n")).then_inc(s.ld_ew, 16)
                    sp.dma_start(we2[:, e0 * HR:e1 * HR].rearrange("k (c n) -> k c n", n=D),
                                 a["L1_ffn_We2"][e0:e1].rearrange("e (c k) n -> k (e c) n", k=P)).then_inc(s.ld_ew, 16)
                    sp.dma_start(be1_row[:, e0 * 2 * HR:e1 * 2 * HR],
                                 a["L1_ffn_be1"][e0:e1].rearrange("(o e) n -> o (e n)", o=1)
                                 .broadcast_to([P, 8 * HR])).then_inc(s.ld_ew, 16)

            sp.wait_ge(s.ph_dve, (15, 20)[k0])
            sp.dma_start(u_rows.rearrange("(t p) d -> p t d", p=P), U[:, :, :]).then_inc(s.u_stored, 16)
            for sem in (s.st_y0, s.st_y1, s.st_y2, s.st_y3):
                sp.wait_ge(sem, 16 * NXG * (k0 + 1))
            half = NT // 2
            for h in range(2):
                for n in range(2):
                    dst = (U[:, :, :], uT[:, :].rearrange("p (t d) -> p t d", d=D))[n][:, h * half:(h + 1) * half, :]
                    r0 = (n * NT + h * half) * P
                    sp.dma_start(dst, y_rows[r0:r0 + half * P, :].rearrange("(t p) d -> p t d", p=P))\
                        .then_inc((s.gat0, s.gat1)[h], 16)

        def la_pe(pe, ph):
            def proj(c):
                pe.wait_ge(s.n_xn, c + 1)
                if c:
                    pe.wait_ge(s.n_feat, 2 * c)
                    pe.wait_ge(s.n_g, c)
                for k, w in ((0, nqkv[:, 0:D]), (2, ngate[:, :]), (1, nqkv[:, D:2 * D])):
                    pe.matmul(B[k][:, :], w, xn[:, :], start=True, stop=True).then_inc(s.n_proj, 1)
                if c:
                    pe.wait_ge(s.n_v, c)
                for j in range(CT):
                    m = pe.matmul(B[3][:, j * P:(j + 1) * P], xn[:, j * P:(j + 1) * P], nqkv[:, 2 * D:3 * D],
                                  start=True, stop=True)
                m.then_inc(s.n_proj, 1)

            proj(0)
            for c in range(NCH):
                q_, k_, v_ = qf[c % 2], kf[c % 2], vA[c % 2]
                pe.wait_ge(s.n_feat, 2 * c + 2)
                if c:
                    pe.wait_ge(s.n_am, 2 * c)
                for b in range(2):
                    q0 = b * SEQ
                    pe.matmul(B[4 + b][:, 0:SEQ], k_[:, q0:q0 + P], q_[:, q0:q0 + SEQ], start=True, stop=True)
                    pe.matmul(B[4 + b][:, SEQ:384], k_[:, q0 + P:q0 + SEQ], q_[:, q0 + P:q0 + SEQ],
                              start=True, stop=True).then_inc(s.n_att, 1)
                if c + 1 < NCH:
                    proj(c + 1)
                if c:
                    pe.wait_ge(s.n_out, c)
                for b in range(2):
                    pe.wait_ge(s.n_am, 2 * c + b + 1)
                    if b == 0:
                        pe.wait_ge(s.n_v, c + 1)
                    w = D + 1
                    pe.matmul(B[6 + b][:, 0:w], am[b][:, 0:P], v_[:, 2 * b, :], start=True, stop=True)
                    pe.matmul(B[6 + b][:, w:2 * w], am[b][:, P:SEQ], v_[:, 2 * b, :], start=True, stop=False)
                    pe.matmul(B[6 + b][:, w:2 * w], am[b][:, SEQ:384], v_[:, 2 * b + 1, :], start=False, stop=True)\
                        .then_inc(s.n_num, 1)
                pe.wait_ge(s.n_o, c + 1)
                for j in range(CT):
                    m = pe.transpose(B[7][:, j * P:(j + 1) * P], osb[:, j, :], ident[:, :])
                m.then_inc(s.n_oT_ps, 1)
                pe.wait_ge(s.n_oT, c + 1)
                for j in range(CT):
                    m = pe.matmul(B[6][:, j * P:(j + 1) * P], noT[:, j * P:(j + 1) * P], nproj[:, :],
                                  start=True, stop=True)
                m.then_inc(s.n_yps, 1)
            phase_end(pe, "pe", ph)

        def la_act(act, ph):
            act.preload_act_table(ACT.Exp)

            def normed(c):
                if c:
                    act.wait_ge(s.n_proj, 4 * c)
                act.activation(xn[:, :], uT[:, c * CH:(c + 1) * CH], ACT.Identity, bias=vec[:, V_LNB:V_LNB + 1],
                               scale=vec[:, V_LNG:V_LNG + 1]).then_inc(s.n_xn, 1)

            def exps(c):
                act.wait_ge(s.n_min, 2 * c + 1)
                act.activation(z0[:, :], z0[:, :], ACT.Exp).then_inc(s.n_exp, 1)
                act.wait_ge(s.n_g, c + 1)
                act.activation(z2[:, :], z2[:, :], ACT.Exp, scale=-1.0).then_inc(s.n_gexp, 1)
                act.wait_ge(s.n_min, 2 * c + 2)
                act.activation(z1[:, :], z1[:, :], ACT.Exp).then_inc(s.n_exp, 1)
                if c + 1 < NCH:
                    normed(c + 1)

            normed(0)
            exps(0)
            for c in range(NCH):
                if c + 1 < NCH:
                    exps(c + 1)
                act.wait_ge(s.n_oT_ps, c + 1)
                if c:
                    act.wait_ge(s.n_yps, c)
                act.activation(noT[:, :], B[7][:, :], ACT.Copy).then_inc(s.n_oT, 1)
            phase_end(act, "act", ph)

        def la_dve(dve, ph):
            bq, bk = (vec[:, V_LQKVB + k:V_LQKVB + k + 1] for k in range(2))

            def features_first(c):
                q_ = qf[c % 2]
                dve.wait_ge(s.n_proj, 4 * c + 1)
                if c:
                    dve.wait_ge(s.n_feat, 2 * c)
                if c > 1:
                    dve.wait_ge(s.n_att, 2 * c - 2)
                dve.tensor_scalar(z0[:, :], B[0][:, :], bq, 0.0, ALU.add, ALU.min).then_inc(s.n_min, 1)
                dve.tensor_scalar(q_[:, :], B[0][:, :], bq, 0.0, ALU.add, ALU.max).then_inc(s.n_gd, 1)
                dve.wait_ge(s.n_proj, 4 * c + 2)
                dve.tensor_scalar(z2[:, :], B[2][:, :], vec[:, V_LGATE:V_LGATE + 1], -80.0, ALU.add, ALU.max)\
                    .then_inc(s.n_g, 1)

            def features(c):
                q_, k_, v_ = qf[c % 2], kf[c % 2], vA[c % 2]
                dve.wait_ge(s.n_exp, 2 * c + 1)
                dve.wait_ge(s.n_gd, 4 * c + 1)
                dve.tensor_tensor(q_[:, :], q_[:, :], z0[:, :], ALU.add).then_inc(s.n_feat, 1)
                dve.wait_ge(s.n_gexp, c + 1)
                dve.tensor_scalar(z2[:, :], z2[:, :], 1.0, None, ALU.add).then_inc(s.n_gd, 1)
                dve.wait_ge(s.n_gd, 4 * c + 2)
                dve.reciprocal(z2[:, :], z2[:, :]).then_inc(s.n_gd, 1)
                dve.wait_ge(s.n_gd, 4 * c + 3)
                dve.wait_ge(s.n_proj, 4 * c + 3)
                dve.scalar_tensor_tensor(k_[:, :], B[1][:, :], bk, z2[:, :], ALU.add, ALU.mult).then_inc(s.n_gd, 1)
                dve.wait_ge(s.n_gd, 4 * c + 4)
                dve.tensor_scalar(z1[:, :], k_[:, :], 0.0, None, ALU.min).then_inc(s.n_min, 1)
                dve.wait_ge(s.n_proj, 4 * c + 4)
                if c > 1:
                    dve.wait_ge(s.n_num, 2 * c - 2)
                dve.tensor_tensor(v_[:, :, 0:D], B[3][:, :].rearrange("p (t d) -> p t d", t=CT),
                                  bc(lbv_row[:, :].unsqueeze(1), [P, CT, D]), ALU.add).then_inc(s.n_v, 1)
                dve.wait_ge(s.n_exp, 2 * c + 2)
                dve.scalar_tensor_tensor(k_[:, :], k_[:, :], 0.0, z1[:, :], ALU.max, ALU.add).then_inc(s.n_feat, 1)

            features_first(0)
            features(0)
            for c in range(NCH):
                for b in range(2):
                    dve.wait_ge(s.n_att, 2 * c + b + 1)
                    if c:
                        dve.wait_ge(s.n_num, 2 * c - 1 + b)
                    dve.tensor_tensor(am[b][:, :], B[4 + b][:, 0:384], causal[:, :], ALU.mult).then_inc(s.n_am, 1)
                if c + 1 < NCH:
                    features_first(c + 1)
                for b in range(2):
                    dve.wait_ge(s.n_num, 2 * c + b + 1)
                    if c:
                        dve.wait_ge(s.n_rec, c)
                    dve.tensor_scalar(ndr[:, 0, 2 * b:2 * b + 2],
                                      B[6 + b][:, 0:2 * (D + 1)].rearrange("p (t d) -> p t d", t=2)[:, :, D],
                                      DEN_EPS, None, ALU.add).then_inc(s.n_den, 1)
                dve.wait_ge(s.n_den, 2 * c + 2)
                if c:
                    dve.wait_ge(s.n_o, c)
                dve.reciprocal(ndr[:, 1, :], ndr[:, 0, :]).then_inc(s.n_rec, 1)
                dve.wait_ge(s.n_rec, c + 1)
                if c:
                    dve.wait_ge(s.n_oT_ps, c)
                for j in range(CT):
                    o0 = (j % 2) * (D + 1)
                    m = dve.tensor_scalar(osb[:, j, :], B[6 + j // 2][:, o0:o0 + D], ndr[:, 1, j:j + 1], None, ALU.mult)
                m.then_inc(s.n_o, 1)
                if c + 1 < NCH:
                    features(c + 1)
                dve.wait_ge(s.n_yps, c + 1)
                dve.tensor_tensor(U[:, c * CT:(c + 1) * CT, :], B[6][:, :].rearrange("p (t d) -> p t d", t=CT),
                                  bc(lbp_row[:, :].unsqueeze(1), [P, CT, D]), ALU.add).then_inc(s.n_out, 1)
            phase_end(dve, "dve", ph)

        def fin_dve(dve, coef, k0=None):
            if k0 is not None:
                for c in range(NCH):
                    add_experts(dve, k0, c)
                    dve.wait_ge(s.x_sum, 2 * (k0 * NT + (c + 1) * CT))
                    dve.sem_inc(s.fin_x, 1)
                return
            with dve.Fori(0, NCH) as c:
                xc = X[:, bass.ts(c, CT), :]
                dve.scalar_tensor_tensor(xc, U[:, bass.ts(c, CT), :], coef, xc, ALU.mult, ALU.add).then_inc(s.fin_x, 1)

        def fin_sync(sp):
            per_seq = out.rearrange("b (t p) d -> p (b t) d", p=P)
            for c in range(NCH):
                sp.wait_ge(s.fin_x, c + 1)
                sp.dma_start(per_seq[:, c * CT:(c + 1) * CT, :], X[:, c * CT:(c + 1) * CT, :]).then_inc(s.out_done, 16)
            sp.wait_ge(s.out_done, 16 * NCH)

        def nothing(eng, me, ph):
            phase_end(eng, me, ph)

        COEF = [0.0, 0.5, 1.0, 0.5, 0.5, 1.0, 0.5]

        @block.sync
        def _(sp):
            setup_sync(sp)
            if stages >= 1:
                ffn_sync(sp, 0, 2)
            if stages >= 3:
                ffn_sync(sp, 1, 10)
            if stages >= 4:
                me_sync(sp, 0)
            if stages >= 6:
                me_sync(sp, 1)
            fin_sync(sp)

        @block.tensor
        def _(pe):
            tr_pe(pe, 0, 1)
            setup2_pe(pe, 2)
            if stages >= 1:
                ffn(pe, "pe", 0, 2)
            if stages >= 2:
                tr_pe(pe, 1, 7)
                ap_pe(pe, 8)
                aa_pe(pe, 9)
            if stages >= 3:
                tr_pe(pe, 2, 10)
                ffn(pe, "pe", 1, 10)
            if stages >= 4:
                tr_pe(pe, 3, 15)
                mr_pe(pe, 0, 16)
                me_pe(pe, 0, 17)
            if stages >= 5:
                tr_pe(pe, 4, 18)
                la_pe(pe, 19)
            if stages >= 6:
                tr_pe(pe, 5, 20)
                mr_pe(pe, 1, 21)
                me_pe(pe, 1, 22)

        @block.scalar
        def _(act):
            tr_act(act, 0, 1)
            nothing(act, "act", 2)
            if stages >= 1:
                ffn(act, "act", 0, 2)
            if stages >= 2:
                tr_act(act, 1, 7)
                ap_act(act, 8)
                aa_act(act, 9)
            if stages >= 3:
                tr_act(act, 2, 10)
                ffn(act, "act", 1, 10)
            if stages >= 4:
                tr_act(act, 3, 15)
                mr_act(act, 0, 16)
                me_act(act, 0, 17)
            if stages >= 5:
                tr_act(act, 4, 18)
                la_act(act, 19)
            if stages >= 6:
                tr_act(act, 5, 20)
                mr_act(act, 1, 21)
                me_act(act, 1, 22)

        @block.vector
        def _(dve):
            tr_dve(dve, 0, 0.0, 1)
            setup2_dve(dve, 2)
            if stages >= 1:
                ffn(dve, "dve", 0, 2)
            if stages >= 2:
                tr_dve(dve, 1, COEF[1], 7)
                ap_dve(dve, 8)
                aa_dve(dve, 9)
            if stages >= 3:
                tr_dve(dve, 2, COEF[2], 10)
                ffn(dve, "dve", 1, 10)
            if stages >= 4:
                tr_dve(dve, 3, COEF[3], 15)
                mr_dve(dve, 0, COEF[4], 16)
                me_dve(dve, 0, 17)
            if stages >= 5:
                tr_dve(dve, 4, 0.0, 18, added=True)
                la_dve(dve, 19)
            if stages >= 6:
                tr_dve(dve, 5, COEF[5], 20)
                mr_dve(dve, 1, COEF[6], 21)
                me_dve(dve, 1, 22)
            fin_dve(dve, COEF[stages], {4: 0, 6: 1}.get(stages))

        @block.gpsimd
        def _(pool):
            setup_pool(pool)
            tr_pool(pool, 0, 1)
            setup2_pool(pool, 2)
            if stages >= 1:
                ffn(pool, "pool", 0, 2)
            if stages >= 2:
                tr_pool(pool, 1, 7)
                vm_zeros(pool)
                nothing(pool, "pool", 8)
                aa_pool(pool, 9)
            if stages >= 3:
                tr_pool(pool, 2, 10, kT_zeros)
                ffn(pool, "pool", 1, 10)
            if stages >= 4:
                tr_pool(pool, 3, 15)
                mr_pool(pool, 0, 16)
                me_pool(pool, 0, 17)
            if stages >= 5:
                tr_pool(pool, 4, 18, vA_ones, twice=True)
                nothing(pool, "pool", 19)
            if stages >= 6:
                tr_pool(pool, 5, 20)
                mr_pool(pool, 1, 21)
                me_pool(pool, 1, 22)


_INS = ["L0_attn_x", "L0_attn_qkv_w", "L0_attn_qkv_b", "L0_attn_out_w", "L0_attn_out_b", "L0_attn_decay_alpha",
        "L0_ffn_wqkv", "L0_ffn_q_scale", "L0_ffn_k_scale", "L0_ffn_wo", "L0_ffn_ln_g", "L0_ffn_ln_b", "L0_ffn_w1",
        "L0_ffn_b1", "L0_ffn_w2", "L0_ffn_b2", "L1_attn_w_qkv", "L1_attn_b_qkv", "L1_attn_w_gate", "L1_attn_b_gate",
        "L1_attn_w_proj", "L1_attn_b_proj", "L1_attn_ln_g", "L1_attn_ln_b", "L1_ffn_Ws1", "L1_ffn_bs1", "L1_ffn_Ws2",
        "L1_ffn_bs2", "L1_ffn_We1", "L1_ffn_be1", "L1_ffn_We2", "L1_ffn_be2", "L1_ffn_Wr", "L1_ffn_br"]


def kernel(**inputs):
    import concourse.bacc as bacc
    from concourse.bass_utils import run_bass_kernel_spmd

    nc = bacc.Bacc("TRN2", target_bir_lowering=False, num_devices=1)
    arrays, aps = {}, {}
    for name in _INS:
        arrays[f"in_{name}"] = np.ascontiguousarray(inputs[name])
    for name, value in constants().items():
        arrays[f"in_{name}"] = np.ascontiguousarray(value.reshape(value.shape))
    for name, value in arrays.items():
        aps[name[3:]] = nc.dram_tensor(name, value.shape, mybir.dt.from_np(value.dtype), kind="ExternalInput").ap()
    out = nc.dram_tensor("out_0", (NBATCH, SEQ, D), F32, kind="ExternalOutput").ap()
    build(nc, aps, out)
    r = run_bass_kernel_spmd(nc, [arrays], core_ids=[0])
    return r.results[0]["out_0"]
```
